# Optimizing a Trainium2 kernel written in Bass

```python
import numpy as np
import jax
import jax.numpy as jnp

def _softmax(x, axis=-1):
    return jax.nn.softmax(x, axis=axis)

def _gelu(x):
    return jax.nn.gelu(x, approximate=True)

def _silu(x):
    return jax.nn.silu(x)

def _sigmoid(x):
    return jax.nn.sigmoid(x)

def _layernorm(x, axis=-1, eps=1e-05):
    m = jnp.mean(x, axis=axis, keepdims=True)
    v = jnp.var(x, axis=axis, keepdims=True)
    return (x - m) / jnp.sqrt(v + eps)

def _scatter_add(tgt, idx, src, axis=0):
    return tgt.at[idx].add(src)

def _segment_sum(src, seg, n):
    return jax.ops.segment_sum(src, seg, n)
kernel_name = 'mk_adj_ffn_d1_adj_r2_be4cb0'

def setup_inputs(seed: int=0):
    np.random.seed(seed)
    _w = jnp.asarray

    def _rec_inputs():
        import jax
        import jax.numpy as jnp
        _gk = jax.random.key(seed)
        x = -0.000929 + 1 * jax.random.normal(jax.random.fold_in(_gk, 1), (3327, 128), jnp.float32)
        _w = (1.0 + jnp.arange(3327, dtype=jnp.float32)) ** (-0.5)
        _w = _w / _w.mean()
        _pij = jnp.clip(0.00120228 * _w[:, None] * _w[None, :], 0.0, 1.0)
        _a = jax.random.uniform(jax.random.fold_in(_gk, 2), (3327, 3327)) < _pij
        _a = jnp.logical_or(_a, jnp.eye(3327, dtype=bool))
        _af = _a.astype(jnp.float32)
        _af = _af * jax.random.uniform(jax.random.fold_in(_gk, 3), (3327, 3327), jnp.float32, 0.05, 1)
        adj = _af
        return (x, adj)
    x, adj = _rec_inputs()

    def _L0_gnn_setup():
        import jax, jax.numpy as jnp
        import numpy as np
        N, H, HEADS = (2048, 128, 3)
        ALPHA = 0.2
        NEG_INF = -9000000000000000.0

        def _sign_adj(key, n, density):
            k1, k2 = jax.random.split(key)
            mask = jax.random.uniform(k1, (n, n)) < density
            sign = jnp.where(jax.random.uniform(k2, (n, n)) < 0.5, -1.0, 1.0)
            adj = jnp.where(mask, sign, 0.0).astype(jnp.float32)
            idx = jnp.arange(n)
            return adj.at[idx, idx].set(1.0)

        def _gru_cell(x, hstate, Wih, Whh, bih, bhh):
            gi = x @ Wih.T + bih
            gh = hstate @ Whh.T + bhh
            ir, iz, inn = jnp.split(gi, 3, axis=1)
            hr, hz, hn = jnp.split(gh, 3, axis=1)
            r = jax.nn.sigmoid(ir + hr)
            z = jax.nn.sigmoid(iz + hz)
            n = jnp.tanh(inn + r * hn)
            return (1.0 - z) * n + z * hstate

        def _gat_head(h, node_adj, edge_adj, W, a):
            hW = h @ W
            hp = (node_adj > 0).astype(hW.dtype) @ hW
            hm = (node_adj < 0).astype(hW.dtype) @ hW
            e_plus = jax.nn.leaky_relu(jnp.concatenate([hp, hm], axis=1) @ a, ALPHA)[:, 0]
            e_minus = jax.nn.leaky_relu(jnp.concatenate([hm, hp], axis=1) @ a, ALPHA)[:, 0]
            att = jnp.where(edge_adj > 0, e_plus[None, :], NEG_INF)
            att = jnp.where(edge_adj < 0, e_minus[None, :], att)
            att = jax.nn.softmax(att, axis=1)
            return att * edge_adj @ hW
        key = jax.random.key(seed)
        ks = jax.random.split(key, 16)
        std = 0.01
        gain = 1.414
        return {'h': jax.random.normal(ks[0], (N, H), jnp.float32), 'node_adj': _sign_adj(ks[1], N, 0.005), 'edge_adj': _sign_adj(ks[2], N, 0.005), 'gat_W': jax.random.normal(ks[3], (HEADS, H, H), jnp.float32) * (gain / np.sqrt(H, dtype=np.float32)), 'gat_a': jax.random.normal(ks[4], (HEADS, 2 * H, 1), jnp.float32) * 0.1, 'edge_Wih': jax.random.normal(ks[5], (3 * H, H), jnp.float32) * std, 'edge_Whh': jax.random.normal(ks[6], (3 * H, H), jnp.float32) * std, 'edge_bih': jnp.zeros((3 * H,), jnp.float32), 'edge_bhh': jnp.zeros((3 * H,), jnp.float32), 'node_Wih': jax.random.normal(ks[7], (3 * H, H), jnp.float32) * std, 'node_Whh': jax.random.normal(ks[8], (3 * H, H), jnp.float32) * std, 'node_bih': jnp.zeros((3 * H,), jnp.float32), 'node_bhh': jnp.zeros((3 * H,), jnp.float32)}
    _L0_gnn_all = _L0_gnn_setup()
    _L0_gnn_in = {k: v for k, v in _L0_gnn_all.items() if k in ('gat_W', 'gat_a', 'edge_Wih', 'edge_Whh', 'edge_bih', 'edge_bhh', 'node_Wih', 'node_Whh', 'node_bih', 'node_bhh')}
    del _L0_gnn_all

    def _L0_ffn_setup():
        import jax, jax.numpy as jnp
        import numpy as np
        B, T, C = (64, 192, 128)
        NH, NKV = (4, 2)
        HD = C // NH
        NREP = NH // NKV
        NE, TOPK = (8, 2)
        HID = int(8 / 3 * C)
        EPS_RMS = 1e-06

        def _rope_tables(t_len):
            inv_freq = 1.0 / 10000.0 ** (np.arange(0, HD, 2, dtype=np.float32) / HD)
            t = np.arange(t_len, dtype=np.float32)
            freqs = np.outer(t, inv_freq)
            emb = np.concatenate([freqs, freqs], axis=-1)
            return (jnp.asarray(np.cos(emb)), jnp.asarray(np.sin(emb)))

        def _rotate_half(x):
            h = x.shape[-1] // 2
            return jnp.concatenate([-x[..., h:], x[..., :h]], axis=-1)

        def _rmsnorm(v, w):
            return v * jax.lax.rsqrt(jnp.mean(v * v, axis=-1, keepdims=True) + EPS_RMS) * w
        key = jax.random.key(seed)
        ks = jax.random.split(key, 10)
        s = lambda k, shape: jax.random.normal(k, shape, jnp.float32) * 0.02
        return {'x': jax.random.normal(ks[0], (B, T, C), jnp.float32), 'ln1_w': jnp.ones((C,), jnp.float32), 'ln2_w': jnp.ones((C,), jnp.float32), 'wq': s(ks[1], (NH * HD, C)), 'wk': s(ks[2], (NKV * HD, C)), 'wv': s(ks[3], (NKV * HD, C)), 'wo': s(ks[4], (C, C)), 'router_w': s(ks[5], (NE, C)), 'w1': s(ks[6], (NE, HID, C)), 'w2': s(ks[7], (NE, C, HID)), 'w3': s(ks[8], (NE, HID, C))}
    _L0_ffn_all = _L0_ffn_setup()
    _L0_ffn_in = {k: v for k, v in _L0_ffn_all.items() if k in ('ln1_w', 'ln2_w', 'wq', 'wk', 'wv', 'wo', 'router_w', 'w1', 'w2', 'w3')}
    del _L0_ffn_all
    return {'x': x, 'adj': adj, 'L0_gnn_gat_W': _L0_gnn_in['gat_W'], 'L0_gnn_gat_a': _L0_gnn_in['gat_a'], 'L0_gnn_edge_Wih': _L0_gnn_in['edge_Wih'], 'L0_gnn_edge_Whh': _L0_gnn_in['edge_Whh'], 'L0_gnn_edge_bih': _L0_gnn_in['edge_bih'], 'L0_gnn_edge_bhh': _L0_gnn_in['edge_bhh'], 'L0_gnn_node_Wih': _L0_gnn_in['node_Wih'], 'L0_gnn_node_Whh': _L0_gnn_in['node_Whh'], 'L0_gnn_node_bih': _L0_gnn_in['node_bih'], 'L0_gnn_node_bhh': _L0_gnn_in['node_bhh'], 'L0_ffn_ln1_w': _L0_ffn_in['ln1_w'], 'L0_ffn_ln2_w': _L0_ffn_in['ln2_w'], 'L0_ffn_wq': _L0_ffn_in['wq'], 'L0_ffn_wk': _L0_ffn_in['wk'], 'L0_ffn_wv': _L0_ffn_in['wv'], 'L0_ffn_wo': _L0_ffn_in['wo'], 'L0_ffn_router_w': _L0_ffn_in['router_w'], 'L0_ffn_w1': _L0_ffn_in['w1'], 'L0_ffn_w2': _L0_ffn_in['w2'], 'L0_ffn_w3': _L0_ffn_in['w3']}

def reference(x, adj, L0_gnn_gat_W, L0_gnn_gat_a, L0_gnn_edge_Wih, L0_gnn_edge_Whh, L0_gnn_edge_bih, L0_gnn_edge_bhh, L0_gnn_node_Wih, L0_gnn_node_Whh, L0_gnn_node_bih, L0_gnn_node_bhh, L0_ffn_ln1_w, L0_ffn_ln2_w, L0_ffn_wq, L0_ffn_wk, L0_ffn_wv, L0_ffn_wo, L0_ffn_router_w, L0_ffn_w1, L0_ffn_w2, L0_ffn_w3):
    import jax
    import jax.numpy as jnp

    def _L0_gnn_ref(h, node_adj, edge_adj, gat_W, gat_a, edge_Wih, edge_Whh, edge_bih, edge_bhh, node_Wih, node_Whh, node_bih, node_bhh):
        import jax, jax.numpy as jnp
        import numpy as np
        N, H, HEADS = (2048, 128, 3)
        ALPHA = 0.2
        NEG_INF = -9000000000000000.0

        def _sign_adj(key, n, density):
            k1, k2 = jax.random.split(key)
            mask = jax.random.uniform(k1, (n, n)) < density
            sign = jnp.where(jax.random.uniform(k2, (n, n)) < 0.5, -1.0, 1.0)
            adj = jnp.where(mask, sign, 0.0).astype(jnp.float32)
            idx = jnp.arange(n)
            return adj.at[idx, idx].set(1.0)

        def _gru_cell(x, hstate, Wih, Whh, bih, bhh):
            gi = x @ Wih.T + bih
            gh = hstate @ Whh.T + bhh
            ir, iz, inn = jnp.split(gi, 3, axis=1)
            hr, hz, hn = jnp.split(gh, 3, axis=1)
            r = jax.nn.sigmoid(ir + hr)
            z = jax.nn.sigmoid(iz + hz)
            n = jnp.tanh(inn + r * hn)
            return (1.0 - z) * n + z * hstate

        def _gat_head(h, node_adj, edge_adj, W, a):
            hW = h @ W
            hp = (node_adj > 0).astype(hW.dtype) @ hW
            hm = (node_adj < 0).astype(hW.dtype) @ hW
            e_plus = jax.nn.leaky_relu(jnp.concatenate([hp, hm], axis=1) @ a, ALPHA)[:, 0]
            e_minus = jax.nn.leaky_relu(jnp.concatenate([hm, hp], axis=1) @ a, ALPHA)[:, 0]
            att = jnp.where(edge_adj > 0, e_plus[None, :], NEG_INF)
            att = jnp.where(edge_adj < 0, e_minus[None, :], att)
            att = jax.nn.softmax(att, axis=1)
            return att * edge_adj @ hW
        dn = jnp.diag(node_adj)
        de = jnp.diag(edge_adj)
        idx = jnp.arange(node_adj.shape[0])
        node_adj_norm = node_adj.at[idx, idx].add(-dn)
        edge_adj_norm = edge_adj.at[idx, idx].add(-de)
        node_support = node_adj_norm @ h
        edge_output = _gru_cell(node_support, h, edge_Wih, edge_Whh, edge_bih, edge_bhh)
        edge_support = _gat_head(h, node_adj_norm, edge_adj_norm, gat_W[0], gat_a[0])
        for i in range(1, HEADS):
            edge_support = edge_support + _gat_head(h, node_adj_norm, edge_adj_norm, gat_W[i], gat_a[i])
        edge_support = edge_support / HEADS
        node_output = _gru_cell(edge_support, h, node_Wih, node_Whh, node_bih, node_bhh)
        return de[:, None] * edge_output + dn[:, None] * node_output

    def _L0_ffn_ref(x, ln1_w, ln2_w, wq, wk, wv, wo, router_w, w1, w2, w3):
        import jax, jax.numpy as jnp
        import numpy as np
        B, T, C = (64, 192, 128)
        NH, NKV = (4, 2)
        HD = C // NH
        NREP = NH // NKV
        NE, TOPK = (8, 2)
        HID = int(8 / 3 * C)
        EPS_RMS = 1e-06

        def _rope_tables(t_len):
            inv_freq = 1.0 / 10000.0 ** (np.arange(0, HD, 2, dtype=np.float32) / HD)
            t = np.arange(t_len, dtype=np.float32)
            freqs = np.outer(t, inv_freq)
            emb = np.concatenate([freqs, freqs], axis=-1)
            return (jnp.asarray(np.cos(emb)), jnp.asarray(np.sin(emb)))

        def _rotate_half(x):
            h = x.shape[-1] // 2
            return jnp.concatenate([-x[..., h:], x[..., :h]], axis=-1)

        def _rmsnorm(v, w):
            return v * jax.lax.rsqrt(jnp.mean(v * v, axis=-1, keepdims=True) + EPS_RMS) * w
        Bx, Tx, Cx = x.shape
        h = _rmsnorm(x, ln1_w)
        q = (h @ wq.T).reshape(Bx, Tx, NH, HD).transpose(0, 2, 1, 3)
        k = (h @ wk.T).reshape(Bx, Tx, NKV, HD).transpose(0, 2, 1, 3)
        v = (h @ wv.T).reshape(Bx, Tx, NKV, HD).transpose(0, 2, 1, 3)
        cos, sin = _rope_tables(Tx)
        cos, sin = (cos[None, None], sin[None, None])
        q = q * cos + _rotate_half(q) * sin
        k = k * cos + _rotate_half(k) * sin
        k = jnp.repeat(k, NREP, axis=1)
        v = jnp.repeat(v, NREP, axis=1)
        scores = jnp.einsum('bhtd,bhsd->bhts', q, k) / jnp.sqrt(jnp.float32(HD))
        causal = jnp.tril(jnp.ones((Tx, Tx), dtype=bool))
        scores = jnp.where(causal[None, None], scores, jnp.float32(-1e+30))
        att = jax.nn.softmax(scores, axis=-1)
        y = jnp.einsum('bhts,bhsd->bhtd', att, v).transpose(0, 2, 1, 3).reshape(Bx, Tx, Cx)
        x = x + y @ wo.T
        flat = _rmsnorm(x, ln2_w).reshape(-1, Cx)
        probs = jax.nn.softmax(flat @ router_w.T, axis=-1)
        tp, ti = jax.lax.top_k(probs, TOPK)
        tp = tp / (jnp.sum(tp, axis=-1, keepdims=True) + 1e-09)
        weights = jnp.sum(tp[..., None] * jax.nn.one_hot(ti, NE, dtype=flat.dtype), axis=1)
        out = jnp.zeros_like(flat)
        for e in range(NE):
            hh = jax.nn.silu(flat @ w1[e].T) * (flat @ w3[e].T)
            out = out + weights[:, e:e + 1] * (hh @ w2[e].T)
        return x + out.reshape(Bx, Tx, Cx)
    x = x + _L0_gnn_ref(_layernorm(x, axis=-1), adj, adj, L0_gnn_gat_W, L0_gnn_gat_a, L0_gnn_edge_Wih, L0_gnn_edge_Whh, L0_gnn_edge_bih, L0_gnn_edge_bhh, L0_gnn_node_Wih, L0_gnn_node_Whh, L0_gnn_node_bih, L0_gnn_node_bhh)
    x = x + _L0_ffn_ref(_layernorm(x, axis=-1)[None], L0_ffn_ln1_w, L0_ffn_ln2_w, L0_ffn_wq, L0_ffn_wk, L0_ffn_wv, L0_ffn_wo, L0_ffn_router_w, L0_ffn_w1, L0_ffn_w2, L0_ffn_w3)[0]
    return x

_drawn_inputs = setup_inputs


def setup_inputs(seed=0):
    import zlib

    import numpy as np

    out = dict(_drawn_inputs(seed))
    spreads = {'L0_gnn_edge_bih': (0.0, 0.379),
     'L0_gnn_edge_bhh': (0.0, 0.642),
     'L0_gnn_node_bih': (0.0, 0.408),
     'L0_gnn_node_bhh': (0.0, 0.626),
     'L0_ffn_ln1_w': (1.0, 0.6),
     'L0_ffn_ln2_w': (1.0, 0.6)}
    factors = {'L0_gnn_gat_W': 6.214,
     'L0_gnn_gat_a': 8.0,
     'L0_gnn_edge_Whh': 3.91,
     'L0_gnn_node_Wih': 6.155,
     'L0_gnn_node_Whh': 3.875,
     'L0_ffn_wq': 8.0,
     'L0_ffn_wk': 8.0,
     'L0_ffn_wv': 8.0,
     'L0_ffn_wo': 8.0,
     'L0_ffn_router_w': 8.0,
     'L0_ffn_w1': 8.0,
     'L0_ffn_w2': 8.0,
     'L0_ffn_w3': 8.0}
    for name, (base, spread) in spreads.items():
        noise = np.random.default_rng([zlib.crc32(name.encode()), seed]).standard_normal(out[name].shape)
        drawn = base * np.exp(spread * noise) if base else spread * noise
        out[name] = jnp.asarray(drawn.astype(out[name].dtype))
    for name, factor in factors.items():
        out[name] = (out[name] * factor).astype(out[name].dtype)
    return out
```

```python
from contextlib import ExitStack

import concourse.bass as bass
from concourse import mybir

P = 128
N = 3327
NB = (N + P - 1) // P
NP = NB * P
C = 128
HEADS = 3
ALPHA = 0.2
NEG_INF = -9000000000000000.0
LOWEST = -3.0e38
PARTS = 3
EROWS = 2 * HEADS
EW = 32
EP = 2 * EW
RING = 4
LN_EPS = 1e-5
BANK = 512

SWEEPS = [(0, 14), (14, 12)]
CHUNKS = [(0, 8), (8, 6), (14, 6), (20, 6)]

AH, KV, HD = 4, 2, 32
NE, TOPK, HID = 8, 2, 341
RMS_EPS = 1e-6
STACK = PARTS * HD
HTILES = [(0, 128), (128, 128), (256, 85)]
QCH = [(4 * c, min(4, NB - 4 * c)) for c in range((NB + 3) // 4)]

ALU = mybir.AluOpType
ACT = mybir.ActivationFunctionType
F32 = mybir.dt.float32
BF16 = mybir.dt.bfloat16
I32 = mybir.dt.int32
AX = mybir.AxisListType.X
ds = bass.ds


def pieces(cols, size=BANK):
    return [(a, min(size, cols - a)) for a in range(0, cols, size)]


def chain(engine, sem):
    done = [0]

    def step(instruction):
        done[0] += 1
        instruction.then_inc(sem, 1)
        engine.wait_ge(sem, done[0])
    return step


def row_stats(v, step, x, xc, sq, mean, var):
    step(v.tensor_reduce(mean, x, AX, ALU.add))
    step(v.tensor_scalar(mean, mean, 1.0 / C, None, ALU.mult))
    step(v.tensor_tensor(xc, x, mean.unsqueeze(2).to_broadcast([P, NB, C]), ALU.subtract))
    step(v.tensor_tensor(sq, xc, xc, ALU.mult))
    step(v.tensor_reduce(var, sq, AX, ALU.add))


def norm_program(nc, t, T):
    X, H, SQ, HTR = T["X"], T["H"], T["SQ"], T["HTR"]
    with ExitStack() as ctx:
        sem = lambda name: ctx.enter_context(nc.semaphore(name))
        ps = ctx.enter_context(nc.psum_tensor("n_ps", [P, 8, BANK], F32))
        s_x, s_c, s_dve, s_var, s_rt, s_h = map(sem, ("n_x", "n_c", "n_dve", "n_var", "n_rt", "n_h"))
        s_tr, s_ht, s_u, s_uc, s_U = map(sem, ("n_tr", "n_ht", "n_u", "n_uc", "n_U"))
        mean = ctx.enter_context(nc.sbuf_tensor("n_mean", [P, NB], F32))
        var = ctx.enter_context(nc.sbuf_tensor("n_var_t", [P, NB], F32))
        wt = ctx.enter_context(nc.sbuf_tensor("n_wt", [P, HEADS, C], F32))
        av = ctx.enter_context(nc.sbuf_tensor("n_av", [P, HEADS, 2], F32))
        uc = ctx.enter_context(nc.sbuf_tensor("n_ucol", [P, 2, HEADS], F32))
        U = ctx.enter_context(nc.sbuf_tensor("n_Uf", [P, NB, EROWS], F32))
        Ub = ctx.enter_context(nc.sbuf_tensor("n_Ub", [P, NB, EROWS], BF16))
        banks = [(b0, min(4, NB - b0)) for b0 in range(0, NB, 4)]
        block = ctx.enter_context(nc.Block())

        @block.sync
        def _(sp):
            sp.dma_start(X, t["x"].rearrange("(b p) c -> p b c", p=P)).then_inc(s_x, 16)
            sp.dma_start(T["eye"][:], t["eye"]).then_inc(s_c, 16)
            sp.dma_start(T["noteye"][:], t["noteye"]).then_inc(s_c, 16)
            sp.dma_start(T["dcol"][:], t["diag"]).then_inc(s_c, 16)
            sp.dma_start(wt[:], t["gat_WT"].rearrange("h c d -> c h d")).then_inc(s_c, 16)
            sp.dma_start(av[:], t["gat_a"]).then_inc(s_c, 16)
            sp.dma_start(T["selE"][:], t["selE"]).then_inc(s_c, 16)
            sp.dma_start(T["selB"][:], t["selB"]).then_inc(s_c, 16)
            sp.wait_ge(s_x, 16)
            sp.wait_ge(s_c, 16 * 7)

        @block.vector
        def _(v):
            step = chain(v, s_dve)
            v.memset(T["ones"][:], 1.0)
            v.memset(T["eps"][:, 0:1], LN_EPS)
            v.memset(T["eps"][:, 1:2], RMS_EPS)
            step(v.memset(T["U3"][:], 0.0))
            step(v.memset(T["U3"][:, :, 1, 0:1], 1.0))
            v.wait_ge(s_x, 16)
            row_stats(v, step, X, H, SQ, mean[:], var[:])
            v.sem_inc(s_var, 1)
            v.wait_ge(s_rt, 1)
            step(v.reciprocal(mean[:], var[:]))
            v.tensor_tensor(H, H, mean[:].unsqueeze(2).to_broadcast([P, NB, C]), ALU.mult).then_inc(s_h, 1)
            v.wait_ge(s_u, 1)
            v.tensor_copy(uc[:], ps[:, 7, 0:EROWS].rearrange("p (h k) -> p k h", k=2)).then_inc(s_uc, 1)
            v.wait_ge(s_U, 1)
            step(v.tensor_copy(U[:], ps[:, 7, 8:8 + NB * EROWS].rearrange("p (b e) -> p b e", e=EROWS)))
            for k in range(PARTS):
                step(v.tensor_copy(Ub[:], U[:]))
                e0 = 1 + k * EROWS
                v.tensor_copy(T["U3"][:, :, 0, e0:e0 + EROWS], Ub[:])
                v.tensor_copy(T["U3"][:, :, 1, e0:e0 + HEADS], Ub[:, :, HEADS:EROWS])
                step(v.tensor_copy(T["U3"][:, :, 1, e0 + HEADS:e0 + EROWS], Ub[:, :, 0:HEADS]))
                step(v.tensor_tensor(U[:], U[:], Ub[:], ALU.subtract))

        @block.scalar
        def _(a):
            a.wait_ge(s_var, 1)
            a.activation(var[:], var[:], ACT.Sqrt, bias=T["eps"][:, 0:1], scale=1.0 / C).then_inc(s_rt, 1)
            for k, (b0, nb) in enumerate(banks):
                a.wait_ge(s_tr, k + 1)
                a.copy(HTR[:, b0 * P:(b0 + nb) * P], ps[:, k % 6, 0:nb * P]).then_inc(s_ht, 1)

        @block.tensor
        def _(pe):
            pe.wait_ge(s_c, 16 * 7)
            for h in range(HEADS):
                m = pe.matmul(ps[:, 7, 2 * h:2 * h + 2], wt[:, h, :], av[:, h, :], start=True, stop=True)
            m.then_inc(s_u, 1)
            pe.wait_ge(s_h, 1)
            for k, (b0, nb) in enumerate(banks):
                if k >= 6:
                    pe.wait_ge(s_ht, k - 5)
                for b in range(nb):
                    m = pe.transpose(ps[:, k % 6, b * P:(b + 1) * P], H[:, b0 + b, :], T["eye"][:])
                m.then_inc(s_tr, 1)
            pe.wait_ge(s_ht, len(banks))
            pe.wait_ge(s_uc, 1)
            for b in range(NB):
                o = 8 + b * EROWS
                m = pe.matmul(ps[:, 7, o:o + EROWS], HTR[:, b * P:(b + 1) * P],
                              uc[:].rearrange("p k h -> p (k h)"), start=True, stop=True)
            m.then_inc(s_U, 1)


def slot_sems(ctx, nc, name, slots=2):
    return [ctx.enter_context(nc.semaphore(f"{name}{u}")) for u in range(slots)]


class Tile:

    def __init__(self, row, n, slot, landed, diagonal, fixed, start, sign):
        self.row, self.n, self.slot, self.landed = row, n, slot, landed
        self.diagonal, self.fixed, self.start, self.sign = diagonal, fixed, start, sign


def tile_loop(engine, first, blocks, base, body, signs=(1,), peel=False):
    n = base
    for si, sign in enumerate(signs):
        for start, count, diagonal in ((first, blocks, True), (first + blocks, NB - first - blocks, False),
                                       (0, first, False)):
            def tile(k, at):
                m = n + at
                return Tile(RING * k + (start + at), RING * k + m, m % RING,
                            16 * k + 16 * (m // RING + 1), diagonal,
                            RING * k + (first * len(signs) + si * blocks + at + 1), m == base, sign)
            lead = min(RING, count) if peel and n == base else 0
            for at in range(lead):
                body(tile(0, at))
            turns = (count - lead) // RING
            if turns:
                with engine.Fori(0, turns) as k:
                    for u in range(RING):
                        body(tile(k, lead + u))
            for at in range(lead + turns * RING, count):
                body(tile(0, at))
            n += count


def spmm_program(nc, t, T):
    H, NS, E = T["H"], T["NS"], T["E"]
    W = max(b for _, b in SWEEPS) * P
    with ExitStack() as ctx:
        sem = lambda name: ctx.enter_context(nc.semaphore("a_" + name))
        tile = lambda name, shape, dt=F32: ctx.enter_context(nc.sbuf_tensor("a_" + name, shape, dt))
        at, mp, mm = tile("at", [P, RING, W]), tile("mp", [P, RING, W], BF16), tile("mm", [P, RING, W], BF16)
        hst, ust = tile("h", [P, RING, C]), tile("u", [P, RING, 2, EW], BF16)
        neg = tile("neg", [P, 1])
        ps = ctx.enter_context(nc.psum_tensor("a_ps", [P, 4 * BANK], F32))
        pe_e = ctx.enter_context(nc.psum_tensor("a_pe", [P, 4 * BANK], F32))
        s_tile = slot_sems(ctx, nc, "a_tile", RING)
        s_free, s_fix, s_mask, s_w, s_sum, s_out, s_neg = map(
            sem, ("free", "fix", "mask", "w", "sum", "out", "neg"))
        block = ctx.enter_context(nc.Block())

        @block.sync
        def _(sp):
            for i, (first, nb) in enumerate(SWEEPS):
                def load(b):
                    sp.wait_ge(s_free, b.n + 1)
                    sp.dma_start(at[:, b.slot, 0:nb * P], t["adjT"][ds(b.row * P, P), first * P:(first + nb) * P]
                                 ).then_inc(s_tile[b.slot], 16)
                tile_loop(sp, first, nb, i * NB, load)
            sp.wait_ge(s_neg, 2)

        @block.gpsimd
        def _(g):
            for i, (first, nb) in enumerate(SWEEPS):
                def stage(b):
                    g.wait_ge(s_free, b.n + 1)
                    g.tensor_copy(hst[:, b.slot, :], H[:, ds(b.row, 1), :].rearrange("p b c -> p (b c)"))
                    g.tensor_copy(ust[:, b.slot, :, :], T["U3"][:, ds(b.row, 1), :, :].rearrange(
                        "p b k e -> p (b k) e")).then_inc(s_w, 1)
                tile_loop(g, first, nb, i * NB, stage)
            g.wait_ge(s_neg, 2)

        @block.vector
        def _(v):
            for i, (first, nb) in enumerate(SWEEPS):
                def masks(b):
                    v.wait_ge(s_tile[b.slot], b.landed)
                    tile = at[:, b.slot, 0:nb * P]
                    if b.diagonal:
                        d = at[:, b.slot, ds((b.row - first) * P, P)]
                        v.tensor_tensor(d, d, T["noteye"][:], ALU.mult).then_inc(s_fix, 1)
                        v.wait_ge(s_fix, b.fixed)
                    v.wait_ge(s_free, b.n + 1)
                    v.tensor_scalar(mp[:, b.slot, 0:nb * P], tile, 0.0, None, ALU.is_gt)
                    v.tensor_scalar(mm[:, b.slot, 0:nb * P], tile, 0.0, None, ALU.is_lt).then_inc(s_mask, 1)
                tile_loop(v, first, nb, i * NB, masks)
                v.wait_ge(s_sum, i + 1)
                v.tensor_copy(E[0:EP, first * P:(first + nb) * P], pe_e[0:EP, 0:nb * P]).then_inc(s_out, 1)
            v.wait_ge(s_out, 2 * len(SWEEPS))
            v.tensor_reduce(neg[0:1, :], E[EW:EW + 1, :], AX, ALU.max).then_inc(s_neg, 1)
            v.wait_ge(s_neg, 1)
            v.tensor_scalar(T["signed"][0:1, :], neg[0:1, :], 0.0, None, ALU.is_gt).then_inc(s_neg, 1)
            v.wait_ge(s_neg, 2)

        @block.scalar
        def _(a):
            for i, (first, nb) in enumerate(SWEEPS):
                a.wait_ge(s_sum, i + 1)
                a.copy(NS[:, first * P:(first + nb) * P], ps[:, 0:nb * P]).then_inc(s_out, 1)
            a.wait_ge(s_neg, 2)

        @block.tensor
        def _(pe):
            pe.sem_inc(s_free, RING)
            for i, (first, nb) in enumerate(SWEEPS):
                if i:
                    pe.wait_ge(s_out, 2 * i)
                def products(b):
                    u = b.slot
                    pe.wait_ge(s_w, b.n + 1)
                    pe.wait_ge(s_mask, b.n + 1)
                    for a, w in pieces(nb * P):
                        pe.matmul(ps[:, a:a + w], hst[:, u, :], at[:, u, a:a + w],
                                  start=b.start, stop=False, skip_group_check=True)
                        for k, mask in enumerate((mp, mm)):
                            m = pe.matmul(pe_e[k * EW:(k + 1) * EW, a:a + w], ust[:, u, k, :], mask[:, u, a:a + w],
                                          start=b.start, stop=False, skip_group_check=True,
                                          tile_position=(0, k * EW))
                    m.then_inc(s_free, 1)
                tile_loop(pe, first, nb, i * NB, products, peel=True)
                pe.wait_ge(s_free, RING + (i + 1) * NB)
                pe.sem_inc(s_sum, 1)
            pe.wait_ge(s_neg, 2)


def columns_program(nc, t, T):
    E, Ecol = T["E"], T["Ecol"]
    with ExitStack() as ctx:
        ps = ctx.enter_context(nc.psum_tensor(T["path"] + "c_ps", [P, BANK], F32))
        s_col, s_dve = (T["sem"](n) for n in ("c_col", "c_dve"))
        block = ctx.enter_context(nc.Block())

        @block.tensor
        def _(pe):
            for b in range(NB):
                m = pe.matmul(ps[:, b * EROWS:(b + 1) * EROWS], E[0:EP, b * P:(b + 1) * P],
                              T["selE"][:], start=True, stop=True)
            m.then_inc(s_col, 1)

        @block.vector
        def _(v):
            step = chain(v, s_dve)
            v.wait_ge(s_col, 1)
            step(v.tensor_copy(Ecol[:], ps[:, 0:NB * EROWS]))
            step(v.scalar_tensor_tensor(Ecol[:], Ecol[:], ALPHA, Ecol[:], ALU.mult, ALU.max))
            step(v.tensor_scalar(T["EcolN"][:], Ecol[:], -1.0, None, ALU.mult))


def scores_program(nc, t, T, si, sign):
    E, EB, S, AR = T["E"], T["EB"], T["S"], T["AR"]
    nmax, den = T["nmax"][:, si], T["den"][:, si]
    cols, pre = pieces(NP), T["path"] + f"r{si}_"
    with ExitStack() as ctx:
        sem = lambda name: T["sem"](f"r{si}_{name}")
        mx = ctx.enter_context(nc.sbuf_tensor(pre + "mx", [P, 2, HEADS], F32))
        nm = ctx.enter_context(nc.sbuf_tensor(pre + "nm", [P, 2, HEADS], F32))
        ps = ctx.enter_context(nc.psum_tensor(pre + "ps", [P, 8, BANK], F32))
        s_a = [sem(f"a{u}") for u in range(2)]
        s_eb, s_ebc, s_dve, s_afree, s_fix, s_bias, s_go, s_max, s_nm, s_exp = map(
            sem, ("eb", "ebc", "dve", "afree", "fix", "bias", "go", "max", "nm", "exp"))
        block = ctx.enter_context(nc.Block())

        @block.sync
        def _(sp):
            with sp.Fori(0, NB // 2) as k:
                for u in range(2):
                    n = 2 * k + u
                    sp.wait_ge(s_afree, n + 1)
                    sp.dma_start(AR[u], t["adj"][ds(n * P, P), :]).then_inc(s_a[u], 16)

        @block.vector
        def _(v):
            v.sem_inc(s_afree, 2)
            step = chain(v, s_dve)
            for h in range(HEADS):
                v.wait_ge(s_ebc, (h + 1) * len(cols))
                step(v.scalar_tensor_tensor(EB[h], EB[h], ALPHA, EB[h], ALU.mult, ALU.max))
            with v.Fori(0, NB // 2) as k:
                for u in range(2):
                    n = 2 * k + u
                    v.wait_ge(s_a[u], 16 * k + 16)
                    d = AR[u][:, ds(n * P, P)]
                    v.tensor_tensor(d, d, T["noteye"][:], ALU.mult).then_inc(s_fix, 1)
                    v.wait_ge(s_fix, n + 1)
                    v.tensor_scalar(AR[u], AR[u], 0.0, NEG_INF, ALU.is_le if sign > 0 else ALU.is_ge,
                                    ALU.mult).then_inc(s_bias, 1)
                    v.wait_ge(s_bias, n + 1)
                    for h in range(HEADS):
                        v.wait_ge(s_exp, 3 * n + (h + 1))
                        v.sem_inc(s_go, 1)
                        v.tensor_tensor_reduce(S[h], AR[u], EB[h], 1.0, LOWEST, ALU.add, ALU.max,
                                               mx[:, u, h:h + 1]).then_inc(s_max, 1)
                        v.wait_ge(s_max, 3 * n + (h + 1))
                        v.tensor_scalar(nm[:, u, h:h + 1], mx[:, u, h:h + 1], -1.0, None,
                                        ALU.mult).then_inc(s_nm, 1)
                    v.sem_inc(s_afree, 1)
                    v.wait_ge(s_nm, 3 * n + 3)
                    v.tensor_copy(nmax[:, ds(3 * n, HEADS)], nm[:, u, :])

        @block.scalar
        def _(a):
            a.sem_inc(s_exp, 3)
            for h in range(HEADS):
                for k, (c0, w) in enumerate(cols):
                    i = h * len(cols) + k
                    a.wait_ge(s_eb, i + 1)
                    a.copy(EB[h][:, c0:c0 + w], ps[:, i % 8, 0:w]).then_inc(s_ebc, 1)
            with a.Fori(0, NB // 2) as k:
                for u in range(2):
                    n = 2 * k + u
                    for h in range(HEADS):
                        a.wait_ge(s_nm, 3 * n + (h + 1))
                        a.activation(S[h], S[h], ACT.Exp, bias=nm[:, u, h:h + 1],
                                     accum_out=den[:, ds(3 * n + h, 1)]).then_inc(s_exp, 1)

        @block.tensor
        def _(pe):
            for h in range(HEADS):
                for k, (c0, w) in enumerate(cols):
                    i = h * len(cols) + k
                    if i >= 8:
                        pe.wait_ge(s_ebc, i - 7)
                    pe.matmul(ps[:, i % 8, 0:w], T["selB"][:, si * HEADS + h, :], E[0:EP, c0:c0 + w],
                              start=True, stop=True).then_inc(s_eb, 1)


def spread_program(nc, t, T, signs):
    NM, nmax, den, rden = T["NM"], T["nmax"], T["den"], T["rden"]
    with ExitStack() as ctx:
        sem = lambda name: T["sem"]("s_" + name)
        dg = ctx.enter_context(nc.sbuf_tensor(T["path"] + "s_dg", [P, 2, HEADS, P], F32))
        corr = ctx.enter_context(nc.sbuf_tensor(T["path"] + "s_corr", [P, 2, NB * HEADS], F32))
        ps = ctx.enter_context(nc.psum_tensor(T["path"] + "s_ps", [P, 2, BANK], F32))
        s_dve, s_corr, s_exp, s_diag, s_bc, s_bank = map(sem, ("dve", "corr", "exp", "diag", "bc", "bank"))
        block = ctx.enter_context(nc.Block())

        @block.vector
        def _(v):
            step = chain(v, s_dve)
            if len(signs) == 2:
                step(v.tensor_tensor(rden[:], nmax[:, 0], nmax[:, 1], ALU.min))
                for i in range(2):
                    m = v.tensor_tensor(corr[:, i], rden[:], nmax[:, i], ALU.subtract)
                m.then_inc(s_corr, 1)
                v.wait_ge(s_exp, 2)
                for i in range(2):
                    m = v.tensor_tensor(den[:, i], den[:, i], corr[:, i], ALU.mult)
                step(m)
                step(v.tensor_copy(nmax[:, 0], rden[:]))
                step(v.tensor_tensor(den[:, 0], den[:, 0], den[:, 1], ALU.add))
            step(v.tensor_scalar(den[:, 0], den[:, 0], float(HEADS), None, ALU.mult))
            step(v.reciprocal(rden[:], den[:, 0]))
            with v.Fori(0, NB // 2) as k:
                for u in range(2):
                    n = 2 * k + u
                    v.wait_ge(s_bc, n + 1)
                    v.tensor_tensor(dg[:, u], T["eye"][:].unsqueeze(1).to_broadcast([P, HEADS, P]),
                                    nmax[:, 0, ds(3 * n, HEADS)].unsqueeze(2).to_broadcast([P, HEADS, P]),
                                    ALU.mult).then_inc(s_diag, 1)

        @block.scalar
        def _(a):
            a.sem_inc(s_bank, 2)
            if len(signs) == 2:
                a.wait_ge(s_corr, 1)
                for i in range(2):
                    a.activation(corr[:, i], corr[:, i], ACT.Exp).then_inc(s_exp, 1)
            with a.Fori(0, NB // 2) as k:
                for u in range(2):
                    n = 2 * k + u
                    a.wait_ge(s_bc, n + 3)
                    a.copy(NM[:, :, ds(n * P, P)],
                           ps[:, u, 0:HEADS * P].rearrange("p (h i) -> p h i", h=HEADS)).then_inc(s_bank, 1)

        @block.tensor
        def _(pe):
            pe.sem_inc(s_bc, 2)
            with pe.Fori(0, NB // 2) as k:
                for u in range(2):
                    n = 2 * k + u
                    pe.wait_ge(s_diag, n + 1)
                    pe.wait_ge(s_bank, n + 1)
                    pe.matmul(ps[:, u, 0:HEADS * P], T["ones"][:], dg[:, u].rearrange("p h i -> p (h i)"),
                              start=True, stop=True).then_inc(s_bc, 1)


def gat_program(nc, t, T, signs):
    H, NM, ES = T["H"], T["NM"], T["ES"]
    W = max(b for _, b in CHUNKS) * P
    ON_ACT = HEADS - 1
    ND = HEADS - 1
    total = NB * len(signs)
    with ExitStack() as ctx:
        sem = lambda name: T["sem"]("g_" + name)
        tile = lambda name, shape: ctx.enter_context(nc.sbuf_tensor(T["path"] + "g_" + name, shape, F32))
        at, y, gs = tile("at", [P, RING, W]), tile("y", [P, RING, HEADS, W]), tile("gs", [P, HEADS, W])
        hst, wg = tile("h", [P, RING, C]), tile("w", [P, HEADS, C])
        G = ctx.enter_context(nc.psum_tensor(T["path"] + "g_G", [P, HEADS, 2 * BANK], F32))
        pj = ctx.enter_context(nc.psum_tensor(T["path"] + "g_pj", [P, 2, BANK], F32))
        s_tile = [sem(f"tile{u}") for u in range(RING)]
        s_wg, s_z, s_relu, s_afree, s_fix, s_sign, s_h, s_y, s_w, s_free = map(
            sem, ("wg", "z", "relu", "afree", "fix", "sign", "h", "y", "w", "free"))
        s_sum, s_gs, s_pj, s_es, s_dve = map(sem, ("sum", "gs", "pj", "es", "dve"))
        block = ctx.enter_context(nc.Block())

        @block.sync
        def _(sp):
            sp.dma_start(wg[:], t["gat_W"].rearrange("h d c -> d h c")).then_inc(s_wg, 16)
            for i, (first, nb) in enumerate(CHUNKS):
                def load(b):
                    sp.wait_ge(s_afree, b.n + 1)
                    sp.dma_start(at[:, b.slot, 0:nb * P], t["adjT"][ds(b.row * P, P), first * P:(first + nb) * P]
                                 ).then_inc(s_tile[b.slot], 16)
                tile_loop(sp, first, nb, i * total, load, signs)
            sp.wait_ge(s_wg, 16)

        @block.gpsimd
        def _(g):
            for i, (first, nb) in enumerate(CHUNKS):
                def stage(b):
                    g.wait_ge(s_free, b.n + 1)
                    g.tensor_copy(hst[:, b.slot, :],
                                  H[:, ds(b.row, 1), :].rearrange("p b c -> p (b c)")).then_inc(s_h, 1)
                tile_loop(g, first, nb, i * total, stage, signs)

        @block.scalar
        def _(a):
            for i, (first, nb) in enumerate(CHUNKS):
                def exps(b):
                    e0 = 0 if b.sign > 0 else HEADS
                    a.wait_ge(s_free, b.n + 1)
                    last = y[:, b.slot, ON_ACT, 0:nb * P]
                    a.activation(last, NM[:, ON_ACT, first * P:(first + nb) * P], ACT.Relu,
                                 bias=T["EcolN"][:, ds(b.row * EROWS + (e0 + ON_ACT), 1)],
                                 scale=-1.0).then_inc(s_relu, 1)
                    for h in range(ND):
                        yh = y[:, b.slot, h, 0:nb * P]
                        a.wait_ge(s_z, ND * b.n + (h + 1))
                        a.activation(yh, yh, ACT.Exp).then_inc(s_y, 1)
                    a.wait_ge(s_relu, b.n + 1)
                    a.activation(last, last, ACT.Exp, scale=-1.0).then_inc(s_y, 1)
                tile_loop(a, first, nb, i * total, exps, signs)
                a.wait_ge(s_sum, i + 1)
                if i:
                    a.wait_ge(s_es, first)
                for h in range(HEADS):
                    a.copy(gs[:, h, 0:nb * P], G[:, h, 0:nb * P]).then_inc(s_gs, 1)

        @block.vector
        def _(v):
            v.sem_inc(s_afree, RING)
            step = chain(v, s_dve)
            for i, (first, nb) in enumerate(CHUNKS):
                def weigh(b):
                    u = b.slot
                    e0 = 0 if b.sign > 0 else HEADS
                    v.wait_ge(s_free, b.n + 1)
                    for h in range(ND):
                        v.tensor_scalar(y[:, u, h, 0:nb * P], NM[:, h, first * P:(first + nb) * P],
                                        T["Ecol"][:, ds(b.row * EROWS + (e0 + h), 1)], 0.0, ALU.add,
                                        ALU.min).then_inc(s_z, 1)
                    v.wait_ge(s_tile[u], b.landed)
                    if b.diagonal:
                        d = at[:, u, ds((b.row - first) * P, P)]
                        v.tensor_tensor(d, d, T["noteye"][:], ALU.mult).then_inc(s_fix, 1)
                        v.wait_ge(s_fix, b.fixed)
                    if len(signs) == 2:
                        v.tensor_scalar(at[:, u, 0:nb * P], at[:, u, 0:nb * P], 0.0, None,
                                        ALU.max if b.sign > 0 else ALU.min).then_inc(s_sign, 1)
                        v.wait_ge(s_sign, b.n + 1)
                    for h in range(HEADS):
                        v.wait_ge(s_y, HEADS * b.n + (h + 1))
                        yh = y[:, u, h, 0:nb * P]
                        v.tensor_tensor(yh, yh, at[:, u, 0:nb * P], ALU.mult).then_inc(s_w, 1)
                    v.wait_ge(s_w, HEADS * b.n + HEADS)
                    v.sem_inc(s_afree, 1)
                tile_loop(v, first, nb, i * total, weigh, signs)
                for b in range(nb):
                    q = first + b
                    v.wait_ge(s_pj, q + 1)
                    for h in range(HEADS):
                        x, r = pj[:, q % 2, h * C:(h + 1) * C], T["rden"][:, HEADS * q + h:HEADS * q + h + 1]
                        if h == 0:
                            step(v.tensor_scalar(ES[:, q, :], x, r, None, ALU.mult))
                        elif h < HEADS - 1:
                            step(v.scalar_tensor_tensor(ES[:, q, :], x, r, ES[:, q, :], ALU.mult, ALU.add))
                        else:
                            v.scalar_tensor_tensor(ES[:, q, :], x, r, ES[:, q, :], ALU.mult,
                                                   ALU.add).then_inc(s_es, 1)

        @block.tensor
        def _(pe):
            pe.sem_inc(s_free, RING)
            pe.wait_ge(s_wg, 16)
            for i, (first, nb) in enumerate(CHUNKS):
                def products(b):
                    pe.wait_ge(s_h, b.n + 1)
                    for h in range(HEADS):
                        pe.wait_ge(s_w, HEADS * b.n + (h + 1))
                        for a, w in pieces(nb * P):
                            m = pe.matmul(G[:, h, a:a + w], hst[:, b.slot, :], y[:, b.slot, h, a:a + w],
                                          start=b.start, stop=False, skip_group_check=True)
                    m.then_inc(s_free, 1)
                tile_loop(pe, first, nb, i * total, products, signs, peel=True)
                pe.wait_ge(s_free, RING + (i + 1) * total)
                pe.sem_inc(s_sum, 1)
                pe.wait_ge(s_gs, HEADS * (i + 1))
                for b in range(nb):
                    q = first + b
                    if q >= 2:
                        pe.wait_ge(s_es, q - 1)
                    for h in range(HEADS):
                        m = pe.matmul(pj[:, q % 2, h * C:(h + 1) * C], gs[:, h, b * P:(b + 1) * P],
                                      wg[:, h, :], start=True, stop=True)
                    m.then_inc(s_pj, 1)


def graph_attention(nc, t, T, E, XR, signs):
    T["path"] = "signed_" if len(signs) == 2 else "positive_"
    for engine in (nc.sync, nc.gpsimd, nc.scalar, nc.vector, nc.tensor):
        engine.nop()
    with nc.sbuf_tensor(T["path"] + "NM", [P, HEADS, NP], F32) as NM:
        T["NM"] = NM[:]
        columns_program(nc, t, T)
        with ExitStack() as ctx:
            big = lambda name: ctx.enter_context(nc.sbuf_tensor(T["path"] + name, [P, NP], F32))[:]
            T["EB"] = [big(f"EB{h}") for h in range(HEADS)]
            T["S"] = [NM[:, h, :] for h in range(HEADS)]
            T["AR"] = [XR[:].rearrange("p b c -> p (b c)"), big("AR1")]
            for si, sign in enumerate(signs):
                scores_program(nc, t, T, si, sign)
        spread_program(nc, t, T, signs)
        T["ES"] = E[:].rearrange("p (b c) -> p b c", c=C)
        gat_program(nc, t, T, signs)


def transpose_all(pe, ps, src, eye, s_done, s_free, base=0):
    for k, (b0, nb) in enumerate(QCH):
        if base + k >= 2:
            pe.wait_ge(s_free, base + k - 1)
        for b in range(nb):
            m = pe.transpose(ps[:, (base + k) % 2, b * P:(b + 1) * P], src[:, b0 + b, :], eye)
        m.then_inc(s_done, 1)


def gru_program(nc, t, T):
    H, NS, ES, X, HTR, EST, OT = (T[k] for k in ("H", "NS", "ES", "X", "HTR", "EST", "OT"))
    nk = len(QCH)
    with ExitStack() as ctx:
        sem = lambda name: ctx.enter_context(nc.semaphore(name))
        tile = lambda name, shape: ctx.enter_context(nc.sbuf_tensor("u_" + name, shape, F32))
        ps = ctx.enter_context(nc.psum_tensor("u_ps", [P, 8, BANK], F32))
        wi, wh = tile("wi", [P, 2, 3 * C]), tile("wh", [P, 2, 3 * C])
        bi, bh, brz = tile("bi", [P, 2, 3]), tile("bh", [P, 2, 3]), tile("brz", [P, 2, 3])
        rz, pre, cand, mix = (tile(n, [P, 2, 2 * BANK]) for n in ("rz", "pre", "cand", "mix"))
        s_in, s_tr, s_trc, s_brz, s_slot, s_mm, s_rz, s_pre, s_cand, s_mix, s_o, s_to, s_x2, s_gfree = map(
            sem, ("u_in", "u_tr", "u_trc", "u_brz", "u_slot", "u_mm", "u_rz", "u_pre", "u_cand",
                  "u_mix", "u_o", "u_to", "u_x2", "u_gfree"))
        NIN = 9
        block = ctx.enter_context(nc.Block())

        @block.sync
        def _(sp):
            sp.dma_start(X, t["x"].rearrange("(b p) c -> p b c", p=P)).then_inc(s_in, 16)
            for g, kind in enumerate(("edge", "node")):
                sp.dma_start(wi[:, g, :], t[kind + "_WihT"]).then_inc(s_in, 16)
                sp.dma_start(wh[:, g, :], t[kind + "_WhhT"]).then_inc(s_in, 16)
                sp.dma_start(bi[:, g, :], t[kind + "_bih"]).then_inc(s_in, 16)
                sp.dma_start(bh[:, g, :], t[kind + "_bhh"]).then_inc(s_in, 16)
            sp.wait_ge(s_in, 16 * NIN)

        @block.tensor
        def _(pe):
            transpose_all(pe, ps, H, T["eye"][:], s_tr, s_trc)
            transpose_all(pe, ps, ES, T["eye"][:], s_tr, s_trc, nk)
            pe.wait_ge(s_in, 16 * NIN)
            pe.wait_ge(s_trc, 2 * nk)

            def gates(c0, c, w):
                for g, src in enumerate((NS, EST)):
                    pe.wait_ge(s_slot, 2 * c + g + 1)
                    b = 4 * g
                    s, h = src[:, ds(c0, w)], HTR[:, ds(c0, w)]
                    for k in range(2):
                        pe.matmul(ps[:, b + k, 0:w], wi[:, g, k * C:(k + 1) * C], s, start=True, stop=False)
                        pe.matmul(ps[:, b + k, 0:w], wh[:, g, k * C:(k + 1) * C], h, start=False, stop=True)
                    pe.matmul(ps[:, b + 2, 0:w], wi[:, g, 2 * C:3 * C], s, start=True, stop=True)
                    pe.matmul(ps[:, b + 3, 0:w], wh[:, g, 2 * C:3 * C], h, start=True,
                              stop=True).then_inc(s_mm, 1)
            chunk_loop(pe, gates)
            pe.wait_ge(s_o, 2 * nk)
            for k, (b0, nb) in enumerate(QCH):
                if k >= 2:
                    pe.wait_ge(s_x2, QCH[k - 2][0] + QCH[k - 2][1])
                for b in range(nb):
                    m = pe.transpose(ps[:, k % 2, b * P:(b + 1) * P], OT[:, (b0 + b) * P:(b0 + b + 1) * P],
                                     T["eye"][:])
                m.then_inc(s_to, 1)

        @block.scalar
        def _(a):
            for i, dst in enumerate((HTR, EST)):
                for k, (b0, nb) in enumerate(QCH):
                    a.wait_ge(s_tr, i * nk + k + 1)
                    a.copy(dst[:, b0 * P:(b0 + nb) * P], ps[:, (i * nk + k) % 2, 0:nb * P]).then_inc(s_trc, 1)
            a.wait_ge(s_brz, 1)

            def act(c0, c, w):
                for g in range(2):
                    b = 4 * g
                    a.wait_ge(s_mm, 2 * c + g + 1)
                    a.wait_ge(s_gfree, 2 * c + g + 1)
                    for k in range(2):
                        i = a.activation(rz[:, g, k * BANK:k * BANK + w], ps[:, b + k, 0:w], ACT.Sigmoid,
                                         bias=brz[:, g, k:k + 1])
                    i.then_inc(s_rz, 1)
                    a.wait_ge(s_pre, 4 * c + 2 * g + 2)
                    a.activation(cand[:, g, 0:w], pre[:, g, 0:w], ACT.Tanh,
                                 bias=bi[:, g, 2:3]).then_inc(s_cand, 1)
            chunk_loop(a, act)

        @block.vector
        def _(v):
            v.sem_inc(s_slot, 2)
            v.sem_inc(s_gfree, 2)
            v.wait_ge(s_in, 16 * NIN)
            v.tensor_tensor(brz[:], bi[:], bh[:], ALU.add).then_inc(s_brz, 1)

            def cells(c0, c, w):
                for g in range(2):
                    b = 4 * g
                    m = 2 * c + g
                    v.wait_ge(s_rz, m + 1)
                    v.scalar_tensor_tensor(pre[:, g, 0:w], ps[:, b + 3, 0:w], bh[:, g, 2:3],
                                           rz[:, g, 0:w], ALU.add, ALU.mult).then_inc(s_pre, 1)
                    v.wait_ge(s_pre, 2 * m + 1)
                    v.tensor_tensor(pre[:, g, 0:w], pre[:, g, 0:w], ps[:, b + 2, 0:w],
                                    ALU.add).then_inc(s_pre, 1)
                    v.wait_ge(s_cand, m + 1)
                    v.sem_inc(s_slot, 1)
                    v.tensor_tensor(mix[:, g, 0:w], HTR[:, ds(c0, w)], cand[:, g, 0:w],
                                    ALU.subtract).then_inc(s_mix, 1)
                    v.wait_ge(s_mix, 3 * m + 1)
                    v.tensor_tensor(mix[:, g, 0:w], mix[:, g, 0:w], rz[:, g, BANK:BANK + w],
                                    ALU.mult).then_inc(s_mix, 1)
                    v.wait_ge(s_mix, 3 * m + 2)
                    if g == 0:
                        v.tensor_tensor(OT[:, ds(c0, w)], mix[:, g, 0:w], cand[:, g, 0:w],
                                        ALU.add).then_inc(s_mix, 1)
                        v.wait_ge(s_mix, 3 * m + 3)
                        v.sem_inc(s_o, 1)
                        v.sem_inc(s_gfree, 1)
                    else:
                        v.tensor_tensor(mix[:, g, 0:w], mix[:, g, 0:w], cand[:, g, 0:w],
                                        ALU.add).then_inc(s_mix, 1)
                        v.wait_ge(s_mix, 3 * m + 3)
                        v.sem_inc(s_gfree, 1)
                        v.tensor_tensor(OT[:, ds(c0, w)], OT[:, ds(c0, w)], mix[:, g, 0:w],
                                        ALU.add).then_inc(s_o, 1)
            chunk_loop(v, cells)
            for b in range(NB):
                v.wait_ge(s_to, b // 4 + 1)
                v.scalar_tensor_tensor(X[:, b, :], ps[:, (b // 4) % 2, (b % 4) * P:(b % 4 + 1) * P],
                                       T["dcol"][:, b:b + 1], X[:, b, :], ALU.mult, ALU.add).then_inc(s_x2, 1)


def rms_sum(v, step, x, sq, total):
    step(v.tensor_tensor(sq, x, x, ALU.mult))
    step(v.tensor_reduce(total, sq, AX, ALU.add))


def turned_to(engine, s_tr, s_out, ps, dst, scale):
    for k, (b0, nb) in enumerate(QCH):
        engine.wait_ge(s_tr, k + 1)
        engine.activation(dst[:, b0 * P:(b0 + nb) * P], ps[:, k % 2, 0:nb * P], ACT.Copy,
                          scale=scale).then_inc(s_out, 1)


def chunk_loop(engine, body):
    full = NP // BANK
    with engine.Fori(0, full) as c:
        body(c * BANK, c, BANK)
    body(full * BANK, full, NP - full * BANK)


def qkv_program(nc, t, T):
    X, XL, HT, QA, QB, KA, KB, V = (T[k] for k in ("X", "XL", "HT", "QA", "QB", "KA", "KB", "V"))
    nk, full = len(QCH), NP // BANK
    KVD = KV * HD
    with ExitStack() as ctx:
        sem = lambda name: ctx.enter_context(nc.semaphore("q_" + name))
        tile = lambda name, shape, dt=F32: ctx.enter_context(nc.sbuf_tensor("q_" + name, shape, dt))
        ps = ctx.enter_context(nc.psum_tensor("q_ps", [P, 8, BANK], F32))
        sq = r = tile("sq", [P, NB, C])
        mean, var, ms = tile("mean", [P, NB]), tile("var_", [P, NB]), tile("ms", [P, NB])
        ln = tile("ln", [P, 1])
        wq, wqp, wk, wkp, wv = (tile(n, [P, m]) for n, m in (
            ("wq", C), ("wqp", C), ("wk", KVD), ("wkp", KVD), ("wv", KVD)))
        cs = tile("cs", [P, 2, 2, BANK])
        rot = tile("rot", [P, 2, 2, BANK])
        parts = [tile("part" + n, [P, 2, NP], BF16) for n in ("h", "m", "l")]
        s_in, s_dve, s_var, s_rt, s_ms, s_rt2, s_r, s_tr, s_ht = map(
            sem, ("in", "dve", "var", "rt", "ms", "rt2", "r", "tr", "ht"))
        s_v, s_vc, s_mm, s_slot, s_rot, s_rc, s_part, s_stack = map(
            sem, ("v", "vc", "mm", "slot", "rot", "rc", "part", "stack"))
        s_cs = slot_sems(ctx, nc, "q_cs")
        s_csfree = sem("csfree")
        NIN = 6
        block = ctx.enter_context(nc.Block())

        @block.sync
        def _(sp):
            for dst, name in ((ln, "ln1"), (wq, "wqT"), (wqp, "wqpT"), (wk, "wkT"), (wkp, "wkpT"), (wv, "wvT")):
                sp.dma_start(dst[:], t[name]).then_inc(s_in, 16)

            def tables(col, c, u, w):
                sp.wait_ge(s_csfree, c + 1)
                sp.dma_start(cs[:, u, :, 0:w], t["rope"][:, :, ds(col, w)]).then_inc(s_cs[u], 16)
            with sp.Fori(0, full // 2) as k:
                for u in range(2):
                    tables(k * (2 * BANK) + u * BANK, 2 * k + u, u, BANK)
            tables(full * BANK, full, full % 2, NP - full * BANK)
            sp.wait_ge(s_part, full + 1)
            hi, mid, lo = parts
            n = 0
            for i, (dst, heads, order) in enumerate((
                    (QA, AH, (hi, hi, mid)), (QB, AH, (hi, mid, lo)),
                    (KA, KV, (hi, mid, hi)), (KB, KV, (lo, mid, hi)))):
                for h in range(heads):
                    for j, part in enumerate(order):
                        sp.dma_start(dst[HD * j:HD * (j + 1), h, :],
                                     part[HD * h:HD * (h + 1), i // 2, :]).then_inc(s_stack, 16)
                        n += 1
            sp.wait_ge(s_stack, 16 * n)

        @block.vector
        def _(v):
            step = chain(v, s_dve)
            v.sem_inc(s_csfree, 2)
            v.sem_inc(s_slot, 1)
            v.memset(KA[3 * HD:3 * HD + 2, :, :], 1.0)
            step(v.memset(V[:, :, :, HD:HD + 1], 1.0))
            row_stats(v, step, X, XL, sq[:], mean[:], var[:])
            v.sem_inc(s_var, 1)
            v.wait_ge(s_rt, 1)
            step(v.reciprocal(mean[:], var[:]))
            step(v.tensor_tensor(XL, XL, mean[:].unsqueeze(2).to_broadcast([P, NB, C]), ALU.mult))
            rms_sum(v, step, XL, sq[:], ms[:])
            v.sem_inc(s_ms, 1)
            v.wait_ge(s_rt2, 1)
            step(v.reciprocal(mean[:], ms[:]))
            v.tensor_tensor(r[:], XL, mean[:].unsqueeze(2).to_broadcast([P, NB, C]), ALU.mult).then_inc(s_r, 1)
            for k in range((NB + 7) // 8):
                nb = min(8, NB - 8 * k)
                v.wait_ge(s_v, k + 1)
                v.tensor_copy(V[:, 8 * k:8 * k + nb, :, 0:HD],
                              ps[:, 4 + k, 0:nb * KVD].rearrange("p (b k d) -> p b k d", b=nb, k=KV)
                              ).then_inc(s_vc, 1)

            def rotate(col, c, u, landed, w):
                v.wait_ge(s_mm, c + 1)
                v.wait_ge(s_cs[u], landed)
                for i, rows in enumerate((P, KVD)):
                    for j in range(2):
                        m = v.tensor_tensor(rot[0:rows, i, j, 0:w], ps[0:rows, 2 * i + j, 0:w],
                                            cs[0:rows, u, j, 0:w], ALU.mult)
                m.then_inc(s_rot, 1)
                v.wait_ge(s_rot, 6 * c + 1)
                v.sem_inc(s_slot, 1)
                v.sem_inc(s_csfree, 1)
                both = [(rot[0:rows, i, 0, 0:w], rot[0:rows, i, 1, 0:w],
                         *(p[0:rows, i, ds(col, w)] for p in parts)) for i, rows in enumerate((P, KVD))]
                for x, y, hi, mid, lo in both:
                    m = v.tensor_tensor(x, x, y, ALU.add)
                m.then_inc(s_rot, 1)
                v.wait_ge(s_rot, 6 * c + 2)
                for x, y, hi, mid, lo in both:
                    m = v.tensor_copy(hi, x)
                m.then_inc(s_rot, 1)
                v.wait_ge(s_rot, 6 * c + 3)
                for x, y, hi, mid, lo in both:
                    m = v.tensor_tensor(x, x, hi, ALU.subtract)
                m.then_inc(s_rot, 1)
                v.wait_ge(s_rot, 6 * c + 4)
                for x, y, hi, mid, lo in both:
                    m = v.tensor_copy(mid, x)
                m.then_inc(s_rot, 1)
                v.wait_ge(s_rot, 6 * c + 5)
                for x, y, hi, mid, lo in both:
                    m = v.tensor_tensor(lo, x, mid, ALU.subtract)
                m.then_inc(s_rot, 1)
                v.wait_ge(s_rot, 6 * c + 6)
                v.sem_inc(s_part, 1)
            with v.Fori(0, full // 2) as k:
                for u in range(2):
                    rotate(k * (2 * BANK) + u * BANK, 2 * k + u, u, 16 * k + 16, BANK)
            rotate(full * BANK, full, full % 2, 16 * (full // 2) + 16, NP - full * BANK)

        @block.scalar
        def _(a):
            a.wait_ge(s_var, 1)
            a.activation(var[:], var[:], ACT.Sqrt, bias=T["eps"][:, 0:1], scale=1.0 / C).then_inc(s_rt, 1)
            a.wait_ge(s_ms, 1)
            a.activation(ms[:], ms[:], ACT.Sqrt, bias=T["eps"][:, 1:2], scale=1.0 / C).then_inc(s_rt2, 1)
            a.wait_ge(s_in, 16 * NIN)
            turned_to(a, s_tr, s_ht, ps, HT, ln[:])

        @block.tensor
        def _(pe):
            pe.wait_ge(s_r, 1)
            transpose_all(pe, ps, r[:], T["eye"][:], s_tr, s_ht)
            pe.wait_ge(s_ht, nk)
            for b in range(NB):
                m = pe.matmul(ps[:, 4 + b // 8, (b % 8) * KVD:(b % 8 + 1) * KVD],
                              HT[:, b * P:(b + 1) * P], wv[:], start=True, stop=True)
                if b % 8 == 7 or b == NB - 1:
                    m.then_inc(s_v, 1)

            def project(col, c, w):
                pe.wait_ge(s_slot, c + 1)
                h = HT[:, ds(col, w)]
                pe.matmul(ps[:, 0, 0:w], wq[:], h, start=True, stop=True)
                pe.matmul(ps[:, 1, 0:w], wqp[:], h, start=True, stop=True)
                pe.matmul(ps[0:KVD, 2, 0:w], wk[:], h, start=True, stop=True)
                pe.matmul(ps[0:KVD, 3, 0:w], wkp[:], h, start=True, stop=True).then_inc(s_mm, 1)
            chunk_loop(pe, project)


def maxima_program(nc, t, T):
    QA, KA = T["QA"], T["KA"]
    with ExitStack() as ctx:
        sem = lambda name: ctx.enter_context(nc.semaphore("m_" + name))
        tile = lambda name, shape, dt=F32: ctx.enter_context(nc.sbuf_tensor("m_" + name, shape, dt))
        ps = ctx.enter_context(nc.psum_tensor("m_ps", [P, 8, BANK], F32))
        pm = tile("pm", [P, len(QCH), AH, 4])
        mx, hi, rest, lo = (tile(n, [P, AH, 4], dt) for n, dt in (
            ("mx", F32), ("hi", BF16), ("rest", F32), ("lo", BF16)))
        dg = tile("dg", [P, 2, AH, 4 * P], BF16)
        s_mm, s_red, s_dve, s_dg, s_row, s_rowc = map(sem, ("mm", "red", "dve", "dg", "row", "rowc"))
        before = [AH * sum(c + 1 for c in range(n)) for n in range(len(QCH) + 1)]
        block = ctx.enter_context(nc.Block())

        @block.tensor
        def _(pe):
            pe.sem_inc(s_red, 2)
            for c, (q0, nb) in enumerate(QCH):
                def scores(key, i, c, nb, q0, last):
                    for h in range(AH):
                        g = h % 2
                        pe.wait_ge(s_red, i + (h + 1))
                        for s in range(nb):
                            q = (q0 + s) * P
                            w = min(BANK, NP - c * BANK) if last else BANK
                            m = pe.matmul(ps[:, 4 * g + s, 0:w], QA[0:STACK, h, q:q + P],
                                          KA[0:STACK, h // (AH // KV), ds(key, w)],
                                          start=True, stop=not last)
                            if last:
                                m = pe.matmul(ps[:, 4 * g + s, 0:w], T["eyeb"][:], T["cmask"][:, s, 0:w],
                                              start=False, stop=True)
                        m.then_inc(s_mm, 1)
                if c:
                    with pe.Fori(0, c) as kc:
                        scores(kc * BANK, AH * kc + before[c], c, nb, q0, False)
                scores(c * BANK, AH * c + before[c], c, nb, q0, True)
                pe.wait_ge(s_dg, c + 1)
                pe.wait_ge(s_red, before[c + 1] + 2)
                for h in range(AH):
                    for k in range(2):
                        m = pe.matmul(ps[STACK:STACK + 2, 4 + h, 0:nb * P], T["pick"][:, k, :],
                                      dg[:, k, h, 0:nb * P], start=(k == 0), stop=(k == 1),
                                      tile_position=(0, STACK))
                m.then_inc(s_row, 1)
                pe.wait_ge(s_rowc, c + 1)

        @block.vector
        def _(v):
            step = chain(v, s_dve)
            for c, (q0, nb) in enumerate(QCH):
                def reduce(i, kc, w):
                    for h in range(AH):
                        v.wait_ge(s_mm, i + (h + 1))
                        v.tensor_reduce(pm[:, ds(kc, 1), h, 0:nb].rearrange("p k s -> p (k s)"),
                                        ps[:, 4 * (h % 2):4 * (h % 2) + nb, 0:w], AX, ALU.max
                                        ).then_inc(s_red, 1)
                if c:
                    with v.Fori(0, c) as kc:
                        reduce(AH * kc + before[c], kc, BANK)
                reduce(AH * c + before[c], c, min(BANK, NP - c * BANK))
                v.wait_ge(s_red, before[c + 1] + 2)
                if c:
                    step(v.tensor_reduce(mx[:, :, 0:nb], pm[:, 0:c + 1, :, 0:nb].rearrange("p k h s -> p h s k"),
                                         AX, ALU.max))
                else:
                    step(v.tensor_copy(mx[:, :, 0:nb], pm[:, 0, :, 0:nb]))
                step(v.tensor_scalar(hi[:, :, 0:nb], mx[:, :, 0:nb], -1.0, None, ALU.mult))
                step(v.scalar_tensor_tensor(rest[:, :, 0:nb], mx[:, :, 0:nb], -1.0, hi[:, :, 0:nb],
                                            ALU.mult, ALU.subtract))
                step(v.tensor_copy(lo[:, :, 0:nb], rest[:, :, 0:nb]))
                if c:
                    v.wait_ge(s_row, c)
                for k, part in enumerate((hi, lo)):
                    for h in range(AH):
                        m = v.tensor_tensor(dg[:, k, h, 0:nb * P].rearrange("p (s i) -> p s i", s=nb),
                                            T["eyeb"][:].unsqueeze(1).to_broadcast([P, nb, P]),
                                            part[:, h, 0:nb].unsqueeze(2).to_broadcast([P, nb, P]), ALU.mult)
                m.then_inc(s_dg, 1)

        @block.scalar
        def _(a):
            for c, (q0, nb) in enumerate(QCH):
                a.wait_ge(s_row, c + 1)
                a.copy(QA[STACK:STACK + 2, :, q0 * P:(q0 + nb) * P],
                       ps[STACK:STACK + 2, 4:8, 0:nb * P]).then_inc(s_rowc, 1)


def attention_program(nc, t, T):
    QA, QB, KA, KB, V, XL = (T[k] for k in ("QA", "QB", "KA", "KB", "V", "XL"))
    REP = AH // KV
    with ExitStack() as ctx:
        sem = lambda name: ctx.enter_context(nc.semaphore("t_" + name))
        tile = lambda name, shape, dt=F32: ctx.enter_context(nc.sbuf_tensor("t_" + name, shape, dt))
        S = ctx.enter_context(nc.psum_tensor("t_S", [P, AH, BANK], F32))
        O = ctx.enter_context(nc.psum_tensor("t_O", [P, AH, BANK], F32))
        pt = tile("pt", [P, 2, AH, BANK])
        vst = tile("vst", [P, 2, KV, HD + 1])
        os_ = tile("os", [HD + 1, AH, BANK])
        wo = tile("wo", [HD + 1, AH, C + 1])
        rd = tile("rd", [P, NB, AH])
        s_in, s_v, s_s, s_e, s_pv, s_o, s_os, s_pj, s_x, s_rd = map(
            sem, ("in", "v", "s", "e", "pv", "o", "os", "pj", "x", "rd"))
        base = [sum(4 * c + QCH[c][1] for c in range(n)) for n in range(len(QCH) + 1)]
        block = ctx.enter_context(nc.Block())

        def key_loop(engine, c, nb, body, peel=False):
            k0 = 0
            if c:
                if peel:
                    for u in range(2):
                        body(u, base[c] + u, u, 0, u == 0)
                    k0 = 1
                with engine.Fori(k0, 2 * c) as k:
                    for u in range(2):
                        body(2 * k + u, 2 * k + (base[c] + u), u, 0, False)
            for i in range(nb):
                body(4 * c + i, base[c] + 4 * c + i, i % 2, i * P, c == 0 and i == 0)

        @block.sync
        def _(sp):
            sp.dma_start(wo[:], t["woT"]).then_inc(s_in, 16)
            sp.wait_ge(s_in, 16)

        @block.gpsimd
        def _(g):
            for c, (q0, nb) in enumerate(QCH):
                def stage(kb, n, u, col, start):
                    g.wait_ge(s_pv, n + 1)
                    g.tensor_copy(vst[:, u, :, :], V[:, ds(kb, 1), :, :].rearrange(
                        "p b k d -> p (b k) d")).then_inc(s_v, 1)
                key_loop(g, c, nb, stage)

        @block.tensor
        def _(pe):
            pe.sem_inc(s_pv, 2)
            pe.wait_ge(s_in, 16)
            for c, (q0, nb) in enumerate(QCH):
                w = nb * P

                def keys(kb, n, u, col, start):
                    diagonal = isinstance(kb, int) and kb >= 4 * c
                    for h in range(AH):
                        pe.wait_ge(s_e, AH * n + (h + 1))
                        q = slice(q0 * P + col, q0 * P + w)
                        pe.matmul(S[:, h, col:w], KA[0:STACK + 2, h // REP, ds(kb * P, P)],
                                  QA[0:STACK + 2, h, q], start=True, stop=False)
                        m = pe.matmul(S[:, h, col:w], KB[0:STACK, h // REP, ds(kb * P, P)],
                                      QB[0:STACK, h, q], start=False, stop=not diagonal)
                        if diagonal:
                            m = pe.matmul(S[:, h, col:col + P], T["eyeb"][:], T["cmaskT"][:],
                                          start=False, stop=True)
                        m.then_inc(s_s, 1)
                    pe.wait_ge(s_v, n + 1)
                    for h in range(AH):
                        pe.wait_ge(s_e, AH * n + (AH + h + 1))
                        m = pe.matmul(O[0:HD + 1, h, col:w], vst[:, u, h // REP, :], pt[:, u, h, col:w],
                                      start=start, stop=False, skip_group_check=True)
                    m.then_inc(s_pv, 1)
                key_loop(pe, c, nb, keys, peel=True)
                pe.wait_ge(s_pv, 2 + base[c + 1])
                pe.sem_inc(s_o, 1)
                pe.wait_ge(s_os, c + 1)
                for s in range(nb):
                    b = q0 + s
                    if b >= 2:
                        pe.wait_ge(s_x, b - 1)
                    for h in range(AH):
                        m = pe.matmul(S[:, 2 * (b % 2) + h // 2, (h % 2) * (C + 1):(h % 2 + 1) * (C + 1)],
                                      os_[:, h, s * P:(s + 1) * P], wo[:, h, :], start=True, stop=True)
                    m.then_inc(s_pj, 1)
                pe.wait_ge(s_x, q0 + nb)

        @block.scalar
        def _(a):
            a.sem_inc(s_e, AH)
            for c, (q0, nb) in enumerate(QCH):
                w = nb * P

                def exps(kb, n, u, col, start):
                    a.wait_ge(s_pv, n + 1)
                    for h in range(AH):
                        a.wait_ge(s_s, AH * n + (h + 1))
                        a.activation(pt[:, u, h, col:w], S[:, h, col:w], ACT.Exp,
                                     scale=float(HD) ** -0.5).then_inc(s_e, 1)
                key_loop(a, c, nb, exps)
                a.wait_ge(s_o, c + 1)
                if c:
                    a.wait_ge(s_pj, q0)
                a.copy(os_[:, :, 0:w], O[0:HD + 1, :, 0:w]).then_inc(s_os, 1)

        @block.vector
        def _(v):
            for b in range(NB):
                v.wait_ge(s_pj, b + 1)
                two = S[:, 2 * (b % 2):2 * (b % 2) + 2, 0:2 * (C + 1)].rearrange("p a (h c) -> p a h c", h=2)
                v.reciprocal(rd[:, b, :].rearrange("p (a h) -> p a h", a=2), two[:, :, :, C]).then_inc(s_rd, 1)
                v.wait_ge(s_rd, AH * b + 1)
                for h in range(AH):
                    m = v.scalar_tensor_tensor(XL[:, b, :], two[:, h // 2, h % 2, 0:C], rd[:, b, h:h + 1],
                                               XL[:, b, :], ALU.mult, ALU.add)
                    if h < AH - 1:
                        m.then_inc(s_rd, 1)
                        v.wait_ge(s_rd, AH * b + h + 2)
                    else:
                        m.then_inc(s_x, 1)


def experts_program(nc, t, T, out):
    X, XL, HT = T["X"], T["XL"], T["HT"]
    full = NP // BANK
    with ExitStack() as ctx:
        sem = lambda name: ctx.enter_context(nc.semaphore("e_" + name))
        tile = lambda name, shape, dt=F32: ctx.enter_context(nc.sbuf_tensor("e_" + name, shape, dt))
        ps = ctx.enter_context(nc.psum_tensor("e_ps", [P, 8, BANK], F32))
        sq = r = tile("sq", [P, NB, C])
        ms, inv, ln = tile("ms", [P, NB]), tile("inv", [P, NB]), tile("ln", [P, 1])
        rw, tie = tile("rw", [P, NE]), tile("tie", [P, NE, NE])
        w1, w3, w2 = tile("w1", [P, NE, HID]), tile("w3", [P, NE, HID]), tile("w2", [P, NE, len(HTILES), C])
        pr, sel = tile("pr", [P, NB, NE]), tile("sel", [P, NB, NE])
        big = [tile(f"pair{k}", [P, NB, NE, NE]) for k in range(2)]
        red = tile("red", [P, NB])
        wt = tile("wt", [P, NB, NE])
        sg = tile("sg", [P, 2, len(HTILES), BANK])
        s_in, s_w, s_dve, s_ms, s_rt, s_r, s_tr, s_ht, s_lg, s_ex, s_exd = map(
            sem, ("in", "w", "dve", "ms", "rt", "r", "tr", "ht", "lg", "ex", "exd"))
        s_gu, s_sg, s_hh, s_y, s_yc, s_out = map(sem, ("gu", "sg", "hh", "y", "yc", "out"))
        nt = len(HTILES)
        block = ctx.enter_context(nc.Block())

        @block.sync
        def _(sp):
            for dst, name in ((ln, "ln2"), (rw, "routerT"), (tie, "tie")):
                sp.dma_start(dst[:], t[name]).then_inc(s_in, 16)
            sp.dma_start(w1[:], t["w1T"]).then_inc(s_w, 16)
            sp.dma_start(w3[:], t["w3T"]).then_inc(s_w, 16)
            for i, (r0, rows) in enumerate(HTILES):
                sp.dma_start(w2[0:rows, :, i, :], t["w2T"][r0:r0 + rows]).then_inc(s_w, 16)
            sp.wait_ge(s_out, 1)
            sp.dma_start(out.rearrange("(b p) c -> p b c", p=P), X).then_inc(s_out, 16)
            sp.wait_ge(s_out, 17)

        @block.vector
        def _(v):
            step = chain(v, s_dve)
            rms_sum(v, step, XL, sq[:], ms[:])
            v.sem_inc(s_ms, 1)
            v.wait_ge(s_rt, 1)
            step(v.reciprocal(inv[:], ms[:]))
            v.tensor_tensor(r[:], XL, inv[:].unsqueeze(2).to_broadcast([P, NB, C]), ALU.mult).then_inc(s_r, 1)
            v.wait_ge(s_lg, 1)
            lg = ps[:, 7, 0:NB * NE].rearrange("p (b e) -> p b e", e=NE)
            step(v.tensor_reduce(red[:], lg, AX, ALU.max))
            v.tensor_tensor(pr[:], lg, red[:].unsqueeze(2).to_broadcast([P, NB, NE]), ALU.subtract).then_inc(s_ex, 1)
            v.wait_ge(s_exd, 1)
            step(v.tensor_reduce(red[:], pr[:], AX, ALU.add))
            step(v.reciprocal(inv[:], red[:]))
            step(v.tensor_tensor(pr[:], pr[:], inv[:].unsqueeze(2).to_broadcast([P, NB, NE]), ALU.mult))
            v.wait_ge(s_in, 48)
            for b in range(NB):
                mine = pr[:, b, :].unsqueeze(2).to_broadcast([P, NE, NE])
                other = pr[:, b, :].unsqueeze(1).to_broadcast([P, NE, NE])
                v.tensor_tensor(big[0][:, b], other, mine, ALU.is_gt)
                m = v.tensor_tensor(big[1][:, b], other, mine, ALU.is_equal)
            step(m)
            step(v.tensor_tensor(big[1][:].rearrange("p b e j -> p b (e j)"),
                                 big[1][:].rearrange("p b e j -> p b (e j)"),
                                 tie[:].rearrange("p e j -> p (e j)").unsqueeze(1).to_broadcast([P, NB, NE * NE]),
                                 ALU.mult))
            step(v.tensor_tensor(big[0][:].rearrange("p b e j -> p (b e j)"),
                                 big[0][:].rearrange("p b e j -> p (b e j)"),
                                 big[1][:].rearrange("p b e j -> p (b e j)"), ALU.add))
            step(v.tensor_reduce(sel[:].rearrange("p b e -> p (b e)"),
                                 big[0][:].rearrange("p b e j -> p (b e) j"), AX, ALU.add))
            step(v.scalar_tensor_tensor(wt[:].rearrange("p b e -> p (b e)"), sel[:].rearrange("p b e -> p (b e)"),
                                        float(TOPK), pr[:].rearrange("p b e -> p (b e)"), ALU.is_lt, ALU.mult))
            step(v.tensor_reduce(red[:], wt[:], AX, ALU.add))
            step(v.tensor_scalar(red[:], red[:], 1e-9, None, ALU.add))
            step(v.reciprocal(inv[:], red[:]))
            step(v.tensor_tensor(wt[:], wt[:], inv[:].unsqueeze(2).to_broadcast([P, NB, NE]), ALU.mult))

            def combine(b0, c, w, e):
                v.wait_ge(s_y, NE * c + (e + 3))
                for s in range(w // P):
                    x = XL[:, ds(b0 + s, 1), :].rearrange("p b c -> p (b c)")
                    m = v.scalar_tensor_tensor(x, ps[:, 6 + e % 2, s * P:(s + 1) * P],
                                               wt[:, ds(b0 + s, 1), e], x, ALU.mult, ALU.add)
                m.then_inc(s_yc, 1)

            def experts(col, b0, c, w):
                for e in range(NE):
                    for i, (r0, rows) in enumerate(HTILES):
                        v.wait_ge(s_sg, nt * NE * c + (nt * e + i + 1))
                        h = sg[0:rows, e % 2, i, 0:w]
                        v.tensor_tensor(h, h, ps[0:rows, 2 * i + 1, 0:w], ALU.mult).then_inc(s_hh, 1)
                        if i == 1 and e:
                            combine(b0, c, w, e - 1)
                combine(b0, c, w, NE - 1)
            with v.Fori(0, full) as c:
                experts(c * BANK, c * 4, c, BANK)
            experts(full * BANK, full * 4, full, NP - full * BANK)
            v.wait_ge(s_yc, NE * (full + 1) + 2)
            v.tensor_tensor(X, X, XL, ALU.add).then_inc(s_out, 1)

        @block.scalar
        def _(a):
            a.wait_ge(s_ms, 1)
            a.activation(ms[:], ms[:], ACT.Sqrt, bias=T["eps"][:, 1:2], scale=1.0 / C).then_inc(s_rt, 1)
            a.wait_ge(s_in, 48)
            turned_to(a, s_tr, s_ht, ps, HT, ln[:])
            a.wait_ge(s_ex, 1)
            a.activation(pr[:], pr[:], ACT.Exp).then_inc(s_exd, 1)

            def silus(col, c, w):
                for e in range(NE):
                    for i, (r0, rows) in enumerate(HTILES):
                        a.wait_ge(s_gu, nt * NE * c + (nt * e + i + 1))
                        a.wait_ge(s_y, NE * c + (e + 1))
                        a.activation(sg[0:rows, e % 2, i, 0:w], ps[0:rows, 2 * i, 0:w],
                                     ACT.Silu).then_inc(s_sg, 1)
            chunk_loop(a, silus)

        @block.tensor
        def _(pe):
            pe.wait_ge(s_r, 1)
            transpose_all(pe, ps, r[:], T["eye"][:], s_tr, s_ht)
            pe.wait_ge(s_ht, len(QCH))
            pe.wait_ge(s_in, 48)
            for b in range(NB):
                m = pe.matmul(ps[:, 7, b * NE:(b + 1) * NE], HT[:, b * P:(b + 1) * P], rw[:],
                              start=True, stop=True)
            m.then_inc(s_lg, 1)
            pe.wait_ge(s_w, 16 * (2 + nt))
            pe.wait_ge(s_ex, 1)
            pe.sem_inc(s_y, 2)
            pe.sem_inc(s_yc, 2)
            pe.sem_inc(s_hh, nt)

            def down(c, w, e):
                pe.wait_ge(s_hh, nt * NE * c + (nt * (e + 2)))
                pe.wait_ge(s_yc, NE * c + (e + 1))
                for s in range(w // P):
                    for i, (r0, rows) in enumerate(HTILES):
                        m = pe.matmul(ps[:, 6 + e % 2, s * P:(s + 1) * P], sg[0:rows, e % 2, i, s * P:(s + 1) * P],
                                      w2[0:rows, e, i, :], start=(i == 0), stop=(i == nt - 1))
                m.then_inc(s_y, 1)

            def experts(col, c, w):
                h = HT[:, ds(col, w)]
                for e in range(NE):
                    for i, (r0, rows) in enumerate(HTILES):
                        pe.wait_ge(s_hh, nt * NE * c + (nt * e + i + 1))
                        pe.matmul(ps[0:rows, 2 * i, 0:w], w1[:, e, r0:r0 + rows], h, start=True, stop=True)
                        pe.matmul(ps[0:rows, 2 * i + 1, 0:w], w3[:, e, r0:r0 + rows], h, start=True,
                                  stop=True).then_inc(s_gu, 1)
                        if i == 0 and e:
                            down(c, w, e - 1)
                down(c, w, NE - 1)
            chunk_loop(pe, experts)


def build(nc, t, out):
    with ExitStack() as ctx:
        sb = lambda name, shape, dt=F32: ctx.enter_context(nc.sbuf_tensor(name, shape, dt))
        T = {}
        T["eye"], T["noteye"], T["ones"] = sb("eye", [P, P]), sb("noteye", [P, P]), sb("ones", [P, P])
        T["eps"] = sb("eps", [P, 2])
        T["dcol"] = sb("dcol", [P, NB])
        XR = sb("XR", [P, NB, C])
        with ExitStack() as graph:
            gb = lambda name, shape, dt=F32: graph.enter_context(nc.sbuf_tensor(name, shape, dt))
            T["selE"], T["selB"] = gb("selE", [EP, EROWS]), gb("selB", [EP, EROWS, P])
            T["Ecol"], T["EcolN"] = gb("Ecol", [P, NB * EROWS]), gb("EcolN", [P, NB * EROWS])
            T["nmax"], T["den"] = gb("nmax", [P, 2, NB * HEADS]), gb("den", [P, 2, NB * HEADS])
            T["rden"] = gb("rden", [P, NB * HEADS])
            T["signed"] = gb("signed", [P, 1], I32)
            H = gb("H", [P, NB, C])
            NS = gb("NS", [P, NP])
            T["H"], T["NS"] = H[:], NS[:]
            with ExitStack() as c1:
                E = c1.enter_context(nc.sbuf_tensor("E", [P, NP], F32))
                T["E"] = E[:]
                with ExitStack() as c2:
                    T["U3"] = c2.enter_context(nc.sbuf_tensor("U3", [P, NB, 2, EW], BF16))
                    with ExitStack() as c3:
                        T["X"] = XR[:]
                        T["SQ"] = c3.enter_context(nc.sbuf_tensor("SQ", [P, NB, C], F32))[:]
                        T["HTR"] = c3.enter_context(nc.sbuf_tensor("HT1", [P, NP], F32))[:]
                        norm_program(nc, t, T)
                    spmm_program(nc, t, T)
                shared = {}
                T["sem"] = lambda name: shared.get(name) or shared.setdefault(
                    name, graph.enter_context(nc.semaphore(name)))
                signed = nc.values_load(T["signed"][0:1, 0:1], min_val=0, max_val=1)
                with nc.If(signed > 0):
                    graph_attention(nc, t, T, E, XR, (1, -1))
                with nc.Else():
                    graph_attention(nc, t, T, E, XR, (1,))
                T["ES"] = E[:].rearrange("p (b c) -> p b c", c=C)
                with ExitStack() as c6:
                    big = lambda name: c6.enter_context(nc.sbuf_tensor(name, [P, NP], F32))[:]
                    T["X"] = XR[:]
                    T["HTR"], T["EST"], T["OT"] = big("HT2"), big("EST"), big("OT")
                    gru_program(nc, t, T)

        T["eyeb"], T["cmask"] = sb("eyeb", [P, P], BF16), sb("cmask", [P, 4, BANK], BF16)
        T["cmaskT"], T["pick"] = sb("cmaskT", [P, P], BF16), sb("pick", [P, 2, 2], BF16)
        T["XL"] = sb("XL", [P, NB, C])[:]
        T["HT"] = sb("HT", [P, NP])[:]
        load_masks(nc, t, T)
        with ExitStack() as attn:
            ab = lambda name, shape, dt=F32: attn.enter_context(nc.sbuf_tensor(name, shape, dt))[:]
            T["QA"], T["QB"] = ab("QA", [P, AH, NP], BF16), ab("QB", [P, AH, NP], BF16)
            T["KA"], T["KB"] = ab("KA", [P, KV, NP], BF16), ab("KB", [P, KV, NP], BF16)
            T["V"] = ab("V", [P, NB, KV, HD + 1])
            qkv_program(nc, t, T)
            maxima_program(nc, t, T)
            attention_program(nc, t, T)
        experts_program(nc, t, T, out)


def load_masks(nc, t, T):
    with nc.semaphore("c_in") as s, nc.sbuf_tensor("c_f", [P, 4 * BANK + 2 * P + 4], F32) as f, \
            nc.semaphore("c_w") as s_w, nc.Block() as block:
        parts = [(T["cmask"][:].rearrange("p s k -> p (s k)"), 0, 4 * BANK), (T["cmaskT"][:], 4 * BANK, P),
                 (T["eyeb"][:], 4 * BANK + P, P),
                 (T["pick"][:].rearrange("p k m -> p (k m)"), 4 * BANK + 2 * P, 4)]

        @block.sync
        def _(sp):
            sp.dma_start(f[:], t["masks"]).then_inc(s, 16)

        @block.vector
        def _(v):
            v.wait_ge(s, 16)
            for dst, a, w in parts:
                v.tensor_copy(dst, f[:, a:a + w]).then_inc(s_w, 1)
            v.wait_ge(s_w, len(parts))


def kernel(x, adj, **w):
    import numpy as np
    import concourse.bacc as bacc
    from concourse import mybir as mb
    from concourse.bass_utils import run_bass_kernel_spmd as run

    pad = NP - N
    f32 = np.float32
    a = {}
    a["x"] = np.pad(np.asarray(x), ((0, pad), (0, 0)))
    A = np.pad(np.asarray(adj), ((0, pad), (0, pad)))
    a["adj"] = A
    a["adjT"] = np.ascontiguousarray(A.T)
    a["diag"] = np.ascontiguousarray(np.diagonal(A).reshape(NB, P).T)
    a["gat_W"] = np.asarray(w["L0_gnn_gat_W"])
    a["gat_WT"] = np.ascontiguousarray(a["gat_W"].transpose(0, 2, 1))
    a["gat_a"] = np.ascontiguousarray(np.asarray(w["L0_gnn_gat_a"]).reshape(HEADS, 2, C).transpose(2, 0, 1))
    for kind in ("edge", "node"):
        a[kind + "_WihT"] = np.ascontiguousarray(np.asarray(w[f"L0_gnn_{kind}_Wih"]).T)
        a[kind + "_WhhT"] = np.ascontiguousarray(np.asarray(w[f"L0_gnn_{kind}_Whh"]).T)
        a[kind + "_bih"] = np.ascontiguousarray(np.asarray(w[f"L0_gnn_{kind}_bih"]).reshape(3, C).T)
        a[kind + "_bhh"] = np.ascontiguousarray(np.asarray(w[f"L0_gnn_{kind}_bhh"]).reshape(3, C).T)
    a["eye"] = np.eye(P, dtype=f32)
    a["noteye"] = 1 - np.eye(P, dtype=f32)
    selE = np.zeros((2, EW, EROWS), f32)
    for part in range(PARTS):
        selE[:, 1 + part * EROWS + np.arange(EROWS), np.arange(EROWS)] = 1
    a["selE"] = selE.reshape(EP, EROWS)
    a["selB"] = np.ascontiguousarray(np.broadcast_to(a["selE"][:, :, None], (EP, EROWS, P)))
    inv = 1.0 / 10000.0 ** (np.arange(0, HD, 2, dtype=f32) / HD)
    ang = np.outer(np.arange(NP, dtype=f32), inv)
    ang = np.concatenate([ang, ang], axis=1).T
    sign = np.where(np.arange(HD) < HD // 2, -1, 1).astype(f32)[:, None]
    rope = np.stack([np.cos(ang), np.sin(ang) * sign], axis=1).astype(f32)
    a["rope"] = np.ascontiguousarray(np.tile(rope, (AH, 1, 1)))
    q, k = np.arange(P), np.arange(BANK)
    low = f32(-1e30)
    cm = np.stack([np.where(k[None] > q[:, None] + s * P, low, 0) for s in range(4)], axis=1)
    pick = np.broadcast_to(np.eye(2, dtype=f32), (P, 2, 2))
    a["masks"] = np.ascontiguousarray(np.concatenate(
        [cm.reshape(P, -1), np.where(q[:, None] > q[None], low, 0), np.eye(P), pick.reshape(P, 4)],
        axis=1).astype(f32))
    a["tie"] = np.ascontiguousarray(np.broadcast_to(np.tril(np.ones((NE, NE), f32), -1), (P, NE, NE)))

    half = np.concatenate([np.arange(HD // 2, HD), np.arange(HD // 2)])
    wq, wk, wv, wo = (np.asarray(w["L0_ffn_" + n]) for n in ("wq", "wk", "wv", "wo"))
    a["wqT"] = np.ascontiguousarray(wq.T)
    a["wkT"] = np.ascontiguousarray(wk.T)
    a["wqpT"] = np.ascontiguousarray(wq.reshape(AH, HD, C)[:, half].reshape(AH * HD, C).T)
    a["wkpT"] = np.ascontiguousarray(wk.reshape(KV, HD, C)[:, half].reshape(KV * HD, C).T)
    a["wvT"] = np.ascontiguousarray(wv.T)
    woT = np.zeros((HD + 1, AH, C + 1), f32)
    woT[0:HD, :, 0:C] = wo.reshape(C, AH, HD).transpose(2, 1, 0)
    woT[HD, :, C] = 1
    a["woT"] = woT
    a["ln1"] = np.asarray(w["L0_ffn_ln1_w"]).reshape(C, 1)
    a["ln2"] = np.asarray(w["L0_ffn_ln2_w"]).reshape(C, 1)
    a["routerT"] = np.ascontiguousarray(np.asarray(w["L0_ffn_router_w"]).T)
    a["w1T"] = np.ascontiguousarray(np.asarray(w["L0_ffn_w1"]).transpose(2, 0, 1))
    a["w3T"] = np.ascontiguousarray(np.asarray(w["L0_ffn_w3"]).transpose(2, 0, 1))
    a["w2T"] = np.ascontiguousarray(np.asarray(w["L0_ffn_w2"]).transpose(2, 0, 1))

    nc = bacc.Bacc("TRN2", target_bir_lowering=False, num_devices=1)
    arrays, t = {}, {}
    for name, v in a.items():
        arrays["in_" + name] = v
        t[name] = nc.dram_tensor("in_" + name, v.shape, mb.dt.from_np(v.dtype), kind="ExternalInput").ap()
    out = nc.dram_tensor("out_0", (NP, C), mb.dt.float32, kind="ExternalOutput").ap()
    build(nc, t, out)
    r = run(nc, [arrays], core_ids=[0])
    return r.results[0]["out_0"][:N]
```

```python
from contextlib import ExitStack

import concourse.bass as bass
from concourse import mybir

P = 128
N = 3327
NB = (N + P - 1) // P
NP = NB * P
C = 128
HEADS = 3
ALPHA = 0.2
NEG_INF = -9000000000000000.0
LOWEST = -3.0e38
PARTS = 3
EROWS = 2 * HEADS
EW = 32
EP = 2 * EW
RING = 4
LN_EPS = 1e-5
BANK = 512

SWEEPS = [(0, 14), (14, 12)]
CHUNKS = [(0, 8), (8, 6), (14, 6), (20, 6)]

AH, KV, HD = 4, 2, 32
NE, TOPK, HID = 8, 2, 341
RMS_EPS = 1e-6
STACK = PARTS * HD
HTILES = [(0, 128), (128, 128), (256, 85)]
QCH = [(4 * c, min(4, NB - 4 * c)) for c in range((NB + 3) // 4)]

ALU = mybir.AluOpType
ACT = mybir.ActivationFunctionType
F32 = mybir.dt.float32
BF16 = mybir.dt.bfloat16
I32 = mybir.dt.int32
AX = mybir.AxisListType.X
ds = bass.ds


def pieces(cols, size=BANK):
    return [(a, min(size, cols - a)) for a in range(0, cols, size)]


def chain(engine, sem):
    done = [0]

    def step(instruction):
        done[0] += 1
        instruction.then_inc(sem, 1)
        engine.wait_ge(sem, done[0])
    return step


def row_stats(v, step, x, xc, sq, mean, var):
    step(v.tensor_reduce(mean, x, AX, ALU.add))
    step(v.tensor_scalar(mean, mean, 1.0 / C, None, ALU.mult))
    step(v.tensor_tensor(xc, x, mean.unsqueeze(2).to_broadcast([P, NB, C]), ALU.subtract))
    step(v.tensor_tensor(sq, xc, xc, ALU.mult))
    step(v.tensor_reduce(var, sq, AX, ALU.add))


def norm_program(nc, t, T):
    X, H, SQ, HTR = T["X"], T["H"], T["SQ"], T["HTR"]
    with ExitStack() as ctx:
        sem = lambda name: ctx.enter_context(nc.semaphore(name))
        ps = ctx.enter_context(nc.psum_tensor("n_ps", [P, 8, BANK], F32))
        s_x, s_c, s_dve, s_var, s_rt, s_h = map(sem, ("n_x", "n_c", "n_dve", "n_var", "n_rt", "n_h"))
        s_tr, s_ht, s_u, s_uc, s_U = map(sem, ("n_tr", "n_ht", "n_u", "n_uc", "n_U"))
        mean = ctx.enter_context(nc.sbuf_tensor("n_mean", [P, NB], F32))
        var = ctx.enter_context(nc.sbuf_tensor("n_var_t", [P, NB], F32))
        wt = ctx.enter_context(nc.sbuf_tensor("n_wt", [P, HEADS, C], F32))
        av = ctx.enter_context(nc.sbuf_tensor("n_av", [P, HEADS, 2], F32))
        uc = ctx.enter_context(nc.sbuf_tensor("n_ucol", [P, 2, HEADS], F32))
        U = ctx.enter_context(nc.sbuf_tensor("n_Uf", [P, NB, EROWS], F32))
        Ub = ctx.enter_context(nc.sbuf_tensor("n_Ub", [P, NB, EROWS], BF16))
        banks = [(b0, min(4, NB - b0)) for b0 in range(0, NB, 4)]
        block = ctx.enter_context(nc.Block())

        @block.sync
        def _(sp):
            sp.dma_start(X, t["x"].rearrange("(b p) c -> p b c", p=P)).then_inc(s_x, 16)
            sp.dma_start(T["eye"][:], t["eye"]).then_inc(s_c, 16)
            sp.dma_start(T["noteye"][:], t["noteye"]).then_inc(s_c, 16)
            sp.dma_start(T["dcol"][:], t["diag"]).then_inc(s_c, 16)
            sp.dma_start(wt[:], t["gat_WT"].rearrange("h c d -> c h d")).then_inc(s_c, 16)
            sp.dma_start(av[:], t["gat_a"]).then_inc(s_c, 16)
            sp.dma_start(T["selE"][:], t["selE"]).then_inc(s_c, 16)
            sp.dma_start(T["selB"][:], t["selB"]).then_inc(s_c, 16)
            sp.wait_ge(s_x, 16)
            sp.wait_ge(s_c, 16 * 7)

        @block.vector
        def _(v):
            step = chain(v, s_dve)
            v.memset(T["ones"][:], 1.0)
            v.memset(T["eps"][:, 0:1], LN_EPS)
            v.memset(T["eps"][:, 1:2], RMS_EPS)
            step(v.memset(T["U3"][:], 0.0))
            step(v.memset(T["U3"][:, :, 1, 0:1], 1.0))
            v.wait_ge(s_x, 16)
            row_stats(v, step, X, H, SQ, mean[:], var[:])
            v.sem_inc(s_var, 1)
            v.wait_ge(s_rt, 1)
            step(v.reciprocal(mean[:], var[:]))
            v.tensor_tensor(H, H, mean[:].unsqueeze(2).to_broadcast([P, NB, C]), ALU.mult).then_inc(s_h, 1)
            v.wait_ge(s_u, 1)
            v.tensor_copy(uc[:], ps[:, 7, 0:EROWS].rearrange("p (h k) -> p k h", k=2)).then_inc(s_uc, 1)
            v.wait_ge(s_U, 1)
            step(v.tensor_copy(U[:], ps[:, 7, 8:8 + NB * EROWS].rearrange("p (b e) -> p b e", e=EROWS)))
            for k in range(PARTS):
                step(v.tensor_copy(Ub[:], U[:]))
                e0 = 1 + k * EROWS
                v.tensor_copy(T["U3"][:, :, 0, e0:e0 + EROWS], Ub[:])
                v.tensor_copy(T["U3"][:, :, 1, e0:e0 + HEADS], Ub[:, :, HEADS:EROWS])
                step(v.tensor_copy(T["U3"][:, :, 1, e0 + HEADS:e0 + EROWS], Ub[:, :, 0:HEADS]))
                step(v.tensor_tensor(U[:], U[:], Ub[:], ALU.subtract))

        @block.scalar
        def _(a):
            a.wait_ge(s_var, 1)
            a.activation(var[:], var[:], ACT.Sqrt, bias=T["eps"][:, 0:1], scale=1.0 / C).then_inc(s_rt, 1)
            for k, (b0, nb) in enumerate(banks):
                a.wait_ge(s_tr, k + 1)
                a.copy(HTR[:, b0 * P:(b0 + nb) * P], ps[:, k % 6, 0:nb * P]).then_inc(s_ht, 1)

        @block.tensor
        def _(pe):
            pe.wait_ge(s_c, 16 * 7)
            for h in range(HEADS):
                m = pe.matmul(ps[:, 7, 2 * h:2 * h + 2], wt[:, h, :], av[:, h, :], start=True, stop=True)
            m.then_inc(s_u, 1)
            pe.wait_ge(s_h, 1)
            for k, (b0, nb) in enumerate(banks):
                if k >= 6:
                    pe.wait_ge(s_ht, k - 5)
                for b in range(nb):
                    m = pe.transpose(ps[:, k % 6, b * P:(b + 1) * P], H[:, b0 + b, :], T["eye"][:])
                m.then_inc(s_tr, 1)
            pe.wait_ge(s_ht, len(banks))
            pe.wait_ge(s_uc, 1)
            for b in range(NB):
                o = 8 + b * EROWS
                m = pe.matmul(ps[:, 7, o:o + EROWS], HTR[:, b * P:(b + 1) * P],
                              uc[:].rearrange("p k h -> p (k h)"), start=True, stop=True)
            m.then_inc(s_U, 1)


def slot_sems(ctx, nc, name, slots=2):
    return [ctx.enter_context(nc.semaphore(f"{name}{u}")) for u in range(slots)]


class Tile:

    def __init__(self, row, n, slot, landed, diagonal, fixed, start, sign):
        self.row, self.n, self.slot, self.landed = row, n, slot, landed
        self.diagonal, self.fixed, self.start, self.sign = diagonal, fixed, start, sign


def tile_loop(engine, first, blocks, base, body, signs=(1,), peel=False):
    n = base
    for si, sign in enumerate(signs):
        for start, count, diagonal in ((first, blocks, True), (first + blocks, NB - first - blocks, False),
                                       (0, first, False)):
            def tile(k, at):
                m = n + at
                return Tile(RING * k + (start + at), RING * k + m, m % RING,
                            16 * k + 16 * (m // RING + 1), diagonal,
                            RING * k + (first * len(signs) + si * blocks + at + 1), m == base, sign)
            lead = min(RING, count) if peel and n == base else 0
            for at in range(lead):
                body(tile(0, at))
            turns = (count - lead) // RING
            if turns:
                with engine.Fori(0, turns) as k:
                    for u in range(RING):
                        body(tile(k, lead + u))
            for at in range(lead + turns * RING, count):
                body(tile(0, at))
            n += count


def spmm_program(nc, t, T):
    H, NS, E = T["H"], T["NS"], T["E"]
    W = max(b for _, b in SWEEPS) * P
    with ExitStack() as ctx:
        sem = lambda name: ctx.enter_context(nc.semaphore("a_" + name))
        tile = lambda name, shape, dt=F32: ctx.enter_context(nc.sbuf_tensor("a_" + name, shape, dt))
        at, mp, mm = tile("at", [P, RING, W]), tile("mp", [P, RING, W], BF16), tile("mm", [P, RING, W], BF16)
        hst, ust = tile("h", [P, RING, C]), tile("u", [P, RING, 2, EW], BF16)
        neg = tile("neg", [P, 1])
        ps = ctx.enter_context(nc.psum_tensor("a_ps", [P, 4 * BANK], F32))
        pe_e = ctx.enter_context(nc.psum_tensor("a_pe", [P, 4 * BANK], F32))
        s_tile = slot_sems(ctx, nc, "a_tile", RING)
        s_free, s_fix, s_mask, s_w, s_sum, s_out, s_neg = map(
            sem, ("free", "fix", "mask", "w", "sum", "out", "neg"))
        block = ctx.enter_context(nc.Block())

        @block.sync
        def _(sp):
            for i, (first, nb) in enumerate(SWEEPS):
                def load(b):
                    sp.wait_ge(s_free, b.n + 1)
                    sp.dma_start(at[:, b.slot, 0:nb * P], t["adjT"][ds(b.row * P, P), first * P:(first + nb) * P]
                                 ).then_inc(s_tile[b.slot], 16)
                tile_loop(sp, first, nb, i * NB, load)
            sp.wait_ge(s_neg, 2)

        @block.gpsimd
        def _(g):
            for i, (first, nb) in enumerate(SWEEPS):
                def stage(b):
                    g.wait_ge(s_free, b.n + 1)
                    g.tensor_copy(hst[:, b.slot, :], H[:, ds(b.row, 1), :].rearrange("p b c -> p (b c)"))
                    g.tensor_copy(ust[:, b.slot, :, :], T["U3"][:, ds(b.row, 1), :, :].rearrange(
                        "p b k e -> p (b k) e")).then_inc(s_w, 1)
                tile_loop(g, first, nb, i * NB, stage)
            g.wait_ge(s_neg, 2)

        @block.vector
        def _(v):
            for i, (first, nb) in enumerate(SWEEPS):
                def masks(b):
                    v.wait_ge(s_tile[b.slot], b.landed)
                    tile = at[:, b.slot, 0:nb * P]
                    if b.diagonal:
                        d = at[:, b.slot, ds((b.row - first) * P, P)]
                        v.tensor_tensor(d, d, T["noteye"][:], ALU.mult).then_inc(s_fix, 1)
                        v.wait_ge(s_fix, b.fixed)
                    v.wait_ge(s_free, b.n + 1)
                    v.tensor_scalar(mp[:, b.slot, 0:nb * P], tile, 0.0, None, ALU.is_gt)
                    v.tensor_scalar(mm[:, b.slot, 0:nb * P], tile, 0.0, None, ALU.is_lt).then_inc(s_mask, 1)
                tile_loop(v, first, nb, i * NB, masks)
                v.wait_ge(s_sum, i + 1)
                v.tensor_copy(E[0:EP, first * P:(first + nb) * P], pe_e[0:EP, 0:nb * P]).then_inc(s_out, 1)
            v.wait_ge(s_out, 2 * len(SWEEPS))
            v.tensor_reduce(neg[0:1, :], E[EW:EW + 1, :], AX, ALU.max).then_inc(s_neg, 1)
            v.wait_ge(s_neg, 1)
            v.tensor_scalar(T["signed"][0:1, :], neg[0:1, :], 0.0, None, ALU.is_gt).then_inc(s_neg, 1)
            v.wait_ge(s_neg, 2)

        @block.scalar
        def _(a):
            for i, (first, nb) in enumerate(SWEEPS):
                a.wait_ge(s_sum, i + 1)
                a.copy(NS[:, first * P:(first + nb) * P], ps[:, 0:nb * P]).then_inc(s_out, 1)
            a.wait_ge(s_neg, 2)

        @block.tensor
        def _(pe):
            pe.sem_inc(s_free, RING)
            for i, (first, nb) in enumerate(SWEEPS):
                if i:
                    pe.wait_ge(s_out, 2 * i)
                def products(b):
                    u = b.slot
                    pe.wait_ge(s_w, b.n + 1)
                    pe.wait_ge(s_mask, b.n + 1)
                    for a, w in pieces(nb * P):
                        pe.matmul(ps[:, a:a + w], hst[:, u, :], at[:, u, a:a + w],
                                  start=b.start, stop=False, skip_group_check=True)
                        for k, mask in enumerate((mp, mm)):
                            m = pe.matmul(pe_e[k * EW:(k + 1) * EW, a:a + w], ust[:, u, k, :], mask[:, u, a:a + w],
                                          start=b.start, stop=False, skip_group_check=True,
                                          tile_position=(0, k * EW))
                    m.then_inc(s_free, 1)
                tile_loop(pe, first, nb, i * NB, products, peel=True)
                pe.wait_ge(s_free, RING + (i + 1) * NB)
                pe.sem_inc(s_sum, 1)
            pe.wait_ge(s_neg, 2)


def columns_program(nc, t, T):
    E, Ecol = T["E"], T["Ecol"]
    with ExitStack() as ctx:
        ps = ctx.enter_context(nc.psum_tensor(T["path"] + "c_ps", [P, BANK], F32))
        s_col, s_dve = (T["sem"](n) for n in ("c_col", "c_dve"))
        block = ctx.enter_context(nc.Block())

        @block.tensor
        def _(pe):
            for b in range(NB):
                m = pe.matmul(ps[:, b * EROWS:(b + 1) * EROWS], E[0:EP, b * P:(b + 1) * P],
                              T["selE"][:], start=True, stop=True)
            m.then_inc(s_col, 1)

        @block.vector
        def _(v):
            step = chain(v, s_dve)
            v.wait_ge(s_col, 1)
            step(v.tensor_copy(Ecol[:], ps[:, 0:NB * EROWS]))
            step(v.scalar_tensor_tensor(Ecol[:], Ecol[:], ALPHA, Ecol[:], ALU.mult, ALU.max))
            step(v.tensor_scalar(T["EcolN"][:], Ecol[:], -1.0, None, ALU.mult))


def scores_program(nc, t, T, si, sign):
    E, EB, S, AR = T["E"], T["EB"], T["S"], T["AR"]
    nmax, den = T["nmax"][:, si], T["den"][:, si]
    cols, pre = pieces(NP), T["path"] + f"r{si}_"
    with ExitStack() as ctx:
        sem = lambda name: T["sem"](f"r{si}_{name}")
        mx = ctx.enter_context(nc.sbuf_tensor(pre + "mx", [P, 2, HEADS], F32))
        nm = ctx.enter_context(nc.sbuf_tensor(pre + "nm", [P, 2, HEADS], F32))
        ps = ctx.enter_context(nc.psum_tensor(pre + "ps", [P, 8, BANK], F32))
        s_a = [sem(f"a{u}") for u in range(2)]
        s_eb, s_ebc, s_dve, s_afree, s_fix, s_bias, s_go, s_max, s_nm, s_exp = map(
            sem, ("eb", "ebc", "dve", "afree", "fix", "bias", "go", "max", "nm", "exp"))
        block = ctx.enter_context(nc.Block())

        @block.sync
        def _(sp):
            with sp.Fori(0, NB // 2) as k:
                for u in range(2):
                    n = 2 * k + u
                    sp.wait_ge(s_afree, n + 1)
                    sp.dma_start(AR[u], t["adj"][ds(n * P, P), :]).then_inc(s_a[u], 16)

        @block.vector
        def _(v):
            v.sem_inc(s_afree, 2)
            step = chain(v, s_dve)
            for h in range(HEADS):
                v.wait_ge(s_ebc, (h + 1) * len(cols))
                step(v.scalar_tensor_tensor(EB[h], EB[h], ALPHA, EB[h], ALU.mult, ALU.max))
            with v.Fori(0, NB // 2) as k:
                for u in range(2):
                    n = 2 * k + u
                    v.wait_ge(s_a[u], 16 * k + 16)
                    d = AR[u][:, ds(n * P, P)]
                    v.tensor_tensor(d, d, T["noteye"][:], ALU.mult).then_inc(s_fix, 1)
                    v.wait_ge(s_fix, n + 1)
                    v.tensor_scalar(AR[u], AR[u], 0.0, NEG_INF, ALU.is_le if sign > 0 else ALU.is_ge,
                                    ALU.mult).then_inc(s_bias, 1)
                    v.wait_ge(s_bias, n + 1)
                    for h in range(HEADS):
                        v.wait_ge(s_exp, 3 * n + (h + 1))
                        v.sem_inc(s_go, 1)
                        v.tensor_tensor_reduce(S[h], AR[u], EB[h], 1.0, LOWEST, ALU.add, ALU.max,
                                               mx[:, u, h:h + 1]).then_inc(s_max, 1)
                        v.wait_ge(s_max, 3 * n + (h + 1))
                        v.tensor_scalar(nm[:, u, h:h + 1], mx[:, u, h:h + 1], -1.0, None,
                                        ALU.mult).then_inc(s_nm, 1)
                    v.sem_inc(s_afree, 1)
                    v.wait_ge(s_nm, 3 * n + 3)
                    v.tensor_copy(nmax[:, ds(3 * n, HEADS)], nm[:, u, :])

        @block.scalar
        def _(a):
            a.sem_inc(s_exp, 3)
            for h in range(HEADS):
                for k, (c0, w) in enumerate(cols):
                    i = h * len(cols) + k
                    a.wait_ge(s_eb, i + 1)
                    a.copy(EB[h][:, c0:c0 + w], ps[:, i % 8, 0:w]).then_inc(s_ebc, 1)
            with a.Fori(0, NB // 2) as k:
                for u in range(2):
                    n = 2 * k + u
                    for h in range(HEADS):
                        a.wait_ge(s_nm, 3 * n + (h + 1))
                        a.activation(S[h], S[h], ACT.Exp, bias=nm[:, u, h:h + 1],
                                     accum_out=den[:, ds(3 * n + h, 1)]).then_inc(s_exp, 1)

        @block.tensor
        def _(pe):
            for h in range(HEADS):
                for k, (c0, w) in enumerate(cols):
                    i = h * len(cols) + k
                    if i >= 8:
                        pe.wait_ge(s_ebc, i - 7)
                    pe.matmul(ps[:, i % 8, 0:w], T["selB"][:, si * HEADS + h, :], E[0:EP, c0:c0 + w],
                              start=True, stop=True).then_inc(s_eb, 1)


def spread_program(nc, t, T, signs):
    NM, nmax, den, rden = T["NM"], T["nmax"], T["den"], T["rden"]
    with ExitStack() as ctx:
        sem = lambda name: T["sem"]("s_" + name)
        dg = ctx.enter_context(nc.sbuf_tensor(T["path"] + "s_dg", [P, 2, HEADS, P], F32))
        corr = ctx.enter_context(nc.sbuf_tensor(T["path"] + "s_corr", [P, 2, NB * HEADS], F32))
        ps = ctx.enter_context(nc.psum_tensor(T["path"] + "s_ps", [P, 2, BANK], F32))
        s_dve, s_corr, s_exp, s_diag, s_bc, s_bank = map(sem, ("dve", "corr", "exp", "diag", "bc", "bank"))
        block = ctx.enter_context(nc.Block())

        @block.vector
        def _(v):
            step = chain(v, s_dve)
            if len(signs) == 2:
                step(v.tensor_tensor(rden[:], nmax[:, 0], nmax[:, 1], ALU.min))
                for i in range(2):
                    m = v.tensor_tensor(corr[:, i], rden[:], nmax[:, i], ALU.subtract)
                m.then_inc(s_corr, 1)
                v.wait_ge(s_exp, 2)
                for i in range(2):
                    m = v.tensor_tensor(den[:, i], den[:, i], corr[:, i], ALU.mult)
                step(m)
                step(v.tensor_copy(nmax[:, 0], rden[:]))
                step(v.tensor_tensor(den[:, 0], den[:, 0], den[:, 1], ALU.add))
            step(v.tensor_scalar(den[:, 0], den[:, 0], float(HEADS), None, ALU.mult))
            step(v.reciprocal(rden[:], den[:, 0]))
            with v.Fori(0, NB // 2) as k:
                for u in range(2):
                    n = 2 * k + u
                    v.wait_ge(s_bc, n + 1)
                    v.tensor_tensor(dg[:, u], T["eye"][:].unsqueeze(1).to_broadcast([P, HEADS, P]),
                                    nmax[:, 0, ds(3 * n, HEADS)].unsqueeze(2).to_broadcast([P, HEADS, P]),
                                    ALU.mult).then_inc(s_diag, 1)

        @block.scalar
        def _(a):
            a.sem_inc(s_bank, 2)
            if len(signs) == 2:
                a.wait_ge(s_corr, 1)
                for i in range(2):
                    a.activation(corr[:, i], corr[:, i], ACT.Exp).then_inc(s_exp, 1)
            with a.Fori(0, NB // 2) as k:
                for u in range(2):
                    n = 2 * k + u
                    a.wait_ge(s_bc, n + 3)
                    a.copy(NM[:, :, ds(n * P, P)],
                           ps[:, u, 0:HEADS * P].rearrange("p (h i) -> p h i", h=HEADS)).then_inc(s_bank, 1)

        @block.tensor
        def _(pe):
            pe.sem_inc(s_bc, 2)
            with pe.Fori(0, NB // 2) as k:
                for u in range(2):
                    n = 2 * k + u
                    pe.wait_ge(s_diag, n + 1)
                    pe.wait_ge(s_bank, n + 1)
                    pe.matmul(ps[:, u, 0:HEADS * P], T["ones"][:], dg[:, u].rearrange("p h i -> p (h i)"),
                              start=True, stop=True).then_inc(s_bc, 1)


def gat_program(nc, t, T, signs):
    H, NM, ES = T["H"], T["NM"], T["ES"]
    W = max(b for _, b in CHUNKS) * P
    ON_ACT = HEADS - 1
    ND = HEADS - 1
    total = NB * len(signs)
    with ExitStack() as ctx:
        sem = lambda name: T["sem"]("g_" + name)
        tile = lambda name, shape: ctx.enter_context(nc.sbuf_tensor(T["path"] + "g_" + name, shape, F32))
        at, y, gs = tile("at", [P, RING, W]), tile("y", [P, RING, HEADS, W]), tile("gs", [P, HEADS, W])
        hst, wg = tile("h", [P, RING, C]), tile("w", [P, HEADS, C])
        G = ctx.enter_context(nc.psum_tensor(T["path"] + "g_G", [P, HEADS, 2 * BANK], F32))
        pj = ctx.enter_context(nc.psum_tensor(T["path"] + "g_pj", [P, 2, BANK], F32))
        s_tile = [sem(f"tile{u}") for u in range(RING)]
        s_wg, s_z, s_relu, s_afree, s_fix, s_sign, s_h, s_y, s_w, s_free = map(
            sem, ("wg", "z", "relu", "afree", "fix", "sign", "h", "y", "w", "free"))
        s_sum, s_gs, s_pj, s_es, s_dve = map(sem, ("sum", "gs", "pj", "es", "dve"))
        block = ctx.enter_context(nc.Block())

        @block.sync
        def _(sp):
            sp.dma_start(wg[:], t["gat_W"].rearrange("h d c -> d h c")).then_inc(s_wg, 16)
            for i, (first, nb) in enumerate(CHUNKS):
                def load(b):
                    sp.wait_ge(s_afree, b.n + 1)
                    sp.dma_start(at[:, b.slot, 0:nb * P], t["adjT"][ds(b.row * P, P), first * P:(first + nb) * P]
                                 ).then_inc(s_tile[b.slot], 16)
                tile_loop(sp, first, nb, i * total, load, signs)
            sp.wait_ge(s_wg, 16)

        @block.gpsimd
        def _(g):
            for i, (first, nb) in enumerate(CHUNKS):
                def stage(b):
                    g.wait_ge(s_free, b.n + 1)
                    g.tensor_copy(hst[:, b.slot, :],
                                  H[:, ds(b.row, 1), :].rearrange("p b c -> p (b c)")).then_inc(s_h, 1)
                tile_loop(g, first, nb, i * total, stage, signs)

        @block.scalar
        def _(a):
            for i, (first, nb) in enumerate(CHUNKS):
                def exps(b):
                    e0 = 0 if b.sign > 0 else HEADS
                    a.wait_ge(s_free, b.n + 1)
                    last = y[:, b.slot, ON_ACT, 0:nb * P]
                    a.activation(last, NM[:, ON_ACT, first * P:(first + nb) * P], ACT.Relu,
                                 bias=T["EcolN"][:, ds(b.row * EROWS + (e0 + ON_ACT), 1)],
                                 scale=-1.0).then_inc(s_relu, 1)
                    for h in range(ND):
                        yh = y[:, b.slot, h, 0:nb * P]
                        a.wait_ge(s_z, ND * b.n + (h + 1))
                        a.activation(yh, yh, ACT.Exp).then_inc(s_y, 1)
                    a.wait_ge(s_relu, b.n + 1)
                    a.activation(last, last, ACT.Exp, scale=-1.0).then_inc(s_y, 1)
                tile_loop(a, first, nb, i * total, exps, signs)
                a.wait_ge(s_sum, i + 1)
                if i:
                    a.wait_ge(s_es, first)
                for h in range(HEADS):
                    a.copy(gs[:, h, 0:nb * P], G[:, h, 0:nb * P]).then_inc(s_gs, 1)

        @block.vector
        def _(v):
            v.sem_inc(s_afree, RING)
            step = chain(v, s_dve)
            for i, (first, nb) in enumerate(CHUNKS):
                def weigh(b):
                    u = b.slot
                    e0 = 0 if b.sign > 0 else HEADS
                    v.wait_ge(s_free, b.n + 1)
                    for h in range(ND):
                        v.tensor_scalar(y[:, u, h, 0:nb * P], NM[:, h, first * P:(first + nb) * P],
                                        T["Ecol"][:, ds(b.row * EROWS + (e0 + h), 1)], 0.0, ALU.add,
                                        ALU.min).then_inc(s_z, 1)
                    v.wait_ge(s_tile[u], b.landed)
                    if b.diagonal:
                        d = at[:, u, ds((b.row - first) * P, P)]
                        v.tensor_tensor(d, d, T["noteye"][:], ALU.mult).then_inc(s_fix, 1)
                        v.wait_ge(s_fix, b.fixed)
                    if len(signs) == 2:
                        v.tensor_scalar(at[:, u, 0:nb * P], at[:, u, 0:nb * P], 0.0, None,
                                        ALU.max if b.sign > 0 else ALU.min).then_inc(s_sign, 1)
                        v.wait_ge(s_sign, b.n + 1)
                    for h in range(HEADS):
                        v.wait_ge(s_y, HEADS * b.n + (h + 1))
                        yh = y[:, u, h, 0:nb * P]
                        v.tensor_tensor(yh, yh, at[:, u, 0:nb * P], ALU.mult).then_inc(s_w, 1)
                    v.wait_ge(s_w, HEADS * b.n + HEADS)
                    v.sem_inc(s_afree, 1)
                tile_loop(v, first, nb, i * total, weigh, signs)
                for b in range(nb):
                    q = first + b
                    v.wait_ge(s_pj, q + 1)
                    for h in range(HEADS):
                        x, r = pj[:, q % 2, h * C:(h + 1) * C], T["rden"][:, HEADS * q + h:HEADS * q + h + 1]
                        if h == 0:
                            step(v.tensor_scalar(ES[:, q, :], x, r, None, ALU.mult))
                        elif h < HEADS - 1:
                            step(v.scalar_tensor_tensor(ES[:, q, :], x, r, ES[:, q, :], ALU.mult, ALU.add))
                        else:
                            v.scalar_tensor_tensor(ES[:, q, :], x, r, ES[:, q, :], ALU.mult,
                                                   ALU.add).then_inc(s_es, 1)

        @block.tensor
        def _(pe):
            pe.sem_inc(s_free, RING)
            pe.wait_ge(s_wg, 16)
            for i, (first, nb) in enumerate(CHUNKS):
                def products(b):
                    pe.wait_ge(s_h, b.n + 1)
                    for h in range(HEADS):
                        pe.wait_ge(s_w, HEADS * b.n + (h + 1))
                        for a, w in pieces(nb * P):
                            m = pe.matmul(G[:, h, a:a + w], hst[:, b.slot, :], y[:, b.slot, h, a:a + w],
                                          start=b.start, stop=False, skip_group_check=True)
                    m.then_inc(s_free, 1)
                tile_loop(pe, first, nb, i * total, products, signs, peel=True)
                pe.wait_ge(s_free, RING + (i + 1) * total)
                pe.sem_inc(s_sum, 1)
                pe.wait_ge(s_gs, HEADS * (i + 1))
                for b in range(nb):
                    q = first + b
                    if q >= 2:
                        pe.wait_ge(s_es, q - 1)
                    for h in range(HEADS):
                        m = pe.matmul(pj[:, q % 2, h * C:(h + 1) * C], gs[:, h, b * P:(b + 1) * P],
                                      wg[:, h, :], start=True, stop=True)
                    m.then_inc(s_pj, 1)


def graph_attention(nc, t, T, E, XR, signs):
    T["path"] = "signed_" if len(signs) == 2 else "positive_"
    for engine in (nc.sync, nc.gpsimd, nc.scalar, nc.vector, nc.tensor):
        engine.nop()
    with nc.sbuf_tensor(T["path"] + "NM", [P, HEADS, NP], F32) as NM:
        T["NM"] = NM[:]
        columns_program(nc, t, T)
        with ExitStack() as ctx:
            big = lambda name: ctx.enter_context(nc.sbuf_tensor(T["path"] + name, [P, NP], F32))[:]
            T["EB"] = [big(f"EB{h}") for h in range(HEADS)]
            T["S"] = [NM[:, h, :] for h in range(HEADS)]
            T["AR"] = [XR[:].rearrange("p b c -> p (b c)"), big("AR1")]
            for si, sign in enumerate(signs):
                scores_program(nc, t, T, si, sign)
        spread_program(nc, t, T, signs)
        T["ES"] = E[:].rearrange("p (b c) -> p b c", c=C)
        gat_program(nc, t, T, signs)


def transpose_all(pe, ps, src, eye, s_done, s_free, base=0):
    for k, (b0, nb) in enumerate(QCH):
        if base + k >= 2:
            pe.wait_ge(s_free, base + k - 1)
        for b in range(nb):
            m = pe.transpose(ps[:, (base + k) % 2, b * P:(b + 1) * P], src[:, b0 + b, :], eye)
        m.then_inc(s_done, 1)


def gru_program(nc, t, T):
    H, NS, ES, X, HTR, EST, OT = (T[k] for k in ("H", "NS", "ES", "X", "HTR", "EST", "OT"))
    nk = len(QCH)
    with ExitStack() as ctx:
        sem = lambda name: ctx.enter_context(nc.semaphore(name))
        tile = lambda name, shape: ctx.enter_context(nc.sbuf_tensor("u_" + name, shape, F32))
        ps = ctx.enter_context(nc.psum_tensor("u_ps", [P, 8, BANK], F32))
        wi, wh = tile("wi", [P, 2, 3 * C]), tile("wh", [P, 2, 3 * C])
        bi, bh, brz = tile("bi", [P, 2, 3]), tile("bh", [P, 2, 3]), tile("brz", [P, 2, 3])
        rz, pre, cand, mix = (tile(n, [P, 2, 2 * BANK]) for n in ("rz", "pre", "cand", "mix"))
        s_in, s_tr, s_trc, s_brz, s_slot, s_mm, s_rz, s_pre, s_cand, s_mix, s_o, s_to, s_x2, s_gfree = map(
            sem, ("u_in", "u_tr", "u_trc", "u_brz", "u_slot", "u_mm", "u_rz", "u_pre", "u_cand",
                  "u_mix", "u_o", "u_to", "u_x2", "u_gfree"))
        NIN = 9
        block = ctx.enter_context(nc.Block())

        @block.sync
        def _(sp):
            sp.dma_start(X, t["x"].rearrange("(b p) c -> p b c", p=P)).then_inc(s_in, 16)
            for g, kind in enumerate(("edge", "node")):
                sp.dma_start(wi[:, g, :], t[kind + "_WihT"]).then_inc(s_in, 16)
                sp.dma_start(wh[:, g, :], t[kind + "_WhhT"]).then_inc(s_in, 16)
                sp.dma_start(bi[:, g, :], t[kind + "_bih"]).then_inc(s_in, 16)
                sp.dma_start(bh[:, g, :], t[kind + "_bhh"]).then_inc(s_in, 16)
            sp.wait_ge(s_in, 16 * NIN)

        @block.tensor
        def _(pe):
            transpose_all(pe, ps, H, T["eye"][:], s_tr, s_trc)
            transpose_all(pe, ps, ES, T["eye"][:], s_tr, s_trc, nk)
            pe.wait_ge(s_in, 16 * NIN)
            pe.wait_ge(s_trc, 2 * nk)

            def gates(c0, c, w):
                for g, src in enumerate((NS, EST)):
                    pe.wait_ge(s_slot, 2 * c + g + 1)
                    b = 4 * g
                    s, h = src[:, ds(c0, w)], HTR[:, ds(c0, w)]
                    for k in range(2):
                        pe.matmul(ps[:, b + k, 0:w], wi[:, g, k * C:(k + 1) * C], s, start=True, stop=False)
                        pe.matmul(ps[:, b + k, 0:w], wh[:, g, k * C:(k + 1) * C], h, start=False, stop=True)
                    pe.matmul(ps[:, b + 2, 0:w], wi[:, g, 2 * C:3 * C], s, start=True, stop=True)
                    pe.matmul(ps[:, b + 3, 0:w], wh[:, g, 2 * C:3 * C], h, start=True,
                              stop=True).then_inc(s_mm, 1)
            chunk_loop(pe, gates)
            pe.wait_ge(s_o, 2 * nk)
            for k, (b0, nb) in enumerate(QCH):
                if k >= 2:
                    pe.wait_ge(s_x2, QCH[k - 2][0] + QCH[k - 2][1])
                for b in range(nb):
                    m = pe.transpose(ps[:, k % 2, b * P:(b + 1) * P], OT[:, (b0 + b) * P:(b0 + b + 1) * P],
                                     T["eye"][:])
                m.then_inc(s_to, 1)

        @block.scalar
        def _(a):
            for i, dst in enumerate((HTR, EST)):
                for k, (b0, nb) in enumerate(QCH):
                    a.wait_ge(s_tr, i * nk + k + 1)
                    a.copy(dst[:, b0 * P:(b0 + nb) * P], ps[:, (i * nk + k) % 2, 0:nb * P]).then_inc(s_trc, 1)
            a.wait_ge(s_brz, 1)

            def act(c0, c, w):
                for g in range(2):
                    b = 4 * g
                    a.wait_ge(s_mm, 2 * c + g + 1)
                    a.wait_ge(s_gfree, 2 * c + g + 1)
                    for k in range(2):
                        i = a.activation(rz[:, g, k * BANK:k * BANK + w], ps[:, b + k, 0:w], ACT.Sigmoid,
                                         bias=brz[:, g, k:k + 1])
                    i.then_inc(s_rz, 1)
                    a.wait_ge(s_pre, 4 * c + 2 * g + 2)
                    a.activation(cand[:, g, 0:w], pre[:, g, 0:w], ACT.Tanh,
                                 bias=bi[:, g, 2:3]).then_inc(s_cand, 1)
            chunk_loop(a, act)

        @block.vector
        def _(v):
            v.sem_inc(s_slot, 2)
            v.sem_inc(s_gfree, 2)
            v.wait_ge(s_in, 16 * NIN)
            v.tensor_tensor(brz[:], bi[:], bh[:], ALU.add).then_inc(s_brz, 1)

            def cells(c0, c, w):
                for g in range(2):
                    b = 4 * g
                    m = 2 * c + g
                    v.wait_ge(s_rz, m + 1)
                    v.scalar_tensor_tensor(pre[:, g, 0:w], ps[:, b + 3, 0:w], bh[:, g, 2:3],
                                           rz[:, g, 0:w], ALU.add, ALU.mult).then_inc(s_pre, 1)
                    v.wait_ge(s_pre, 2 * m + 1)
                    v.tensor_tensor(pre[:, g, 0:w], pre[:, g, 0:w], ps[:, b + 2, 0:w],
                                    ALU.add).then_inc(s_pre, 1)
                    v.wait_ge(s_cand, m + 1)
                    v.sem_inc(s_slot, 1)
                    v.tensor_tensor(mix[:, g, 0:w], HTR[:, ds(c0, w)], cand[:, g, 0:w],
                                    ALU.subtract).then_inc(s_mix, 1)
                    v.wait_ge(s_mix, 3 * m + 1)
                    v.tensor_tensor(mix[:, g, 0:w], mix[:, g, 0:w], rz[:, g, BANK:BANK + w],
                                    ALU.mult).then_inc(s_mix, 1)
                    v.wait_ge(s_mix, 3 * m + 2)
                    if g == 0:
                        v.tensor_tensor(OT[:, ds(c0, w)], mix[:, g, 0:w], cand[:, g, 0:w],
                                        ALU.add).then_inc(s_mix, 1)
                        v.wait_ge(s_mix, 3 * m + 3)
                        v.sem_inc(s_o, 1)
                        v.sem_inc(s_gfree, 1)
                    else:
                        v.tensor_tensor(mix[:, g, 0:w], mix[:, g, 0:w], cand[:, g, 0:w],
                                        ALU.add).then_inc(s_mix, 1)
                        v.wait_ge(s_mix, 3 * m + 3)
                        v.sem_inc(s_gfree, 1)
                        v.tensor_tensor(OT[:, ds(c0, w)], OT[:, ds(c0, w)], mix[:, g, 0:w],
                                        ALU.add).then_inc(s_o, 1)
            chunk_loop(v, cells)
            for b in range(NB):
                v.wait_ge(s_to, b // 4 + 1)
                v.scalar_tensor_tensor(X[:, b, :], ps[:, (b // 4) % 2, (b % 4) * P:(b % 4 + 1) * P],
                                       T["dcol"][:, b:b + 1], X[:, b, :], ALU.mult, ALU.add).then_inc(s_x2, 1)


def rms_sum(v, step, x, sq, total):
    step(v.tensor_tensor(sq, x, x, ALU.mult))
    step(v.tensor_reduce(total, sq, AX, ALU.add))


def turned_to(engine, s_tr, s_out, ps, dst, scale):
    for k, (b0, nb) in enumerate(QCH):
        engine.wait_ge(s_tr, k + 1)
        engine.activation(dst[:, b0 * P:(b0 + nb) * P], ps[:, k % 2, 0:nb * P], ACT.Copy,
                          scale=scale).then_inc(s_out, 1)


def chunk_loop(engine, body):
    full = NP // BANK
    with engine.Fori(0, full) as c:
        body(c * BANK, c, BANK)
    body(full * BANK, full, NP - full * BANK)


def qkv_program(nc, t, T):
    X, XL, HT, QA, QB, KA, KB, V = (T[k] for k in ("X", "XL", "HT", "QA", "QB", "KA", "KB", "V"))
    nk, full = len(QCH), NP // BANK
    KVD = KV * HD
    with ExitStack() as ctx:
        sem = lambda name: ctx.enter_context(nc.semaphore("q_" + name))
        tile = lambda name, shape, dt=F32: ctx.enter_context(nc.sbuf_tensor("q_" + name, shape, dt))
        ps = ctx.enter_context(nc.psum_tensor("q_ps", [P, 8, BANK], F32))
        sq = r = tile("sq", [P, NB, C])
        mean, var, ms = tile("mean", [P, NB]), tile("var_", [P, NB]), tile("ms", [P, NB])
        ln = tile("ln", [P, 1])
        wq, wqp, wk, wkp, wv = (tile(n, [P, m]) for n, m in (
            ("wq", C), ("wqp", C), ("wk", KVD), ("wkp", KVD), ("wv", KVD)))
        cs = tile("cs", [P, 2, 2, BANK])
        rot = tile("rot", [P, 2, 2, BANK])
        parts = [tile("part" + n, [P, 2, NP], BF16) for n in ("h", "m", "l")]
        s_in, s_dve, s_var, s_rt, s_ms, s_rt2, s_r, s_tr, s_ht = map(
            sem, ("in", "dve", "var", "rt", "ms", "rt2", "r", "tr", "ht"))
        s_v, s_vc, s_mm, s_slot, s_rot, s_rc, s_part, s_stack = map(
            sem, ("v", "vc", "mm", "slot", "rot", "rc", "part", "stack"))
        s_cs = slot_sems(ctx, nc, "q_cs")
        s_csfree = sem("csfree")
        NIN = 6
        block = ctx.enter_context(nc.Block())

        @block.sync
        def _(sp):
            for dst, name in ((ln, "ln1"), (wq, "wqT"), (wqp, "wqpT"), (wk, "wkT"), (wkp, "wkpT"), (wv, "wvT")):
                sp.dma_start(dst[:], t[name]).then_inc(s_in, 16)

            def tables(col, c, u, w):
                sp.wait_ge(s_csfree, c + 1)
                sp.dma_start(cs[:, u, :, 0:w], t["rope"][:, :, ds(col, w)]).then_inc(s_cs[u], 16)
            with sp.Fori(0, full // 2) as k:
                for u in range(2):
                    tables(k * (2 * BANK) + u * BANK, 2 * k + u, u, BANK)
            tables(full * BANK, full, full % 2, NP - full * BANK)
            sp.wait_ge(s_part, full + 1)
            hi, mid, lo = parts
            n = 0
            for i, (dst, heads, order) in enumerate((
                    (QA, AH, (hi, hi, mid)), (QB, AH, (hi, mid, lo)),
                    (KA, KV, (hi, mid, hi)), (KB, KV, (lo, mid, hi)))):
                for h in range(heads):
                    for j, part in enumerate(order):
                        sp.dma_start(dst[HD * j:HD * (j + 1), h, :],
                                     part[HD * h:HD * (h + 1), i // 2, :]).then_inc(s_stack, 16)
                        n += 1
            sp.wait_ge(s_stack, 16 * n)

        @block.vector
        def _(v):
            step = chain(v, s_dve)
            v.sem_inc(s_csfree, 2)
            v.sem_inc(s_slot, 1)
            v.memset(KA[3 * HD:3 * HD + 2, :, :], 1.0)
            step(v.memset(V[:, :, :, HD:HD + 1], 1.0))
            row_stats(v, step, X, XL, sq[:], mean[:], var[:])
            v.sem_inc(s_var, 1)
            v.wait_ge(s_rt, 1)
            step(v.reciprocal(mean[:], var[:]))
            step(v.tensor_tensor(XL, XL, mean[:].unsqueeze(2).to_broadcast([P, NB, C]), ALU.mult))
            rms_sum(v, step, XL, sq[:], ms[:])
            v.sem_inc(s_ms, 1)
            v.wait_ge(s_rt2, 1)
            step(v.reciprocal(mean[:], ms[:]))
            v.tensor_tensor(r[:], XL, mean[:].unsqueeze(2).to_broadcast([P, NB, C]), ALU.mult).then_inc(s_r, 1)
            for k in range((NB + 7) // 8):
                nb = min(8, NB - 8 * k)
                v.wait_ge(s_v, k + 1)
                v.tensor_copy(V[:, 8 * k:8 * k + nb, :, 0:HD],
                              ps[:, 4 + k, 0:nb * KVD].rearrange("p (b k d) -> p b k d", b=nb, k=KV)
                              ).then_inc(s_vc, 1)

            def rotate(col, c, u, landed, w):
                v.wait_ge(s_mm, c + 1)
                v.wait_ge(s_cs[u], landed)
                for i, rows in enumerate((P, KVD)):
                    for j in range(2):
                        m = v.tensor_tensor(rot[0:rows, i, j, 0:w], ps[0:rows, 2 * i + j, 0:w],
                                            cs[0:rows, u, j, 0:w], ALU.mult)
                m.then_inc(s_rot, 1)
                v.wait_ge(s_rot, 6 * c + 1)
                v.sem_inc(s_slot, 1)
                v.sem_inc(s_csfree, 1)
                both = [(rot[0:rows, i, 0, 0:w], rot[0:rows, i, 1, 0:w],
                         *(p[0:rows, i, ds(col, w)] for p in parts)) for i, rows in enumerate((P, KVD))]
                for x, y, hi, mid, lo in both:
                    m = v.tensor_tensor(x, x, y, ALU.add)
                m.then_inc(s_rot, 1)
                v.wait_ge(s_rot, 6 * c + 2)
                for x, y, hi, mid, lo in both:
                    m = v.tensor_copy(hi, x)
                m.then_inc(s_rot, 1)
                v.wait_ge(s_rot, 6 * c + 3)
                for x, y, hi, mid, lo in both:
                    m = v.tensor_tensor(x, x, hi, ALU.subtract)
                m.then_inc(s_rot, 1)
                v.wait_ge(s_rot, 6 * c + 4)
                for x, y, hi, mid, lo in both:
                    m = v.tensor_copy(mid, x)
                m.then_inc(s_rot, 1)
                v.wait_ge(s_rot, 6 * c + 5)
                for x, y, hi, mid, lo in both:
                    m = v.tensor_tensor(lo, x, mid, ALU.subtract)
                m.then_inc(s_rot, 1)
                v.wait_ge(s_rot, 6 * c + 6)
                v.sem_inc(s_part, 1)
            with v.Fori(0, full // 2) as k:
                for u in range(2):
                    rotate(k * (2 * BANK) + u * BANK, 2 * k + u, u, 16 * k + 16, BANK)
            rotate(full * BANK, full, full % 2, 16 * (full // 2) + 16, NP - full * BANK)

        @block.scalar
        def _(a):
            a.wait_ge(s_var, 1)
            a.activation(var[:], var[:], ACT.Sqrt, bias=T["eps"][:, 0:1], scale=1.0 / C).then_inc(s_rt, 1)
            a.wait_ge(s_ms, 1)
            a.activation(ms[:], ms[:], ACT.Sqrt, bias=T["eps"][:, 1:2], scale=1.0 / C).then_inc(s_rt2, 1)
            a.wait_ge(s_in, 16 * NIN)
            turned_to(a, s_tr, s_ht, ps, HT, ln[:])

        @block.tensor
        def _(pe):
            pe.wait_ge(s_r, 1)
            transpose_all(pe, ps, r[:], T["eye"][:], s_tr, s_ht)
            pe.wait_ge(s_ht, nk)
            for b in range(NB):
                m = pe.matmul(ps[:, 4 + b // 8, (b % 8) * KVD:(b % 8 + 1) * KVD],
                              HT[:, b * P:(b + 1) * P], wv[:], start=True, stop=True)
                if b % 8 == 7 or b == NB - 1:
                    m.then_inc(s_v, 1)

            def project(col, c, w):
                pe.wait_ge(s_slot, c + 1)
                h = HT[:, ds(col, w)]
                pe.matmul(ps[:, 0, 0:w], wq[:], h, start=True, stop=True)
                pe.matmul(ps[:, 1, 0:w], wqp[:], h, start=True, stop=True)
                pe.matmul(ps[0:KVD, 2, 0:w], wk[:], h, start=True, stop=True)
                pe.matmul(ps[0:KVD, 3, 0:w], wkp[:], h, start=True, stop=True).then_inc(s_mm, 1)
            chunk_loop(pe, project)


def attention_program(nc, t, T):
    QA, QB, KA, KB, V, XL = (T[k] for k in ("QA", "QB", "KA", "KB", "V", "XL"))
    REP = AH // KV
    nc_ = len(QCH)
    blocks = [nb for _, nb in QCH] + [0]
    base = [sum(4 * c + QCH[c][1] for c in range(n)) for n in range(nc_ + 1)]
    first_turn = [4 * (2 * (c > 0)) + AH * blocks[c + 1] for c in range(nc_)]
    jobs = [AH * blocks[0]]
    for c in range(nc_):
        jobs.append(jobs[c] + (first_turn[c] + (c - 1) * AH * blocks[c + 1] if c else 0)
                    + 2 * AH * blocks[c + 1])
    with ExitStack() as ctx:
        sem = lambda name: ctx.enter_context(nc.semaphore("t_" + name))
        tile = lambda name, shape, dt=F32: ctx.enter_context(nc.sbuf_tensor("t_" + name, shape, dt))
        S = ctx.enter_context(nc.psum_tensor("t_S", [P, AH, BANK], F32))
        O = ctx.enter_context(nc.psum_tensor("t_O", [P, 2, BANK], F32))
        M = ctx.enter_context(nc.psum_tensor("t_M", [P, 2, BANK], F32))
        pt = tile("pt", [P, 2, AH, BANK])
        vst = tile("vst", [P, 2, KV, HD + 1])
        os_, wo = tile("os", [P, 2, BANK]), tile("wo", [P, 2, C + 1])
        rd = tile("rd", [P, NB, 2, 2])
        pm = tile("pm", [P, nc_, AH, 4])
        mx, hi, rest, lo = (tile(n, [P, AH, 4], dt) for n, dt in (
            ("mx", F32), ("hi", BF16), ("rest", F32), ("lo", BF16)))
        dg = tile("dg", [P, 2, AH, 4 * P], BF16)
        s_in, s_v, s_s, s_e, s_pv, s_o, s_os, s_pj, s_rd, s_x = map(
            sem, ("in", "v", "s", "e", "pv", "o", "os", "pj", "rd", "x"))
        s_m, s_mr, s_dve, s_dg, s_row, s_rowc = map(sem, ("m", "mr", "dve", "dg", "row", "rowc"))
        block = ctx.enter_context(nc.Block())

        def key_loop(engine, c, body, peel=False):
            n0, j0 = base[c], jobs[c]
            per = AH * blocks[c + 1]
            if c:
                if peel:
                    for i in range(4):
                        body(i, n0 + i, i % 2, 0, "first", 0, i, j0 + i * (2 + blocks[c + 1]))
                    if c > 1:
                        with engine.Fori(1, c) as k:
                            for i in range(4):
                                body(4 * k + i, 4 * k + (n0 + i), i % 2, 0, "later", k, i,
                                     per * k + (j0 + first_turn[c] - per + i * blocks[c + 1]))
                else:
                    with engine.Fori(0, c) as k:
                        for i in range(4):
                            body(4 * k + i, 4 * k + (n0 + i), i % 2, 0, "later", k, i, 0)
            for i in range(blocks[c]):
                body(4 * c + i, n0 + 4 * c + i, i % 2, i * P, "diagonal", c, i,
                     jobs[c + 1] - (blocks[c] - i) * 2 * AH * blocks[c + 1] // blocks[c])

        def step_jobs(c, kc, i, diagonal):
            nb = blocks[c + 1]
            if not diagonal:
                return [(kc, i, s, False) for s in range(nb)]
            heads = range(i * AH // blocks[c], (i + 1) * AH // blocks[c])
            return [(kc + m, h, s, m == 1) for h in heads for m in range(2) for s in range(nb)]

        @block.sync
        def _(sp):
            for g in range(2):
                sp.dma_start(wo[64 * g:64 * g + HD + 1], t["woT"][:, g::2, :]).then_inc(s_in, 16)
            sp.wait_ge(s_in, 32)

        @block.gpsimd
        def _(g):
            for c in range(nc_):
                def stage(kb, n, u, col, turn, kc, i, j):
                    g.wait_ge(s_pv, n + 1)
                    g.tensor_copy(vst[:, u, :, :], V[:, ds(kb, 1), :, :].rearrange(
                        "p b k d -> p (b k) d")).then_inc(s_v, 1)
                key_loop(g, c, stage)

        @block.tensor
        def _(pe):
            def maximum(j, c, kc, h, s, masked):
                q = (QCH[c][0] + s) * P
                w = blocks[c] * P if masked else BANK
                bank = M[:, s % 2, 0:w]
                pe.wait_ge(s_mr, j + 1)
                m = pe.matmul(bank, QA[0:STACK, h, q:q + P], KA[0:STACK, h // REP, ds(kc * BANK, w)],
                              start=True, stop=not masked)
                if masked:
                    m = pe.matmul(bank, T["eyeb"][:], T["cmask"][:, s, 0:w], start=False, stop=True)
                m.then_inc(s_m, 1)

            def project(j, b):
                s = b % 4
                pe.wait_ge(s_mr, j + 2)
                for g in range(2):
                    r = slice(64 * g, 64 * g + HD + 1)
                    for k in range(2):
                        m = pe.matmul(M[:, g, k * (C + 1):(k + 1) * (C + 1)], os_[r, k, s * P:(s + 1) * P],
                                      wo[r, k, :], start=True, stop=True, tile_position=(64 * g, 0))
                    m.then_inc(s_m, 1)

            def rows(c):
                w = blocks[c] * P
                pe.wait_ge(s_dg, c + 1)
                pe.wait_ge(s_e, AH * (base[c] + 1))
                for h in range(AH):
                    for k in range(2):
                        m = pe.matmul(S[STACK:STACK + 2, h, 0:w], T["pick"][:, k, :], dg[:, k, h, 0:w],
                                      start=(k == 0), stop=(k == 1), tile_position=(0, STACK))
                    m.then_inc(s_row, 1)

            pe.sem_inc(s_pv, 2)
            pe.wait_ge(s_in, 32)
            for j in range(jobs[0]):
                maximum(j, 0, 0, j // blocks[0], j % blocks[0], True)
            for c, (q0, nb) in enumerate(QCH):
                w = nb * P
                rows(c)

                def keys(kb, n, u, col, turn, kc, i, j):
                    diagonal = turn == "diagonal"
                    start = i == 0 and turn == ("first" if c else "diagonal")
                    if turn == "first":
                        pe.wait_ge(s_os, 2 * c)
                        project(j, q0 - 4 + i)
                        j = j + 2
                    todo = step_jobs(c, kc, i, diagonal)
                    for op in range(2 * AH):
                        h = op % AH
                        if op < AH:
                            if start:
                                pe.wait_ge(s_rowc, AH * c + h + 1)
                            pe.wait_ge(s_e, AH * n + (h + 1))
                            q = slice(q0 * P + col, q0 * P + w)
                            pe.matmul(S[:, h, col:w], KA[0:STACK + 2, h // REP, ds(kb * P, P)],
                                      QA[0:STACK + 2, h, q], start=True, stop=False)
                            m = pe.matmul(S[:, h, col:w], KB[0:STACK, h // REP, ds(kb * P, P)],
                                          QB[0:STACK, h, q], start=False, stop=not diagonal)
                            if diagonal:
                                m = pe.matmul(S[:, h, col:col + P], T["eyeb"][:], T["cmaskT"][:],
                                              start=False, stop=True)
                            m.then_inc(s_s, 1)
                        else:
                            if h == 0:
                                pe.wait_ge(s_v, n + 1)
                                if c and start:
                                    pe.wait_ge(s_os, 2 * c)
                            pe.wait_ge(s_e, AH * n + (AH + h + 1))
                            g = 64 * (h % 2)
                            m = pe.matmul(O[g:g + HD + 1, h // 2, col:w], vst[:, u, h // REP, :],
                                          pt[:, u, h, col:w], start=start, stop=False,
                                          skip_group_check=True, tile_position=(0, g))
                            if h == AH - 1:
                                m.then_inc(s_pv, 1)
                        for k, (kc_, h_, s_, masked) in enumerate(todo):
                            if k * 2 * AH // len(todo) == op:
                                maximum(j + k, c + 1, kc_, h_, s_, masked)
                key_loop(pe, c, keys, peel=True)
                pe.wait_ge(s_pv, 2 + base[c + 1])
                pe.sem_inc(s_o, 1)
            pe.wait_ge(s_os, 2 * nc_)
            for b in range(q0, NB):
                project(jobs[nc_] + 2 * (b - q0), b)

        @block.scalar
        def _(a):
            a.sem_inc(s_e, AH)
            for c, (q0, nb) in enumerate(QCH):
                w = nb * P
                for h in range(AH):
                    a.wait_ge(s_row, AH * c + h + 1)
                    a.copy(QA[STACK:STACK + 2, h, q0 * P:q0 * P + w],
                           S[STACK:STACK + 2, h, 0:w]).then_inc(s_rowc, 1)

                def exps(kb, n, u, col, turn, kc, i, j):
                    a.wait_ge(s_pv, n + 1)
                    for h in range(AH):
                        a.wait_ge(s_s, AH * n + (h + 1))
                        a.activation(pt[:, u, h, col:w], S[:, h, col:w], ACT.Exp,
                                     scale=float(HD) ** -0.5).then_inc(s_e, 1)
                key_loop(a, c, exps)
                a.wait_ge(s_o, c + 1)
                if c:
                    a.wait_ge(s_x, q0)
                for g in range(2):
                    a.copy(os_[64 * g:64 * g + HD + 1, :, 0:w],
                           O[64 * g:64 * g + HD + 1, :, 0:w]).then_inc(s_os, 1)

        @block.vector
        def _(v):
            step = chain(v, s_dve)

            def reduce(j, kc, h, s, w):
                v.wait_ge(s_m, j + 1)
                v.tensor_reduce(pm[:, ds(kc, 1), h, s], M[:, s % 2, 0:w], AX, ALU.max).then_inc(s_mr, 1)

            def combine(j, b):
                v.wait_ge(s_m, j + 2)
                heads = M[:, :, 0:2 * (C + 1)].rearrange("p g (k c) -> p g k c", k=2)
                v.reciprocal(rd[:, b, :, :], heads[:, :, :, C]).then_inc(s_rd, 1)
                for i in range(AH):
                    v.wait_ge(s_rd, AH * b + i + 1)
                    m = v.scalar_tensor_tensor(XL[:, b, :], heads[:, i % 2, i // 2, 0:C],
                                               rd[:, b, i % 2, i // 2:i // 2 + 1], XL[:, b, :],
                                               ALU.mult, ALU.add)
                    if i < AH - 1:
                        m.then_inc(s_rd, 1)
                m.then_inc(s_mr, 2)
                v.sem_inc(s_x, 1)

            def parts(c):
                nb = blocks[c]
                v.wait_ge(s_mr, 2 + jobs[c])
                if c:
                    step(v.tensor_reduce(mx[:, :, 0:nb], pm[:, 0:c + 1, :, 0:nb].rearrange("p k h s -> p h s k"),
                                         AX, ALU.max))
                else:
                    step(v.tensor_copy(mx[:, :, 0:nb], pm[:, 0, :, 0:nb]))
                step(v.tensor_scalar(hi[:, :, 0:nb], mx[:, :, 0:nb], -1.0, None, ALU.mult))
                step(v.scalar_tensor_tensor(rest[:, :, 0:nb], mx[:, :, 0:nb], -1.0, hi[:, :, 0:nb],
                                            ALU.mult, ALU.subtract))
                step(v.tensor_copy(lo[:, :, 0:nb], rest[:, :, 0:nb]))
                if c:
                    v.wait_ge(s_row, AH * c)
                for k, part in enumerate((hi, lo)):
                    for h in range(AH):
                        m = v.tensor_tensor(dg[:, k, h, 0:nb * P].rearrange("p (s i) -> p s i", s=nb),
                                            T["eyeb"][:].unsqueeze(1).to_broadcast([P, nb, P]),
                                            part[:, h, 0:nb].unsqueeze(2).to_broadcast([P, nb, P]), ALU.mult)
                m.then_inc(s_dg, 1)

            v.sem_inc(s_mr, 2)
            for j in range(jobs[0]):
                reduce(j, 0, j // blocks[0], j % blocks[0], blocks[0] * P)
            parts(0)
            for c, (q0, nb) in enumerate(QCH):
                def maxima(kb, n, u, col, turn, kc, i, j):
                    diagonal = turn == "diagonal"
                    if turn == "first":
                        combine(j, q0 - 4 + i)
                        j = j + 2
                    for k, (kc_, h, s, masked) in enumerate(step_jobs(c, kc, i, diagonal)):
                        reduce(j + k, kc_, h, s, blocks[c + 1] * P if masked else BANK)
                if c + 1 < nc_:
                    key_loop(v, c, maxima, peel=True)
                    parts(c + 1)
                else:
                    for i in range(4):
                        maxima(i, 0, 0, 0, "first", 0, i, jobs[c] + 2 * i)
            for b in range(q0, NB):
                combine(jobs[nc_] + 2 * (b - q0), b)


def experts_program(nc, t, T, out):
    X, XL, HT = T["X"], T["XL"], T["HT"]
    full = NP // BANK
    with ExitStack() as ctx:
        sem = lambda name: ctx.enter_context(nc.semaphore("e_" + name))
        tile = lambda name, shape, dt=F32: ctx.enter_context(nc.sbuf_tensor("e_" + name, shape, dt))
        ps = ctx.enter_context(nc.psum_tensor("e_ps", [P, 8, BANK], F32))
        sq = r = tile("sq", [P, NB, C])
        ms, inv, ln = tile("ms", [P, NB]), tile("inv", [P, NB]), tile("ln", [P, 1])
        rw, tie = tile("rw", [P, NE]), tile("tie", [P, NE, NE])
        w1, w3, w2 = tile("w1", [P, NE, HID]), tile("w3", [P, NE, HID]), tile("w2", [P, NE, len(HTILES), C])
        pr, sel = tile("pr", [P, NB, NE]), tile("sel", [P, NB, NE])
        big = [tile(f"pair{k}", [P, NB, NE, NE]) for k in range(2)]
        red = tile("red", [P, NB])
        wt = tile("wt", [P, NB, NE])
        sg = tile("sg", [P, 2, len(HTILES), BANK])
        s_in, s_w, s_dve, s_ms, s_rt, s_r, s_tr, s_ht, s_lg, s_ex, s_exd = map(
            sem, ("in", "w", "dve", "ms", "rt", "r", "tr", "ht", "lg", "ex", "exd"))
        s_gu, s_sg, s_hh, s_y, s_yc, s_out = map(sem, ("gu", "sg", "hh", "y", "yc", "out"))
        nt = len(HTILES)
        block = ctx.enter_context(nc.Block())

        @block.sync
        def _(sp):
            for dst, name in ((ln, "ln2"), (rw, "routerT"), (tie, "tie")):
                sp.dma_start(dst[:], t[name]).then_inc(s_in, 16)
            sp.dma_start(w1[:], t["w1T"]).then_inc(s_w, 16)
            sp.dma_start(w3[:], t["w3T"]).then_inc(s_w, 16)
            for i, (r0, rows) in enumerate(HTILES):
                sp.dma_start(w2[0:rows, :, i, :], t["w2T"][r0:r0 + rows]).then_inc(s_w, 16)
            sp.wait_ge(s_out, 1)
            sp.dma_start(out.rearrange("(b p) c -> p b c", p=P), X).then_inc(s_out, 16)
            sp.wait_ge(s_out, 17)

        @block.vector
        def _(v):
            step = chain(v, s_dve)
            rms_sum(v, step, XL, sq[:], ms[:])
            v.sem_inc(s_ms, 1)
            v.wait_ge(s_rt, 1)
            step(v.reciprocal(inv[:], ms[:]))
            v.tensor_tensor(r[:], XL, inv[:].unsqueeze(2).to_broadcast([P, NB, C]), ALU.mult).then_inc(s_r, 1)
            v.wait_ge(s_lg, 1)
            lg = ps[:, 7, 0:NB * NE].rearrange("p (b e) -> p b e", e=NE)
            step(v.tensor_reduce(red[:], lg, AX, ALU.max))
            v.tensor_tensor(pr[:], lg, red[:].unsqueeze(2).to_broadcast([P, NB, NE]), ALU.subtract).then_inc(s_ex, 1)
            v.wait_ge(s_exd, 1)
            step(v.tensor_reduce(red[:], pr[:], AX, ALU.add))
            step(v.reciprocal(inv[:], red[:]))
            step(v.tensor_tensor(pr[:], pr[:], inv[:].unsqueeze(2).to_broadcast([P, NB, NE]), ALU.mult))
            v.wait_ge(s_in, 48)
            for b in range(NB):
                mine = pr[:, b, :].unsqueeze(2).to_broadcast([P, NE, NE])
                other = pr[:, b, :].unsqueeze(1).to_broadcast([P, NE, NE])
                v.tensor_tensor(big[0][:, b], other, mine, ALU.is_gt)
                m = v.tensor_tensor(big[1][:, b], other, mine, ALU.is_equal)
            step(m)
            step(v.tensor_tensor(big[1][:].rearrange("p b e j -> p b (e j)"),
                                 big[1][:].rearrange("p b e j -> p b (e j)"),
                                 tie[:].rearrange("p e j -> p (e j)").unsqueeze(1).to_broadcast([P, NB, NE * NE]),
                                 ALU.mult))
            step(v.tensor_tensor(big[0][:].rearrange("p b e j -> p (b e j)"),
                                 big[0][:].rearrange("p b e j -> p (b e j)"),
                                 big[1][:].rearrange("p b e j -> p (b e j)"), ALU.add))
            step(v.tensor_reduce(sel[:].rearrange("p b e -> p (b e)"),
                                 big[0][:].rearrange("p b e j -> p (b e) j"), AX, ALU.add))
            step(v.scalar_tensor_tensor(wt[:].rearrange("p b e -> p (b e)"), sel[:].rearrange("p b e -> p (b e)"),
                                        float(TOPK), pr[:].rearrange("p b e -> p (b e)"), ALU.is_lt, ALU.mult))
            step(v.tensor_reduce(red[:], wt[:], AX, ALU.add))
            step(v.tensor_scalar(red[:], red[:], 1e-9, None, ALU.add))
            step(v.reciprocal(inv[:], red[:]))
            step(v.tensor_tensor(wt[:], wt[:], inv[:].unsqueeze(2).to_broadcast([P, NB, NE]), ALU.mult))

            def combine(b0, c, w, e):
                v.wait_ge(s_y, NE * c + (e + 3))
                for s in range(w // P):
                    x = XL[:, ds(b0 + s, 1), :].rearrange("p b c -> p (b c)")
                    m = v.scalar_tensor_tensor(x, ps[:, 6 + e % 2, s * P:(s + 1) * P],
                                               wt[:, ds(b0 + s, 1), e], x, ALU.mult, ALU.add)
                m.then_inc(s_yc, 1)

            def experts(col, b0, c, w):
                for e in range(NE):
                    for i, (r0, rows) in enumerate(HTILES):
                        v.wait_ge(s_sg, nt * NE * c + (nt * e + i + 1))
                        h = sg[0:rows, e % 2, i, 0:w]
                        v.tensor_tensor(h, h, ps[0:rows, 2 * i + 1, 0:w], ALU.mult).then_inc(s_hh, 1)
                        if i == 1 and e:
                            combine(b0, c, w, e - 1)
                combine(b0, c, w, NE - 1)
            with v.Fori(0, full) as c:
                experts(c * BANK, c * 4, c, BANK)
            experts(full * BANK, full * 4, full, NP - full * BANK)
            v.wait_ge(s_yc, NE * (full + 1) + 2)
            v.tensor_tensor(X, X, XL, ALU.add).then_inc(s_out, 1)

        @block.scalar
        def _(a):
            a.wait_ge(s_ms, 1)
            a.activation(ms[:], ms[:], ACT.Sqrt, bias=T["eps"][:, 1:2], scale=1.0 / C).then_inc(s_rt, 1)
            a.wait_ge(s_in, 48)
            turned_to(a, s_tr, s_ht, ps, HT, ln[:])
            a.wait_ge(s_ex, 1)
            a.activation(pr[:], pr[:], ACT.Exp).then_inc(s_exd, 1)

            def silus(col, c, w):
                for e in range(NE):
                    for i, (r0, rows) in enumerate(HTILES):
                        a.wait_ge(s_gu, nt * NE * c + (nt * e + i + 1))
                        a.wait_ge(s_y, NE * c + (e + 1))
                        a.activation(sg[0:rows, e % 2, i, 0:w], ps[0:rows, 2 * i, 0:w],
                                     ACT.Silu).then_inc(s_sg, 1)
            chunk_loop(a, silus)

        @block.tensor
        def _(pe):
            pe.wait_ge(s_r, 1)
            transpose_all(pe, ps, r[:], T["eye"][:], s_tr, s_ht)
            pe.wait_ge(s_ht, len(QCH))
            pe.wait_ge(s_in, 48)
            for b in range(NB):
                m = pe.matmul(ps[:, 7, b * NE:(b + 1) * NE], HT[:, b * P:(b + 1) * P], rw[:],
                              start=True, stop=True)
            m.then_inc(s_lg, 1)
            pe.wait_ge(s_w, 16 * (2 + nt))
            pe.wait_ge(s_ex, 1)
            pe.sem_inc(s_y, 2)
            pe.sem_inc(s_yc, 2)
            pe.sem_inc(s_hh, nt)

            def down(c, w, e):
                pe.wait_ge(s_hh, nt * NE * c + (nt * (e + 2)))
                pe.wait_ge(s_yc, NE * c + (e + 1))
                for s in range(w // P):
                    for i, (r0, rows) in enumerate(HTILES):
                        m = pe.matmul(ps[:, 6 + e % 2, s * P:(s + 1) * P], sg[0:rows, e % 2, i, s * P:(s + 1) * P],
                                      w2[0:rows, e, i, :], start=(i == 0), stop=(i == nt - 1))
                m.then_inc(s_y, 1)

            def experts(col, c, w):
                h = HT[:, ds(col, w)]
                for e in range(NE):
                    for i, (r0, rows) in enumerate(HTILES):
                        pe.wait_ge(s_hh, nt * NE * c + (nt * e + i + 1))
                        pe.matmul(ps[0:rows, 2 * i, 0:w], w1[:, e, r0:r0 + rows], h, start=True, stop=True)
                        pe.matmul(ps[0:rows, 2 * i + 1, 0:w], w3[:, e, r0:r0 + rows], h, start=True,
                                  stop=True).then_inc(s_gu, 1)
                        if i == 0 and e:
                            down(c, w, e - 1)
                down(c, w, NE - 1)
            chunk_loop(pe, experts)


def build(nc, t, out):
    with ExitStack() as ctx:
        sb = lambda name, shape, dt=F32: ctx.enter_context(nc.sbuf_tensor(name, shape, dt))
        T = {}
        T["eye"], T["noteye"], T["ones"] = sb("eye", [P, P]), sb("noteye", [P, P]), sb("ones", [P, P])
        T["eps"] = sb("eps", [P, 2])
        T["dcol"] = sb("dcol", [P, NB])
        XR = sb("XR", [P, NB, C])
        with ExitStack() as graph:
            gb = lambda name, shape, dt=F32: graph.enter_context(nc.sbuf_tensor(name, shape, dt))
            T["selE"], T["selB"] = gb("selE", [EP, EROWS]), gb("selB", [EP, EROWS, P])
            T["Ecol"], T["EcolN"] = gb("Ecol", [P, NB * EROWS]), gb("EcolN", [P, NB * EROWS])
            T["nmax"], T["den"] = gb("nmax", [P, 2, NB * HEADS]), gb("den", [P, 2, NB * HEADS])
            T["rden"] = gb("rden", [P, NB * HEADS])
            T["signed"] = gb("signed", [P, 1], I32)
            H = gb("H", [P, NB, C])
            NS = gb("NS", [P, NP])
            T["H"], T["NS"] = H[:], NS[:]
            with ExitStack() as c1:
                E = c1.enter_context(nc.sbuf_tensor("E", [P, NP], F32))
                T["E"] = E[:]
                with ExitStack() as c2:
                    T["U3"] = c2.enter_context(nc.sbuf_tensor("U3", [P, NB, 2, EW], BF16))
                    with ExitStack() as c3:
                        T["X"] = XR[:]
                        T["SQ"] = c3.enter_context(nc.sbuf_tensor("SQ", [P, NB, C], F32))[:]
                        T["HTR"] = c3.enter_context(nc.sbuf_tensor("HT1", [P, NP], F32))[:]
                        norm_program(nc, t, T)
                    spmm_program(nc, t, T)
                shared = {}
                T["sem"] = lambda name: shared.get(name) or shared.setdefault(
                    name, graph.enter_context(nc.semaphore(name)))
                signed = nc.values_load(T["signed"][0:1, 0:1], min_val=0, max_val=1)
                with nc.If(signed > 0):
                    graph_attention(nc, t, T, E, XR, (1, -1))
                with nc.Else():
                    graph_attention(nc, t, T, E, XR, (1,))
                T["ES"] = E[:].rearrange("p (b c) -> p b c", c=C)
                with ExitStack() as c6:
                    big = lambda name: c6.enter_context(nc.sbuf_tensor(name, [P, NP], F32))[:]
                    T["X"] = XR[:]
                    T["HTR"], T["EST"], T["OT"] = big("HT2"), big("EST"), big("OT")
                    gru_program(nc, t, T)

        T["eyeb"], T["cmask"] = sb("eyeb", [P, P], BF16), sb("cmask", [P, 4, BANK], BF16)
        T["cmaskT"], T["pick"] = sb("cmaskT", [P, P], BF16), sb("pick", [P, 2, 2], BF16)
        T["XL"] = sb("XL", [P, NB, C])[:]
        T["HT"] = sb("HT", [P, NP])[:]
        load_masks(nc, t, T)
        with ExitStack() as attn:
            ab = lambda name, shape, dt=F32: attn.enter_context(nc.sbuf_tensor(name, shape, dt))[:]
            T["QA"], T["QB"] = ab("QA", [P, AH, NP], BF16), ab("QB", [P, AH, NP], BF16)
            T["KA"], T["KB"] = ab("KA", [P, KV, NP], BF16), ab("KB", [P, KV, NP], BF16)
            T["V"] = ab("V", [P, NB, KV, HD + 1])
            qkv_program(nc, t, T)
            attention_program(nc, t, T)
        experts_program(nc, t, T, out)


def load_masks(nc, t, T):
    with nc.semaphore("c_in") as s, nc.sbuf_tensor("c_f", [P, 4 * BANK + 2 * P + 4], F32) as f, \
            nc.semaphore("c_w") as s_w, nc.Block() as block:
        parts = [(T["cmask"][:].rearrange("p s k -> p (s k)"), 0, 4 * BANK), (T["cmaskT"][:], 4 * BANK, P),
                 (T["eyeb"][:], 4 * BANK + P, P),
                 (T["pick"][:].rearrange("p k m -> p (k m)"), 4 * BANK + 2 * P, 4)]

        @block.sync
        def _(sp):
            sp.dma_start(f[:], t["masks"]).then_inc(s, 16)

        @block.vector
        def _(v):
            v.wait_ge(s, 16)
            for dst, a, w in parts:
                v.tensor_copy(dst, f[:, a:a + w]).then_inc(s_w, 1)
            v.wait_ge(s_w, len(parts))


def kernel(x, adj, **w):
    import numpy as np
    import concourse.bacc as bacc
    from concourse import mybir as mb
    from concourse.bass_utils import run_bass_kernel_spmd as run

    pad = NP - N
    f32 = np.float32
    a = {}
    a["x"] = np.pad(np.asarray(x), ((0, pad), (0, 0)))
    A = np.pad(np.asarray(adj), ((0, pad), (0, pad)))
    a["adj"] = A
    a["adjT"] = np.ascontiguousarray(A.T)
    a["diag"] = np.ascontiguousarray(np.diagonal(A).reshape(NB, P).T)
    a["gat_W"] = np.asarray(w["L0_gnn_gat_W"])
    a["gat_WT"] = np.ascontiguousarray(a["gat_W"].transpose(0, 2, 1))
    a["gat_a"] = np.ascontiguousarray(np.asarray(w["L0_gnn_gat_a"]).reshape(HEADS, 2, C).transpose(2, 0, 1))
    for kind in ("edge", "node"):
        a[kind + "_WihT"] = np.ascontiguousarray(np.asarray(w[f"L0_gnn_{kind}_Wih"]).T)
        a[kind + "_WhhT"] = np.ascontiguousarray(np.asarray(w[f"L0_gnn_{kind}_Whh"]).T)
        a[kind + "_bih"] = np.ascontiguousarray(np.asarray(w[f"L0_gnn_{kind}_bih"]).reshape(3, C).T)
        a[kind + "_bhh"] = np.ascontiguousarray(np.asarray(w[f"L0_gnn_{kind}_bhh"]).reshape(3, C).T)
    a["eye"] = np.eye(P, dtype=f32)
    a["noteye"] = 1 - np.eye(P, dtype=f32)
    selE = np.zeros((2, EW, EROWS), f32)
    for part in range(PARTS):
        selE[:, 1 + part * EROWS + np.arange(EROWS), np.arange(EROWS)] = 1
    a["selE"] = selE.reshape(EP, EROWS)
    a["selB"] = np.ascontiguousarray(np.broadcast_to(a["selE"][:, :, None], (EP, EROWS, P)))
    inv = 1.0 / 10000.0 ** (np.arange(0, HD, 2, dtype=f32) / HD)
    ang = np.outer(np.arange(NP, dtype=f32), inv)
    ang = np.concatenate([ang, ang], axis=1).T
    sign = np.where(np.arange(HD) < HD // 2, -1, 1).astype(f32)[:, None]
    rope = np.stack([np.cos(ang), np.sin(ang) * sign], axis=1).astype(f32)
    a["rope"] = np.ascontiguousarray(np.tile(rope, (AH, 1, 1)))
    q, k = np.arange(P), np.arange(BANK)
    low = f32(-1e30)
    cm = np.stack([np.where(k[None] > q[:, None] + s * P, low, 0) for s in range(4)], axis=1)
    pick = np.broadcast_to(np.eye(2, dtype=f32), (P, 2, 2))
    a["masks"] = np.ascontiguousarray(np.concatenate(
        [cm.reshape(P, -1), np.where(q[:, None] > q[None], low, 0), np.eye(P), pick.reshape(P, 4)],
        axis=1).astype(f32))
    a["tie"] = np.ascontiguousarray(np.broadcast_to(np.tril(np.ones((NE, NE), f32), -1), (P, NE, NE)))

    half = np.concatenate([np.arange(HD // 2, HD), np.arange(HD // 2)])
    wq, wk, wv, wo = (np.asarray(w["L0_ffn_" + n]) for n in ("wq", "wk", "wv", "wo"))
    a["wqT"] = np.ascontiguousarray(wq.T)
    a["wkT"] = np.ascontiguousarray(wk.T)
    a["wqpT"] = np.ascontiguousarray(wq.reshape(AH, HD, C)[:, half].reshape(AH * HD, C).T)
    a["wkpT"] = np.ascontiguousarray(wk.reshape(KV, HD, C)[:, half].reshape(KV * HD, C).T)
    a["wvT"] = np.ascontiguousarray(wv.T)
    a["woT"] = np.pad(wo.reshape(C, AH, HD).transpose(2, 1, 0), ((0, 1), (0, 0), (0, 1)))
    a["woT"][HD, :, C] = 1.0
    a["ln1"] = np.asarray(w["L0_ffn_ln1_w"]).reshape(C, 1)
    a["ln2"] = np.asarray(w["L0_ffn_ln2_w"]).reshape(C, 1)
    a["routerT"] = np.ascontiguousarray(np.asarray(w["L0_ffn_router_w"]).T)
    a["w1T"] = np.ascontiguousarray(np.asarray(w["L0_ffn_w1"]).transpose(2, 0, 1))
    a["w3T"] = np.ascontiguousarray(np.asarray(w["L0_ffn_w3"]).transpose(2, 0, 1))
    a["w2T"] = np.ascontiguousarray(np.asarray(w["L0_ffn_w2"]).transpose(2, 0, 1))

    nc = bacc.Bacc("TRN2", target_bir_lowering=False, num_devices=1)
    arrays, t = {}, {}
    for name, v in a.items():
        arrays["in_" + name] = v
        t[name] = nc.dram_tensor("in_" + name, v.shape, mb.dt.from_np(v.dtype), kind="ExternalInput").ap()
    out = nc.dram_tensor("out_0", (NP, C), mb.dt.float32, kind="ExternalOutput").ap()
    build(nc, t, out)
    r = run(nc, [arrays], core_ids=[0])
    return r.results[0]["out_0"][:N]
```

```python
from contextlib import ExitStack

import concourse.bass as bass
from concourse import mybir

P = 128
N = 3327
NB = (N + P - 1) // P
NP = NB * P
C = 128
HEADS = 3
ALPHA = 0.2
NEG_INF = -9000000000000000.0
LOWEST = -3.0e38
PARTS = 3
EROWS = 2 * HEADS
EW = 32
EP = 2 * EW
RING = 4
LN_EPS = 1e-5
BANK = 512

SWEEPS = [(0, 14), (14, 12)]
CHUNKS = [(0, 8), (8, 6), (14, 6), (20, 6)]

AH, KV, HD = 4, 2, 32
NE, TOPK, HID = 8, 2, 341
RMS_EPS = 1e-6
STACK = PARTS * HD
GROUPS = [0, 2 * BANK, 4 * BANK, NP]
STACK_DMAS = PARTS * 2 * (AH + KV)
HTILES = [(0, 128), (128, 128), (256, 85)]
QCH = [(4 * c, min(4, NB - 4 * c)) for c in range((NB + 3) // 4)]

ALU = mybir.AluOpType
ACT = mybir.ActivationFunctionType
F32 = mybir.dt.float32
BF16 = mybir.dt.bfloat16
I32 = mybir.dt.int32
AX = mybir.AxisListType.X
ds = bass.ds


def pieces(cols, size=BANK):
    return [(a, min(size, cols - a)) for a in range(0, cols, size)]


def chain(engine, sem):
    done = [0]

    def step(instruction):
        done[0] += 1
        instruction.then_inc(sem, 1)
        engine.wait_ge(sem, done[0])
    return step


def centre(v, x, xc, mean, s_xc):
    for b0, nb in QCH:
        v.tensor_tensor(xc[:, b0:b0 + nb, :], x[:, b0:b0 + nb, :],
                        mean[:, b0:b0 + nb].unsqueeze(2).to_broadcast([P, nb, C]),
                        ALU.subtract).then_inc(s_xc, 1)


def spread_of(a, xc, sq, var, std, eps, s_xc, s_var, s_rt):
    for k, (b0, nb) in enumerate(QCH):
        a.wait_ge(s_xc, k + 1)
        for b in range(b0, b0 + nb):
            m = a.activation(sq[:, b, :], xc[:, b, :], ACT.Square, accum_out=var[:, b:b + 1])
    m.then_inc(s_var, 1)
    a.wait_ge(s_var, 1)
    a.activation(std, var, ACT.Sqrt, bias=eps, scale=1.0 / C).then_inc(s_rt, 1)


def scale_rows(v, dst, src, factor, s_done):
    for b0, nb in QCH:
        v.tensor_tensor(dst[:, b0:b0 + nb, :], src[:, b0:b0 + nb, :],
                        factor[:, b0:b0 + nb].unsqueeze(2).to_broadcast([P, nb, C]),
                        ALU.mult).then_inc(s_done, 1)


def norm_program(nc, t, T):
    X, H, SQ, HTR = T["X"], T["H"], T["SQ"], T["HTR"]
    with ExitStack() as ctx:
        sem = lambda name: ctx.enter_context(nc.semaphore(name))
        ps = ctx.enter_context(nc.psum_tensor("n_ps", [P, 8, BANK], F32))
        s_x, s_c, s_dve, s_xc, s_var, s_rt, s_h = map(
            sem, ("n_x", "n_c", "n_dve", "n_xc", "n_var", "n_rt", "n_h"))
        s_tr, s_ht, s_u, s_uc, s_U = map(sem, ("n_tr", "n_ht", "n_u", "n_uc", "n_U"))
        mean = ctx.enter_context(nc.sbuf_tensor("n_mean", [P, NB], F32))
        var = ctx.enter_context(nc.sbuf_tensor("n_var_t", [P, NB], F32))
        std = ctx.enter_context(nc.sbuf_tensor("n_std", [P, NB], F32))
        wt = ctx.enter_context(nc.sbuf_tensor("n_wt", [P, HEADS, C], F32))
        av = ctx.enter_context(nc.sbuf_tensor("n_av", [P, HEADS, 2], F32))
        uc = ctx.enter_context(nc.sbuf_tensor("n_ucol", [P, 2, HEADS], F32))
        U = ctx.enter_context(nc.sbuf_tensor("n_Uf", [P, NB, EROWS], F32))
        Ub = ctx.enter_context(nc.sbuf_tensor("n_Ub", [P, NB, EROWS], BF16))
        block = ctx.enter_context(nc.Block())

        @block.sync
        def _(sp):
            sp.dma_start(X, t["x"].rearrange("(b p) c -> p b c", p=P)).then_inc(s_x, 16)
            sp.dma_start(T["eye"][:], t["eye"]).then_inc(s_c, 16)
            sp.dma_start(T["noteye"][:], t["noteye"]).then_inc(s_c, 16)
            sp.dma_start(T["dcol"][:], t["diag"]).then_inc(s_c, 16)
            sp.dma_start(wt[:], t["gat_WT"].rearrange("h c d -> c h d")).then_inc(s_c, 16)
            sp.dma_start(av[:], t["gat_a"]).then_inc(s_c, 16)
            sp.dma_start(T["selE"][:], t["selE"]).then_inc(s_c, 16)
            sp.dma_start(T["selB"][:], t["selB"]).then_inc(s_c, 16)
            sp.wait_ge(s_x, 16)
            sp.wait_ge(s_c, 16 * 7)

        @block.vector
        def _(v):
            step = chain(v, s_dve)
            v.memset(T["ones"][:], 1.0)
            v.memset(T["eps"][:, 0:1], LN_EPS)
            v.memset(T["eps"][:, 1:2], RMS_EPS)
            step(v.memset(T["U3"][:], 0.0))
            step(v.memset(T["U3"][:, :, 1, 0:1], 1.0))
            v.wait_ge(s_x, 16)
            step(v.tensor_reduce(mean[:], X, AX, ALU.add))
            step(v.tensor_scalar(mean[:], mean[:], 1.0 / C, None, ALU.mult))
            centre(v, X, H, mean[:], s_xc)
            v.wait_ge(s_rt, 1)
            step(v.reciprocal(mean[:], std[:]))
            scale_rows(v, H, H, mean[:], s_h)
            v.wait_ge(s_u, 1)
            v.tensor_copy(uc[:], ps[:, 7, 0:EROWS].rearrange("p (h k) -> p k h", k=2)).then_inc(s_uc, 1)
            v.wait_ge(s_U, 1)
            step(v.tensor_copy(U[:], ps[:, 7, 8:8 + NB * EROWS].rearrange("p (b e) -> p b e", e=EROWS)))
            for k in range(PARTS):
                step(v.tensor_copy(Ub[:], U[:]))
                e0 = 1 + k * EROWS
                v.tensor_copy(T["U3"][:, :, 0, e0:e0 + EROWS], Ub[:])
                v.tensor_copy(T["U3"][:, :, 1, e0:e0 + HEADS], Ub[:, :, HEADS:EROWS])
                step(v.tensor_copy(T["U3"][:, :, 1, e0 + HEADS:e0 + EROWS], Ub[:, :, 0:HEADS]))
                step(v.tensor_tensor(U[:], U[:], Ub[:], ALU.subtract))

        @block.scalar
        def _(a):
            spread_of(a, H, SQ, var[:], std[:], T["eps"][:, 0:1], s_xc, s_var, s_rt)
            for k, (b0, nb) in enumerate(QCH):
                a.wait_ge(s_tr, k + 1)
                a.copy(HTR[:, b0 * P:(b0 + nb) * P], ps[:, k % 6, 0:nb * P]).then_inc(s_ht, 1)

        @block.tensor
        def _(pe):
            pe.wait_ge(s_c, 16 * 7)
            for h in range(HEADS):
                m = pe.matmul(ps[:, 7, 2 * h:2 * h + 2], wt[:, h, :], av[:, h, :], start=True, stop=True)
            m.then_inc(s_u, 1)
            for k, (b0, nb) in enumerate(QCH):
                pe.wait_ge(s_h, k + 1)
                if k >= 6:
                    pe.wait_ge(s_ht, k - 5)
                for b in range(nb):
                    m = pe.transpose(ps[:, k % 6, b * P:(b + 1) * P], H[:, b0 + b, :], T["eye"][:])
                m.then_inc(s_tr, 1)
            pe.wait_ge(s_ht, len(QCH))
            pe.wait_ge(s_uc, 1)
            for b in range(NB):
                o = 8 + b * EROWS
                m = pe.matmul(ps[:, 7, o:o + EROWS], HTR[:, b * P:(b + 1) * P],
                              uc[:].rearrange("p k h -> p (k h)"), start=True, stop=True)
            m.then_inc(s_U, 1)


def slot_sems(ctx, nc, name, slots=2):
    return [ctx.enter_context(nc.semaphore(f"{name}{u}")) for u in range(slots)]


class Tile:

    def __init__(self, row, n, slot, landed, diagonal, fixed, start, sign, lead):
        self.row, self.n, self.slot, self.landed = row, n, slot, landed
        self.diagonal, self.fixed, self.start, self.sign, self.lead = diagonal, fixed, start, sign, lead


def tile_loop(engine, first, blocks, base, body, signs=(1,), peel=False):
    n = base
    for si, sign in enumerate(signs):
        for start, count, diagonal in ((first, blocks, True), (first + blocks, NB - first - blocks, False),
                                       (0, first, False)):
            def tile(k, at):
                m = n + at
                return Tile(RING * k + (start + at), RING * k + m, m % RING,
                            16 * k + 16 * (m // RING + 1), diagonal,
                            RING * k + (first * len(signs) + si * blocks + at + 1), m == base, sign,
                            m - base if m - base < lead else None)
            lead = min(RING, count) if peel and n == base else 0
            for at in range(lead):
                body(tile(0, at))
            turns = (count - lead) // RING
            if turns:
                with engine.Fori(0, turns) as k:
                    for u in range(RING):
                        body(tile(k, lead + u))
            for at in range(lead + turns * RING, count):
                body(tile(0, at))
            n += count


def spmm_program(nc, t, T):
    H, NS, E = T["H"], T["NS"], T["E"]
    W = max(b for _, b in SWEEPS) * P
    with ExitStack() as ctx:
        sem = lambda name: ctx.enter_context(nc.semaphore("a_" + name))
        tile = lambda name, shape, dt=F32: ctx.enter_context(nc.sbuf_tensor("a_" + name, shape, dt))
        at, mp, mm = tile("at", [P, RING, W]), tile("mp", [P, RING, W], BF16), tile("mm", [P, RING, W], BF16)
        hst, ust = tile("h", [P, RING, C]), tile("u", [P, RING, 2, EW], BF16)
        neg = tile("neg", [P, 1])
        ps = ctx.enter_context(nc.psum_tensor("a_ps", [P, 4 * BANK], F32))
        pe_e = ctx.enter_context(nc.psum_tensor("a_pe", [P, 4 * BANK], F32))
        s_tile = slot_sems(ctx, nc, "a_tile", RING)
        s_free, s_fix, s_mask, s_w, s_sum, s_out, s_neg = map(
            sem, ("free", "fix", "mask", "w", "sum", "out", "neg"))
        block = ctx.enter_context(nc.Block())

        @block.sync
        def _(sp):
            for i, (first, nb) in enumerate(SWEEPS):
                def load(b):
                    sp.wait_ge(s_free, b.n + 1)
                    sp.dma_start(at[:, b.slot, 0:nb * P], t["adjT"][ds(b.row * P, P), first * P:(first + nb) * P]
                                 ).then_inc(s_tile[b.slot], 16)
                tile_loop(sp, first, nb, i * NB, load)
            sp.wait_ge(s_neg, 2)

        @block.gpsimd
        def _(g):
            for i, (first, nb) in enumerate(SWEEPS):
                def stage(b):
                    g.wait_ge(s_free, b.n + 1)
                    g.tensor_copy(hst[:, b.slot, :], H[:, ds(b.row, 1), :].rearrange("p b c -> p (b c)"))
                    g.tensor_copy(ust[:, b.slot, :, :], T["U3"][:, ds(b.row, 1), :, :].rearrange(
                        "p b k e -> p (b k) e")).then_inc(s_w, 1)
                tile_loop(g, first, nb, i * NB, stage)
            g.wait_ge(s_neg, 2)

        @block.vector
        def _(v):
            for i, (first, nb) in enumerate(SWEEPS):
                def masks(b):
                    v.wait_ge(s_tile[b.slot], b.landed)
                    tile = at[:, b.slot, 0:nb * P]
                    if b.diagonal:
                        d = at[:, b.slot, ds((b.row - first) * P, P)]
                        v.tensor_tensor(d, d, T["noteye"][:], ALU.mult).then_inc(s_fix, 1)
                        v.wait_ge(s_fix, b.fixed)
                    v.wait_ge(s_free, b.n + 1)
                    v.tensor_scalar(mp[:, b.slot, 0:nb * P], tile, 0.0, None, ALU.is_gt)
                    v.tensor_scalar(mm[:, b.slot, 0:nb * P], tile, 0.0, None, ALU.is_lt).then_inc(s_mask, 1)
                tile_loop(v, first, nb, i * NB, masks)
                v.wait_ge(s_sum, i + 1)
                for k, (a, w) in enumerate(pieces(nb * P)):
                    m = v.tensor_copy(E[0:EP, first * P + a:first * P + a + w],
                                      pe_e[EP * (k % 2):EP * (k % 2) + EP, a:a + w])
                m.then_inc(s_out, 1)
            v.wait_ge(s_out, 2 * len(SWEEPS))
            v.tensor_reduce(neg[0:1, :], E[EW:EW + 1, :], AX, ALU.max).then_inc(s_neg, 1)
            v.wait_ge(s_neg, 1)
            v.tensor_scalar(T["signed"][0:1, :], neg[0:1, :], 0.0, None, ALU.is_gt).then_inc(s_neg, 1)
            v.wait_ge(s_neg, 2)

        @block.scalar
        def _(a):
            for i, (first, nb) in enumerate(SWEEPS):
                a.wait_ge(s_sum, i + 1)
                a.copy(NS[:, first * P:(first + nb) * P], ps[:, 0:nb * P]).then_inc(s_out, 1)
            a.wait_ge(s_neg, 2)

        @block.tensor
        def _(pe):
            pe.sem_inc(s_free, RING)
            for i, (first, nb) in enumerate(SWEEPS):
                if i:
                    pe.wait_ge(s_out, 2 * i)
                def products(b):
                    u = b.slot
                    pe.wait_ge(s_w, b.n + 1)
                    pe.wait_ge(s_mask, b.n + 1)
                    cols = list(enumerate(pieces(nb * P)))
                    for pair in (cols[0:2], cols[2:4]):
                        for _, (a, w) in pair:
                            pe.matmul(ps[:, a:a + w], hst[:, u, :], at[:, u, a:a + w],
                                      start=b.start, stop=False, skip_group_check=True)
                        for i, (a, w) in pair:
                            for k, mask in enumerate((mp, mm)):
                                r = EP * (i % 2) + EW * k
                                m = pe.matmul(pe_e[r:r + EW, a:a + w], ust[:, u, k, :], mask[:, u, a:a + w],
                                              start=b.start, stop=False, skip_group_check=True,
                                              tile_position=(0, r))
                    m.then_inc(s_free, 1)
                tile_loop(pe, first, nb, i * NB, products, peel=True)
                pe.wait_ge(s_free, RING + (i + 1) * NB)
                pe.sem_inc(s_sum, 1)
            pe.wait_ge(s_neg, 2)


def scores_program(nc, t, T, si, signs):
    E, EB, S, AR, NM, Ecol = (T[k] for k in ("E", "EB", "S", "AR", "NM", "Ecol"))
    sign, spread = signs[si], len(signs) == 1
    nmax, den = T["nmax"][:, si], T["den"][:, si]
    cols, pre = pieces(NP), T["path"] + f"r{si}_"
    COL = 7
    with ExitStack() as ctx:
        sem = lambda name: T["sem"](f"r{si}_{name}")
        mx = ctx.enter_context(nc.sbuf_tensor(pre + "mx", [P, 2, HEADS], F32))
        nm = ctx.enter_context(nc.sbuf_tensor(pre + "nm", [P, 2, HEADS], F32))
        dg = ctx.enter_context(nc.sbuf_tensor(pre + "dg", [P, 2, HEADS, P], F32)) if spread else None
        ps = ctx.enter_context(nc.psum_tensor(pre + "ps", [P, 8, BANK], F32))
        s_a = [sem(f"a{u}") for u in range(2)]
        s_eb, s_cp, s_ebc, s_dve, s_afree, s_fix, s_bias, s_go, s_max, s_nm, s_exp = map(
            sem, ("eb", "cp", "ebc", "dve", "afree", "fix", "bias", "go", "max", "nm", "exp"))
        s_col, s_diag, s_bc, s_bank = map(T["sem"], ("r_col", "r_diag", "r_bc", "r_bank"))
        block = ctx.enter_context(nc.Block())

        @block.sync
        def _(sp):
            with sp.Fori(0, NB // 2) as k:
                for u in range(2):
                    n = 2 * k + u
                    sp.wait_ge(s_afree, n + 1)
                    sp.dma_start(AR[u], t["adj"][ds(n * P, P), :]).then_inc(s_a[u], 16)

        @block.vector
        def _(v):
            v.sem_inc(s_afree, 2)
            step = chain(v, s_dve)

            def relu(h):
                for k, (c0, w) in enumerate(cols):
                    i = h * len(cols) + k
                    v.wait_ge(s_cp, i + 1)
                    v.scalar_tensor_tensor(EB[h][:, c0:c0 + w], EB[h][:, c0:c0 + w], ALPHA, ps[:, i % 8, 0:w],
                                           ALU.mult, ALU.max).then_inc(s_ebc, 1)
                v.wait_ge(s_ebc, (h + 1) * len(cols))

            def biases(n, k, u):
                v.wait_ge(s_a[u], 16 * k + 16)
                d = AR[u][:, ds(n * P, P)]
                v.tensor_tensor(d, d, T["noteye"][:], ALU.mult).then_inc(s_fix, 1)
                v.wait_ge(s_fix, n + 1)
                v.tensor_scalar(AR[u], AR[u], 0.0, NEG_INF, ALU.is_le if sign > 0 else ALU.is_ge,
                                ALU.mult).then_inc(s_bias, 1)
                v.wait_ge(s_bias, n + 1)

            def maximum(n, u, h):
                v.wait_ge(s_exp, 3 * n + (h + 1))
                v.sem_inc(s_go, 1)
                v.tensor_tensor_reduce(S[h], AR[u], EB[h], 1.0, LOWEST, ALU.add, ALU.max,
                                       mx[:, u, h:h + 1]).then_inc(s_max, 1)

            def finish(n, u):
                v.wait_ge(s_max, 3 * n + 3)
                v.sem_inc(s_afree, 1)
                if not spread:
                    v.wait_ge(s_nm, 3 * n + 3)
                    v.tensor_copy(nmax[:, ds(3 * n, HEADS)], nm[:, u, :])

            relu(0)
            biases(0, 0, 0)
            for h in range(HEADS):
                maximum(0, 0, h)
                if h < HEADS - 1:
                    relu(h + 1)
            finish(0, 0)

            def rows(n, k, u):
                biases(n, k, u)
                for h in range(HEADS):
                    maximum(n, u, h)
                finish(n, u)
            rows(1, 0, 1)
            with v.Fori(1, NB // 2) as k:
                for u in range(2):
                    rows(2 * k + u, k, u)
            if si == 0:
                v.wait_ge(s_col, 1)
                step(v.tensor_copy(Ecol[:], ps[:, COL, 0:NB * EROWS]))
                step(v.scalar_tensor_tensor(Ecol[:], Ecol[:], ALPHA, Ecol[:], ALU.mult, ALU.max))
                step(v.tensor_scalar(T["EcolN"][:], Ecol[:], -1.0, None, ALU.mult))
            if spread:
                v.wait_ge(s_exp, 3 * NB + 3)
                step(v.tensor_scalar(den, den, float(HEADS), None, ALU.mult))
                step(v.reciprocal(T["rden"][:], den))

        @block.scalar
        def _(a):
            a.sem_inc(s_exp, 3)
            if spread:
                a.sem_inc(s_bank, 2)

            def copies(h):
                for k, (c0, w) in enumerate(cols):
                    i = h * len(cols) + k
                    a.wait_ge(s_eb, i + 1)
                    a.copy(EB[h][:, c0:c0 + w], ps[:, i % 8, 0:w]).then_inc(s_cp, 1)

            def exps(n, u, h):
                m = nm[:, u, h:h + 1]
                if spread and h == 0:
                    a.wait_ge(s_bc, n + 1)
                a.wait_ge(s_max, 3 * n + (h + 1))
                a.mul(m, mx[:, u, h:h + 1], -1.0).then_inc(s_nm, 1)
                a.wait_ge(s_nm, 3 * n + (h + 1))
                if spread:
                    a.mul(dg[:, u, h, :], T["eye"][:], m).then_inc(s_diag, 1)
                a.activation(S[h], S[h], ACT.Exp, bias=m,
                             accum_out=den[:, ds(3 * n + h, 1)]).then_inc(s_exp, 1)

            def spread_out(n, u):
                if spread:
                    a.wait_ge(s_bc, n + 3)
                    a.copy(NM[:, :, ds(n * P, P)], ps[:, u, 0:HEADS * P].rearrange(
                        "p (h i) -> p h i", h=HEADS)).then_inc(s_bank, 1)

            copies(0)
            copies(1)
            exps(0, 0, 0)
            copies(2)
            exps(0, 0, 1)
            exps(0, 0, 2)
            spread_out(0, 0)
            for h in range(HEADS):
                exps(1, 1, h)
            spread_out(1, 1)
            with a.Fori(1, NB // 2) as k:
                for u in range(2):
                    n = 2 * k + u
                    for h in range(HEADS):
                        exps(n, u, h)
                    spread_out(n, u)

        @block.tensor
        def _(pe):
            if spread:
                pe.sem_inc(s_bc, 2)
            for h in range(HEADS):
                for k, (c0, w) in enumerate(cols):
                    i = h * len(cols) + k
                    if i >= 8:
                        pe.wait_ge(s_ebc, i - 7)
                    pe.matmul(ps[:, i % 8, 0:w], T["selB"][:, si * HEADS + h, :], E[0:EP, c0:c0 + w],
                              start=True, stop=True).then_inc(s_eb, 1)
            pe.wait_ge(s_ebc, HEADS * len(cols))
            if si == 0:
                for b in range(NB):
                    m = pe.matmul(ps[:, COL, b * EROWS:(b + 1) * EROWS], E[0:EP, b * P:(b + 1) * P],
                                  T["selE"][:], start=True, stop=True)
                m.then_inc(s_col, 1)
            if spread:
                with pe.Fori(0, NB // 2) as k:
                    for u in range(2):
                        n = 2 * k + u
                        pe.wait_ge(s_diag, 3 * n + 3)
                        pe.wait_ge(s_bank, n + 1)
                        pe.matmul(ps[:, u, 0:HEADS * P], T["ones"][:], dg[:, u].rearrange("p h i -> p (h i)"),
                                  start=True, stop=True).then_inc(s_bc, 1)


def spread_program(nc, T):
    NM, nmax, den, rden = T["NM"], T["nmax"], T["den"], T["rden"]
    with ExitStack() as ctx:
        sem = lambda name: T["sem"]("s_" + name)
        dg = ctx.enter_context(nc.sbuf_tensor(T["path"] + "s_dg", [P, 2, HEADS, P], F32))
        corr = ctx.enter_context(nc.sbuf_tensor(T["path"] + "s_corr", [P, 2, NB * HEADS], F32))
        ps = ctx.enter_context(nc.psum_tensor(T["path"] + "s_ps", [P, 2, BANK], F32))
        s_dve, s_corr, s_exp, s_diag, s_bc, s_bank = map(sem, ("dve", "corr", "exp", "diag", "bc", "bank"))
        block = ctx.enter_context(nc.Block())

        @block.vector
        def _(v):
            step = chain(v, s_dve)
            step(v.tensor_tensor(rden[:], nmax[:, 0], nmax[:, 1], ALU.min))
            for i in range(2):
                m = v.tensor_tensor(corr[:, i], rden[:], nmax[:, i], ALU.subtract)
            m.then_inc(s_corr, 1)
            v.wait_ge(s_exp, 2)
            for i in range(2):
                m = v.tensor_tensor(den[:, i], den[:, i], corr[:, i], ALU.mult)
            step(m)
            step(v.tensor_copy(nmax[:, 0], rden[:]))
            step(v.tensor_tensor(den[:, 0], den[:, 0], den[:, 1], ALU.add))
            step(v.tensor_scalar(den[:, 0], den[:, 0], float(HEADS), None, ALU.mult))
            step(v.reciprocal(rden[:], den[:, 0]))
            with v.Fori(0, NB // 2) as k:
                for u in range(2):
                    n = 2 * k + u
                    v.wait_ge(s_bc, n + 1)
                    v.tensor_tensor(dg[:, u], T["eye"][:].unsqueeze(1).to_broadcast([P, HEADS, P]),
                                    nmax[:, 0, ds(3 * n, HEADS)].unsqueeze(2).to_broadcast([P, HEADS, P]),
                                    ALU.mult).then_inc(s_diag, 1)

        @block.scalar
        def _(a):
            a.sem_inc(s_bank, 2)
            a.wait_ge(s_corr, 1)
            for i in range(2):
                a.activation(corr[:, i], corr[:, i], ACT.Exp).then_inc(s_exp, 1)
            with a.Fori(0, NB // 2) as k:
                for u in range(2):
                    n = 2 * k + u
                    a.wait_ge(s_bc, n + 3)
                    a.copy(NM[:, :, ds(n * P, P)],
                           ps[:, u, 0:HEADS * P].rearrange("p (h i) -> p h i", h=HEADS)).then_inc(s_bank, 1)

        @block.tensor
        def _(pe):
            pe.sem_inc(s_bc, 2)
            with pe.Fori(0, NB // 2) as k:
                for u in range(2):
                    n = 2 * k + u
                    pe.wait_ge(s_diag, n + 1)
                    pe.wait_ge(s_bank, n + 1)
                    pe.matmul(ps[:, u, 0:HEADS * P], T["ones"][:], dg[:, u].rearrange("p h i -> p (h i)"),
                              start=True, stop=True).then_inc(s_bc, 1)


def gat_program(nc, t, T, signs):
    H, NM, ES = T["H"], T["NM"], T["ES"]
    W = max(b for _, b in CHUNKS) * P
    ON_ACT = HEADS - 1
    ND = HEADS - 1
    total = NB * len(signs)
    with ExitStack() as ctx:
        sem = lambda name: T["sem"]("g_" + name)
        tile = lambda name, shape: ctx.enter_context(nc.sbuf_tensor(T["path"] + "g_" + name, shape, F32))
        at, y, gs = tile("at", [P, RING, W]), tile("y", [P, RING, HEADS, W]), tile("gs", [P, HEADS, W])
        hst, wg = tile("h", [P, RING, C]), tile("w", [P, HEADS, C])
        G = ctx.enter_context(nc.psum_tensor(T["path"] + "g_G", [P, HEADS, 2 * BANK], F32))
        pj = ctx.enter_context(nc.psum_tensor(T["path"] + "g_pj", [P, 2, BANK], F32))

        LEAD = 2

        def delayed(i, b, lag=0):
            if i == 0 or b.lead is None or not 0 <= b.lead - lag < LEAD:
                return range(0)
            first, nb = CHUNKS[i - 1]
            return range(first + (b.lead - lag) * nb // LEAD, first + (b.lead - lag + 1) * nb // LEAD)

        s_tile = [sem(f"tile{u}") for u in range(RING)]
        s_wg, s_z, s_relu, s_fix, s_sign, s_h, s_y, s_w, s_free = map(
            sem, ("wg", "z", "relu", "fix", "sign", "h", "y", "w", "free"))
        s_gs, s_pj, s_es, s_dve = map(sem, ("gs", "pj", "es", "dve"))
        block = ctx.enter_context(nc.Block())

        @block.sync
        def _(sp):
            sp.dma_start(wg[:], t["gat_W"].rearrange("h d c -> d h c")).then_inc(s_wg, 16)
            for i, (first, nb) in enumerate(CHUNKS):
                def load(b):
                    sp.wait_ge(s_free, b.n + 1)
                    sp.dma_start(at[:, b.slot, 0:nb * P], t["adjT"][ds(b.row * P, P), first * P:(first + nb) * P]
                                 ).then_inc(s_tile[b.slot], 16)
                tile_loop(sp, first, nb, i * total, load, signs)
            sp.wait_ge(s_wg, 16)

        @block.gpsimd
        def _(g):
            for i, (first, nb) in enumerate(CHUNKS):
                def stage(b):
                    g.wait_ge(s_free, b.n + 1)
                    g.tensor_copy(hst[:, b.slot, :],
                                  H[:, ds(b.row, 1), :].rearrange("p b c -> p (b c)")).then_inc(s_h, 1)
                tile_loop(g, first, nb, i * total, stage, signs)

        @block.scalar
        def _(a):
            def sums(i):
                first, nb = CHUNKS[i]
                a.wait_ge(s_free, RING + (i + 1) * total)
                if i:
                    a.wait_ge(s_es, first)
                for h in range(HEADS):
                    a.copy(gs[:, h, 0:nb * P], G[:, h, 0:nb * P]).then_inc(s_gs, 1)

            for i, (first, nb) in enumerate(CHUNKS):
                def exps(b):
                    e0 = 0 if b.sign > 0 else HEADS
                    a.wait_ge(s_free, b.n + 1)
                    last = y[:, b.slot, ON_ACT, 0:nb * P]
                    a.activation(last, NM[:, ON_ACT, first * P:(first + nb) * P], ACT.Relu,
                                 bias=T["EcolN"][:, ds(b.row * EROWS + (e0 + ON_ACT), 1)],
                                 scale=-1.0).then_inc(s_relu, 1)
                    for h in range(ND):
                        yh = y[:, b.slot, h, 0:nb * P]
                        a.wait_ge(s_z, ND * b.n + (h + 1))
                        a.activation(yh, yh, ACT.Exp).then_inc(s_y, 1)
                    a.wait_ge(s_relu, b.n + 1)
                    a.activation(last, last, ACT.Exp, scale=-1.0).then_inc(s_y, 1)
                    if i and b.start:
                        sums(i - 1)
                tile_loop(a, first, nb, i * total, exps, signs, peel=True)
            sums(i)

        @block.vector
        def _(v):
            step = chain(v, s_dve)

            def combine(q):
                v.wait_ge(s_pj, q + 1)
                for h in range(HEADS):
                    x, r = pj[:, q % 2, h * C:(h + 1) * C], T["rden"][:, HEADS * q + h:HEADS * q + h + 1]
                    if h == 0:
                        step(v.tensor_scalar(ES[:, q, :], x, r, None, ALU.mult))
                    elif h < HEADS - 1:
                        step(v.scalar_tensor_tensor(ES[:, q, :], x, r, ES[:, q, :], ALU.mult, ALU.add))
                    else:
                        v.scalar_tensor_tensor(ES[:, q, :], x, r, ES[:, q, :], ALU.mult,
                                               ALU.add).then_inc(s_es, 1)

            def weigh(n, slot, nb):
                for h in range(HEADS):
                    v.wait_ge(s_y, HEADS * n + (h + 1))
                    yh = y[:, slot, h, 0:nb * P]
                    v.tensor_tensor(yh, yh, at[:, slot, 0:nb * P], ALU.mult).then_inc(s_w, 1)

            for i, (first, nb) in enumerate(CHUNKS):
                def differences(b):
                    u = b.slot
                    e0 = 0 if b.sign > 0 else HEADS
                    v.wait_ge(s_free, b.n + 1)
                    for h in range(ND):
                        v.tensor_scalar(y[:, u, h, 0:nb * P], NM[:, h, first * P:(first + nb) * P],
                                        T["Ecol"][:, ds(b.row * EROWS + (e0 + h), 1)], 0.0, ALU.add,
                                        ALU.min).then_inc(s_z, 1)
                    v.wait_ge(s_tile[u], b.landed)
                    if b.diagonal:
                        d = at[:, u, ds((b.row - first) * P, P)]
                        v.tensor_tensor(d, d, T["noteye"][:], ALU.mult).then_inc(s_fix, 1)
                        v.wait_ge(s_fix, b.fixed)
                    if len(signs) == 2:
                        v.tensor_scalar(at[:, u, 0:nb * P], at[:, u, 0:nb * P], 0.0, None,
                                        ALU.max if b.sign > 0 else ALU.min).then_inc(s_sign, 1)
                        v.wait_ge(s_sign, b.n + 1)
                    if i or not b.start:
                        weigh(b.n - 1, (u - 1) % RING, CHUNKS[i - 1][1] if b.start else nb)
                    for q in delayed(i, b, lag=2):
                        combine(q)
                tile_loop(v, first, nb, i * total, differences, signs, peel=True)
            weigh(len(CHUNKS) * total - 1, (len(CHUNKS) * total - 1) % RING, nb)
            for q in range(first, NB):
                combine(q)

        @block.tensor
        def _(pe):
            pe.sem_inc(s_free, RING)
            pe.wait_ge(s_wg, 16)

            def project(i, q):
                a = (q - CHUNKS[i][0]) * P
                pe.wait_ge(s_gs, HEADS * (i + 1))
                if q >= 2:
                    pe.wait_ge(s_es, q - 1)
                for h in range(HEADS):
                    m = pe.matmul(pj[:, q % 2, h * C:(h + 1) * C], gs[:, h, a:a + P], wg[:, h, :],
                                  start=True, stop=True)
                m.then_inc(s_pj, 1)

            for i, (first, nb) in enumerate(CHUNKS):
                def products(b):
                    pe.wait_ge(s_h, b.n + 1)
                    for h in range(HEADS):
                        pe.wait_ge(s_w, HEADS * b.n + (h + 1))
                        if b.start and i:
                            pe.wait_ge(s_gs, HEADS * (i - 1) + h + 1)
                        for a, w in pieces(nb * P):
                            m = pe.matmul(G[:, h, a:a + w], hst[:, b.slot, :], y[:, b.slot, h, a:a + w],
                                          start=b.start, stop=False, skip_group_check=True)
                    m.then_inc(s_free, 1)
                    for q in delayed(i, b):
                        project(i - 1, q)
                tile_loop(pe, first, nb, i * total, products, signs, peel=True)
            for q in range(first, NB):
                project(i, q)


def graph_attention(nc, t, T, E, XR, signs):
    T["path"] = "signed_" if len(signs) == 2 else "positive_"
    for engine in (nc.sync, nc.gpsimd, nc.scalar, nc.vector, nc.tensor):
        engine.nop()
    with nc.sbuf_tensor(T["path"] + "NM", [P, HEADS, NP], F32) as NM:
        T["NM"] = NM[:]
        with ExitStack() as ctx:
            big = lambda name: ctx.enter_context(nc.sbuf_tensor(T["path"] + name, [P, NP], F32))[:]
            T["EB"] = [big(f"EB{h}") for h in range(HEADS)]
            T["S"] = [NM[:, h, :] if len(signs) == 2 else big(f"S{h}") for h in range(HEADS)]
            T["AR"] = [XR[:].rearrange("p b c -> p (b c)"), big("AR1")]
            for si in range(len(signs)):
                scores_program(nc, t, T, si, signs)
        if len(signs) == 2:
            spread_program(nc, T)
        T["ES"] = E[:].rearrange("p (b c) -> p b c", c=C)
        gat_program(nc, t, T, signs)


def transpose_all(pe, ps, src, eye, s_done, s_free, base=0, s_src=None):
    for k, (b0, nb) in enumerate(QCH):
        if base + k >= 2:
            pe.wait_ge(s_free, base + k - 1)
        if s_src is not None:
            pe.wait_ge(s_src, k + 1)
        for b in range(nb):
            m = pe.transpose(ps[:, (base + k) % 2, b * P:(b + 1) * P], src[:, b0 + b, :], eye)
        m.then_inc(s_done, 1)


def gru_program(nc, t, T):
    H, NS, ES, X, HTR, EST, OT = (T[k] for k in ("H", "NS", "ES", "X", "HTR", "EST", "OT"))
    nk = len(QCH)
    with ExitStack() as ctx:
        sem = lambda name: ctx.enter_context(nc.semaphore(name))
        tile = lambda name, shape: ctx.enter_context(nc.sbuf_tensor("u_" + name, shape, F32))
        ps = ctx.enter_context(nc.psum_tensor("u_ps", [P, 8, BANK], F32))
        wi, wh = tile("wi", [P, 2, 3 * C]), tile("wh", [P, 2, 3 * C])
        bi, bh, brz = tile("bi", [P, 2, 3]), tile("bh", [P, 2, 3]), tile("brz", [P, 2, 3])
        rz, pre, cand, mix = (tile(n, [P, 2, 2 * BANK]) for n in ("rz", "pre", "cand", "mix"))
        s_in, s_tr, s_trc, s_brz, s_slot, s_mm, s_rz, s_pre, s_cand, s_mix, s_o, s_to, s_x2, s_gfree = map(
            sem, ("u_in", "u_tr", "u_trc", "u_brz", "u_slot", "u_mm", "u_rz", "u_pre", "u_cand",
                  "u_mix", "u_o", "u_to", "u_x2", "u_gfree"))
        NIN = 9
        block = ctx.enter_context(nc.Block())

        @block.sync
        def _(sp):
            sp.dma_start(X, t["x"].rearrange("(b p) c -> p b c", p=P)).then_inc(s_in, 16)
            for g, kind in enumerate(("edge", "node")):
                sp.dma_start(wi[:, g, :], t[kind + "_WihT"]).then_inc(s_in, 16)
                sp.dma_start(wh[:, g, :], t[kind + "_WhhT"]).then_inc(s_in, 16)
                sp.dma_start(bi[:, g, :], t[kind + "_bih"]).then_inc(s_in, 16)
                sp.dma_start(bh[:, g, :], t[kind + "_bhh"]).then_inc(s_in, 16)
            sp.wait_ge(s_in, 16 * NIN)

        @block.tensor
        def _(pe):
            transpose_all(pe, ps, H, T["eye"][:], s_tr, s_trc)
            transpose_all(pe, ps, ES, T["eye"][:], s_tr, s_trc, nk)
            pe.wait_ge(s_in, 16 * NIN)
            pe.wait_ge(s_trc, 2 * nk)

            def gates(c0, c, w):
                for g, src in enumerate((NS, EST)):
                    pe.wait_ge(s_slot, 2 * c + g + 1)
                    b = 4 * g
                    s, h = src[:, ds(c0, w)], HTR[:, ds(c0, w)]
                    for k in range(2):
                        pe.matmul(ps[:, b + k, 0:w], wi[:, g, k * C:(k + 1) * C], s, start=True, stop=False)
                        pe.matmul(ps[:, b + k, 0:w], wh[:, g, k * C:(k + 1) * C], h, start=False, stop=True)
                    pe.matmul(ps[:, b + 2, 0:w], wi[:, g, 2 * C:3 * C], s, start=True, stop=True)
                    pe.matmul(ps[:, b + 3, 0:w], wh[:, g, 2 * C:3 * C], h, start=True,
                              stop=True).then_inc(s_mm, 1)
            chunk_loop(pe, gates)
            pe.wait_ge(s_o, 2 * nk)
            for k, (b0, nb) in enumerate(QCH):
                if k >= 2:
                    pe.wait_ge(s_x2, QCH[k - 2][0] + QCH[k - 2][1])
                for b in range(nb):
                    m = pe.transpose(ps[:, k % 2, b * P:(b + 1) * P], OT[:, (b0 + b) * P:(b0 + b + 1) * P],
                                     T["eye"][:])
                m.then_inc(s_to, 1)

        @block.scalar
        def _(a):
            for i, dst in enumerate((HTR, EST)):
                for k, (b0, nb) in enumerate(QCH):
                    a.wait_ge(s_tr, i * nk + k + 1)
                    a.copy(dst[:, b0 * P:(b0 + nb) * P], ps[:, (i * nk + k) % 2, 0:nb * P]).then_inc(s_trc, 1)
            a.wait_ge(s_brz, 1)

            def act(c0, c, w):
                for g in range(2):
                    b = 4 * g
                    a.wait_ge(s_mm, 2 * c + g + 1)
                    a.wait_ge(s_gfree, 2 * c + g + 1)
                    for k in range(2):
                        i = a.activation(rz[:, g, k * BANK:k * BANK + w], ps[:, b + k, 0:w], ACT.Sigmoid,
                                         bias=brz[:, g, k:k + 1])
                    i.then_inc(s_rz, 1)
                    a.wait_ge(s_pre, 4 * c + 2 * g + 2)
                    a.activation(cand[:, g, 0:w], pre[:, g, 0:w], ACT.Tanh,
                                 bias=bi[:, g, 2:3]).then_inc(s_cand, 1)
            chunk_loop(a, act)

        @block.vector
        def _(v):
            v.sem_inc(s_slot, 2)
            v.sem_inc(s_gfree, 2)
            v.wait_ge(s_in, 16 * NIN)
            v.tensor_tensor(brz[:], bi[:], bh[:], ALU.add).then_inc(s_brz, 1)

            def cells(c0, c, w):
                for g in range(2):
                    b = 4 * g
                    m = 2 * c + g
                    v.wait_ge(s_rz, m + 1)
                    v.scalar_tensor_tensor(pre[:, g, 0:w], ps[:, b + 3, 0:w], bh[:, g, 2:3],
                                           rz[:, g, 0:w], ALU.add, ALU.mult).then_inc(s_pre, 1)
                    v.wait_ge(s_pre, 2 * m + 1)
                    v.tensor_tensor(pre[:, g, 0:w], pre[:, g, 0:w], ps[:, b + 2, 0:w],
                                    ALU.add).then_inc(s_pre, 1)
                    v.wait_ge(s_cand, m + 1)
                    v.sem_inc(s_slot, 1)
                    v.tensor_tensor(mix[:, g, 0:w], HTR[:, ds(c0, w)], cand[:, g, 0:w],
                                    ALU.subtract).then_inc(s_mix, 1)
                    v.wait_ge(s_mix, 3 * m + 1)
                    v.tensor_tensor(mix[:, g, 0:w], mix[:, g, 0:w], rz[:, g, BANK:BANK + w],
                                    ALU.mult).then_inc(s_mix, 1)
                    v.wait_ge(s_mix, 3 * m + 2)
                    if g == 0:
                        v.tensor_tensor(OT[:, ds(c0, w)], mix[:, g, 0:w], cand[:, g, 0:w],
                                        ALU.add).then_inc(s_mix, 1)
                        v.wait_ge(s_mix, 3 * m + 3)
                        v.sem_inc(s_o, 1)
                        v.sem_inc(s_gfree, 1)
                    else:
                        v.tensor_tensor(mix[:, g, 0:w], mix[:, g, 0:w], cand[:, g, 0:w],
                                        ALU.add).then_inc(s_mix, 1)
                        v.wait_ge(s_mix, 3 * m + 3)
                        v.sem_inc(s_gfree, 1)
                        v.tensor_tensor(OT[:, ds(c0, w)], OT[:, ds(c0, w)], mix[:, g, 0:w],
                                        ALU.add).then_inc(s_o, 1)
            chunk_loop(v, cells)
            for b in range(NB):
                v.wait_ge(s_to, b // 4 + 1)
                v.scalar_tensor_tensor(X[:, b, :], ps[:, (b // 4) % 2, (b % 4) * P:(b % 4 + 1) * P],
                                       T["dcol"][:, b:b + 1], X[:, b, :], ALU.mult, ALU.add,
                                       accum_out=T["sums"][:, b:b + 1]).then_inc(s_x2, 1)


def turned_to(engine, s_tr, s_out, ps, dst, scale):
    for k, (b0, nb) in enumerate(QCH):
        engine.wait_ge(s_tr, k + 1)
        engine.activation(dst[:, b0 * P:(b0 + nb) * P], ps[:, k % 2, 0:nb * P], ACT.Copy,
                          scale=scale).then_inc(s_out, 1)


def chunk_loop(engine, body):
    full = NP // BANK
    with engine.Fori(0, full) as c:
        body(c * BANK, c, BANK)
    body(full * BANK, full, NP - full * BANK)


def stack_parts(sp, T, g):
    hi, mid, lo = T["parts"]
    cols = slice(GROUPS[g], GROUPS[g + 1])
    for i, (dst, heads, order) in enumerate((
            (T["QA"], AH, (hi, hi, mid)), (T["KA"], KV, (hi, mid, hi)),
            (T["QB"], AH, (hi, mid, lo)), (T["KB"], KV, (lo, mid, hi)))):
        for h in range(heads):
            for j, part in enumerate(order):
                sp.dma_start(dst[HD * j:HD * (j + 1), h, cols],
                             part[HD * h:HD * (h + 1), i % 2, cols]).then_inc(T["s_stack"][g], 16)


def qkv_program(nc, t, T):
    X, XL, HT, KA, V = (T[k] for k in ("X", "XL", "HT", "KA", "V"))
    nk, full = len(QCH), NP // BANK
    KVD = KV * HD
    with ExitStack() as ctx:
        sem = lambda name: ctx.enter_context(nc.semaphore("q_" + name))
        tile = lambda name, shape, dt=F32: ctx.enter_context(nc.sbuf_tensor("q_" + name, shape, dt))
        ps = ctx.enter_context(nc.psum_tensor("q_ps", [P, 8, BANK], F32))
        sq = r = tile("sq", [P, NB, C])
        mean, var, ms = tile("mean", [P, NB]), tile("var_", [P, NB]), tile("ms", [P, NB])
        ln = tile("ln", [P, 1])
        wq, wqp, wk, wkp, wv = (tile(n, [P, m]) for n, m in (
            ("wq", C), ("wqp", C), ("wk", KVD), ("wkp", KVD), ("wv", KVD)))
        cs = tile("cs", [P, 2, 2, BANK])
        rot = tile("rot", [P, 2, 2, BANK])
        s_in, s_dve, s_xc, s_var, s_rt, s_ms, s_rt2, s_r, s_tr, s_ht = map(
            sem, ("in", "dve", "xc", "var", "rt", "ms", "rt2", "r", "tr", "ht"))
        s_v, s_vc, s_mm, s_slot, s_rot, s_part = map(sem, ("v", "vc", "mm", "slot", "rot", "part"))
        s_cs = slot_sems(ctx, nc, "q_cs")
        s_csfree, s_ones = sem("csfree"), sem("ones")
        NIN = 6
        block = ctx.enter_context(nc.Block())

        def tables(engine, col, c, u, w):
            if c is not u:
                engine.wait_ge(s_csfree, c - 1)
            engine.dma_start(cs[:, u, :, 0:w], t["rope"][:, :, ds(col, w)]).then_inc(s_cs[u], 16)

        @block.sync
        def _(sp):
            for dst, name in ((ln, "ln1"), (wq, "wqT"), (wqp, "wqpT"), (wk, "wkT"), (wkp, "wkpT"), (wv, "wvT")):
                sp.dma_start(dst[:], t[name]).then_inc(s_in, 16)

            for u in range(2):
                tables(sp, u * BANK, u, u, BANK)
            sp.wait_ge(s_part, GROUPS[1] // BANK)
            stack_parts(sp, T, 0)
            sp.wait_ge(s_part, full + 1)
            sp.wait_ge(T["s_stack"][0], 16 * STACK_DMAS)

        @block.gpsimd
        def _(g):
            g.memset(KA[STACK:STACK + 2, :, :], 1.0).then_inc(s_ones, 1)
            g.wait_ge(s_ones, 1)
            g.memset(V[:, :, :, HD:HD + 1], 1.0).then_inc(s_ones, 1)
            g.wait_ge(s_ones, 2)

        @block.vector
        def _(v):
            step = chain(v, s_dve)
            v.sem_inc(s_slot, 1)
            step(v.tensor_scalar(mean[:], T["sums"], 1.0 / C, None, ALU.mult))
            centre(v, X, XL, mean[:], s_xc)
            v.wait_ge(s_rt, 1)
            step(v.reciprocal(mean[:], ms[:]))
            step(v.tensor_tensor(ms[:], var[:], mean[:], ALU.mult))
            step(v.tensor_tensor(ms[:], ms[:], mean[:], ALU.mult))
            v.sem_inc(s_ms, 1)
            v.wait_ge(s_rt2, 1)
            step(v.reciprocal(var[:], ms[:]))
            step(v.tensor_tensor(var[:], var[:], mean[:], ALU.mult))
            scale_rows(v, r, XL, var[:], s_r)
            v.wait_ge(s_r, nk)
            v.tensor_tensor(XL, XL, mean[:].unsqueeze(2).to_broadcast([P, NB, C]), ALU.mult)
            for k in range((NB + 7) // 8):
                nb = min(8, NB - 8 * k)
                v.wait_ge(s_v, k + 1)
                v.tensor_copy(V[:, 8 * k:8 * k + nb, :, 0:HD],
                              ps[:, 4 + k, 0:nb * KVD].rearrange("p (b k d) -> p b k d", b=nb, k=KV)
                              ).then_inc(s_vc, 1)

            def rotate(col, c, u, landed, w):
                v.wait_ge(s_mm, c + 1)
                v.wait_ge(s_cs[u], landed)
                for i, rows in enumerate((P, KVD)):
                    for j in range(2):
                        m = v.tensor_tensor(rot[0:rows, i, j, 0:w], ps[0:rows, 2 * i + j, 0:w],
                                            cs[0:rows, u, j, 0:w], ALU.mult)
                m.then_inc(s_rot, 1)
                v.wait_ge(s_rot, 6 * c + 1)
                v.sem_inc(s_slot, 1)
                v.sem_inc(s_csfree, 1)
                both = [(rot[0:rows, i, 0, 0:w], rot[0:rows, i, 1, 0:w],
                         *(p[0:rows, i, ds(col, w)] for p in T["parts"])) for i, rows in enumerate((P, KVD))]
                for x, y, hi, mid, lo in both:
                    m = v.tensor_tensor(x, x, y, ALU.add)
                m.then_inc(s_rot, 1)
                v.wait_ge(s_rot, 6 * c + 2)
                for x, y, hi, mid, lo in both:
                    m = v.tensor_copy(hi, x)
                m.then_inc(s_rot, 1)
                v.wait_ge(s_rot, 6 * c + 3)
                for x, y, hi, mid, lo in both:
                    m = v.tensor_tensor(x, x, hi, ALU.subtract)
                m.then_inc(s_rot, 1)
                v.wait_ge(s_rot, 6 * c + 4)
                for x, y, hi, mid, lo in both:
                    m = v.tensor_copy(mid, x)
                m.then_inc(s_rot, 1)
                v.wait_ge(s_rot, 6 * c + 5)
                for x, y, hi, mid, lo in both:
                    m = v.tensor_tensor(lo, x, mid, ALU.subtract)
                m.then_inc(s_rot, 1)
                v.wait_ge(s_rot, 6 * c + 6)
                v.sem_inc(s_part, 1)
            with v.Fori(0, full // 2) as k:
                for u in range(2):
                    rotate(k * (2 * BANK) + u * BANK, 2 * k + u, u, 16 * k + 16, BANK)
            rotate(full * BANK, full, full % 2, 16 * (full // 2) + 16, NP - full * BANK)

        @block.scalar
        def _(a):
            spread_of(a, XL, sq, var[:], ms[:], T["eps"][:, 0:1], s_xc, s_var, s_rt)
            a.wait_ge(s_ms, 1)
            a.activation(ms[:], ms[:], ACT.Sqrt, bias=T["eps"][:, 1:2], scale=1.0 / C).then_inc(s_rt2, 1)
            a.wait_ge(s_in, 16 * NIN)
            turned_to(a, s_tr, s_ht, ps, HT, ln[:])
            with a.Fori(1, full // 2) as k:
                for u in range(2):
                    tables(a, k * (2 * BANK) + u * BANK, 2 * k + u, u, BANK)
            tables(a, full * BANK, full, full % 2, NP - full * BANK)

        @block.tensor
        def _(pe):
            transpose_all(pe, ps, r[:], T["eye"][:], s_tr, s_ht, s_src=s_r)
            pe.wait_ge(s_ht, nk)
            for b in range(NB):
                m = pe.matmul(ps[:, 4 + b // 8, (b % 8) * KVD:(b % 8 + 1) * KVD],
                              HT[:, b * P:(b + 1) * P], wv[:], start=True, stop=True)
                if b % 8 == 7 or b == NB - 1:
                    m.then_inc(s_v, 1)

            def project(col, c, w):
                pe.wait_ge(s_slot, c + 1)
                h = HT[:, ds(col, w)]
                pe.matmul(ps[:, 0, 0:w], wq[:], h, start=True, stop=True)
                pe.matmul(ps[:, 1, 0:w], wqp[:], h, start=True, stop=True)
                pe.matmul(ps[0:KVD, 2, 0:w], wk[:], h, start=True, stop=True)
                pe.matmul(ps[0:KVD, 3, 0:w], wkp[:], h, start=True, stop=True).then_inc(s_mm, 1)
            chunk_loop(pe, project)


def attention_program(nc, t, T):
    QA, QB, KA, KB, V, XL = (T[k] for k in ("QA", "QB", "KA", "KB", "V", "XL"))
    REP = AH // KV
    nc_ = len(QCH)
    blocks = [nb for _, nb in QCH] + [0]

    def maxima_of(c, turn, i):
        nb = blocks[c + 1]
        full = [(h, s, False) for h in range(AH) for s in range(nb)]
        if turn == "middle" or (turn == "diagonal" and c):
            return full[i * len(full) // blocks[c]:(i + 1) * len(full) // blocks[c]] if turn == "diagonal" \
                else full[i * nb:(i + 1) * nb]
        todo = full + [(h, s, True) for h in range(AH) for s in range(nb)]
        return todo[i * len(todo) // 3:(i + 1) * len(todo) // 3]

    def projected(c, turn, i):
        per = 4 // blocks[c]
        return range(per * i, per * (i + 1)) if c and turn == "diagonal" else range(0)

    def job_count(c, turn, i):
        return len(maxima_of(c, turn, i)) + 2 * len(projected(c, turn, i))

    base, jobs = [0], [AH * blocks[0] + AH]
    for c in range(nc_):
        base.append(base[c] + blocks[c] + 4 * c)
        jobs.append(jobs[c] + sum(job_count(c, "diagonal", i) for i in range(blocks[c]))
                    + (c - 1) * AH * blocks[c + 1] * (c > 0)
                    + (c > 0) * 2 * AH * blocks[c + 1] + AH * (blocks[c + 1] > 0))

    with ExitStack() as ctx:
        sem = lambda name: ctx.enter_context(nc.semaphore("t_" + name))
        tile = lambda name, shape, dt=F32: ctx.enter_context(nc.sbuf_tensor("t_" + name, shape, dt))
        S = ctx.enter_context(nc.psum_tensor("t_S", [P, AH, BANK], F32))
        O = ctx.enter_context(nc.psum_tensor("t_O", [P, 2, BANK], F32))
        M = ctx.enter_context(nc.psum_tensor("t_M", [P, 2, BANK], F32))
        pt = tile("pt", [P, 2, AH, BANK])
        vst = tile("vst", [P, 2, KV, HD + 1])
        os_, wo = tile("os", [P, 2, BANK]), tile("wo", [P, 2, C + 1])
        rd, sq = tile("rd", [P, NB, 2, 2]), tile("sq", [P, C])
        pm = tile("pm", [P, nc_, AH, 4])
        mx, rest = tile("mx", [P, AH, 4]), tile("rest", [P, AH, 4])
        nm = tile("nm", [P, 2, AH, 4, 2], BF16)
        s_in, s_v, s_s, s_e, s_pv, s_os, s_rd, s_x, s_m, s_mr, s_dve, s_nm = map(
            sem, ("in", "v", "s", "e", "pv", "os", "rd", "x", "m", "mr", "dve", "nm"))
        block = ctx.enter_context(nc.Block())

        def steps(engine, c, body):
            n, j = base[c], jobs[c]
            for i in range(blocks[c]):
                body("diagonal", i, 4 * c + i, n + i, c, j)
                j += job_count(c, "diagonal", i)
            n += blocks[c]
            per = AH * blocks[c + 1]
            if c > 1:
                with engine.Fori(0, c - 1) as k:
                    for i in range(4):
                        body("middle", i, 4 * k + i, 4 * k + (n + i), k, per * k + (j + i * blocks[c + 1]))
            if c:
                j += (c - 1) * per
                for i in range(4):
                    body("last", i, 4 * (c - 1) + i, n + 4 * (c - 1) + i, c - 1, j)
                    j += job_count(c, "last", i)

        def closing(c, turn, i):
            return i == 3 and turn == "last" if c else i == blocks[0] - 1

        @block.sync
        def _(sp):
            for g in range(2):
                sp.dma_start(wo[64 * g:64 * g + HD + 1], t["woT"][:, g::2, :]).then_inc(s_in, 16)
            for g in (1, 2):
                stack_parts(sp, T, g)
            sp.wait_ge(s_in, 32)

        @block.gpsimd
        def _(g):
            for c in range(nc_):
                def stage(turn, i, kb, n, kc, j):
                    g.wait_ge(s_pv, n + 1)
                    g.tensor_copy(vst[:, i % 2, :, :], V[:, ds(kb, 1), :, :].rearrange(
                        "p b k d -> p (b k) d")).then_inc(s_v, 1)
                steps(g, c, stage)

        @block.tensor
        def _(pe):
            def maximum(j, c, kc, h, s, masked):
                q = (QCH[c][0] + s) * P
                w = (s + 1) * P if masked else BANK
                pe.wait_ge(s_mr, j + 1)
                m = pe.matmul(M[:, s % 2, 0:w], QA[0:STACK, h, q:q + P], KA[0:STACK, h // REP, ds(kc * BANK, w)],
                              start=True, stop=not masked)
                if masked:
                    m = pe.matmul(M[:, s % 2, s * P:w], T["eyeb"][:], T["cmask"][:], start=False, stop=True)
                m.then_inc(s_m, 1)

            def project(j, s):
                pe.wait_ge(s_mr, j + 2)
                for g in range(2):
                    r = slice(64 * g, 64 * g + HD + 1)
                    for k in range(2):
                        m = pe.matmul(M[:, g, k * (C + 1):(k + 1) * (C + 1)], os_[r, k, s * P:(s + 1) * P],
                                      wo[r, k, :], start=True, stop=True, tile_position=(64 * g, 0))
                    m.then_inc(s_m, 1)

            def row(j, c, h):
                pe.wait_ge(s_nm, c + 1)
                pe.wait_ge(s_mr, j + 1)
                for s in range(blocks[c]):
                    m = pe.matmul(M[STACK:STACK + 2, h % 2, s * P:(s + 1) * P], nm[:, c % 2, h, s, :],
                                  T["eyeb"][:], start=True, stop=True, tile_position=(0, STACK))
                m.then_inc(s_m, 1)

            pe.sem_inc(s_pv, 2)
            for j in range(AH * blocks[0]):
                maximum(j, 0, 0, j // blocks[0], j % blocks[0], True)
            for h in range(AH):
                row(jobs[0] - AH + h, 0, h)
            for c, (q0, nb) in enumerate(QCH):
                w = nb * P
                if c == 1:
                    pe.wait_ge(s_in, 32)
                if (c + 1) * BANK in GROUPS[1:3]:
                    pe.wait_ge(T["s_stack"][GROUPS.index((c + 1) * BANK)], 16 * STACK_DMAS)

                def keys(turn, i, kb, n, kc, j):
                    diagonal = turn == "diagonal"
                    start = diagonal and i == 0
                    col = i * P if diagonal else 0
                    todo, proj = maxima_of(c, turn, i), projected(c, turn, i)
                    for op in range(2 * AH):
                        h = op % AH
                        if op < AH:
                            if start:
                                pe.wait_ge(s_mr, jobs[c] - AH + h + 3)
                            pe.wait_ge(s_e, AH * n + (h + 1))
                            q = slice(q0 * P + col, q0 * P + w)
                            pe.matmul(S[:, h, col:w], KA[0:STACK + 2, h // REP, ds(kb * P, P)],
                                      QA[0:STACK + 2, h, q], start=True, stop=False)
                            m = pe.matmul(S[:, h, col:w], KB[0:STACK, h // REP, ds(kb * P, P)],
                                          QB[0:STACK, h, q], start=False, stop=not diagonal)
                            if diagonal:
                                m = pe.matmul(S[:, h, col:col + P], T["eyeb"][:], T["cmaskT"][:],
                                              start=False, stop=True)
                            m.then_inc(s_s, 1)
                        else:
                            if h == 0:
                                pe.wait_ge(s_v, n + 1)
                                if c and start:
                                    pe.wait_ge(s_os, 2 * c)
                            pe.wait_ge(s_e, AH * n + (AH + h + 1))
                            g = 64 * (h % 2)
                            m = pe.matmul(O[g:g + HD + 1, h // 2, col:w], vst[:, i % 2, h // REP, :],
                                          pt[:, i % 2, h, col:w], start=start, stop=False,
                                          skip_group_check=True, tile_position=(0, g))
                            if h == AH - 1:
                                m.then_inc(s_pv, 1)
                        for k, (h_, s_, masked) in enumerate(todo):
                            at = k * (AH if proj else 2 * AH) // len(todo)
                            if (at | 1 if at >= AH else at) == op:
                                maximum(j + k, c + 1, c + 1 if masked else kc, h_, s_, masked)
                        if op == AH + 1:
                            for k, s_ in enumerate(proj):
                                project(j + len(todo) + 2 * k, s_)
                        if blocks[c + 1] and closing(c, turn, i) and op in (AH + 1, 2 * AH - 1):
                            for h_ in (op - AH - 1, op - AH) if op == AH + 1 else (2, 3):
                                row(jobs[c + 1] - AH + h_, c + 1, h_)
                steps(pe, c, keys)
            pe.wait_ge(s_os, 2 * nc_)
            for s in range(nb):
                project(jobs[nc_] + 2 * s, s)

        @block.scalar
        def _(a):
            a.sem_inc(s_e, AH)
            for c, (q0, nb) in enumerate(QCH):
                w = nb * P

                def exps(turn, i, kb, n, kc, j):
                    col = i * P if turn == "diagonal" else 0
                    a.wait_ge(s_pv, n + 1)
                    for h in range(AH):
                        a.wait_ge(s_s, AH * n + (h + 1))
                        a.activation(pt[:, i % 2, h, col:w], S[:, h, col:w], ACT.Exp,
                                     scale=float(HD) ** -0.5).then_inc(s_e, 1)
                steps(a, c, exps)
                a.wait_ge(s_pv, base[c + 1] + 2)
                if c:
                    a.wait_ge(s_x, q0)
                a.copy(os_[0:HD + 1, :, 0:w], O[0:HD + 1, :, 0:w]).then_inc(s_os, 1)

        @block.vector
        def _(v):
            step = chain(v, s_dve)

            def reduce(j, kc, h, s, masked):
                w = (s + 1) * P if masked else BANK
                v.wait_ge(s_m, j + 1)
                v.tensor_reduce(pm[:, ds(kc, 1), h, s], M[:, s % 2, 0:w], AX, ALU.max).then_inc(s_mr, 1)

            def combine(j, b):
                v.wait_ge(s_m, j + 2)
                heads = M[:, :, 0:2 * (C + 1)].rearrange("p g (k c) -> p g k c", k=2)
                v.reciprocal(rd[:, b, :, :], heads[:, :, :, C]).then_inc(s_rd, 1)
                for i in range(AH):
                    v.wait_ge(s_rd, AH * b + i + 1)
                    m = v.scalar_tensor_tensor(XL[:, b, :], heads[:, i % 2, i // 2, 0:C],
                                               rd[:, b, i % 2, i // 2:i // 2 + 1], XL[:, b, :],
                                               ALU.mult, ALU.add)
                    if i < AH - 1:
                        m.then_inc(s_rd, 1)
                m.then_inc(s_mr, 2)
                v.wait_ge(s_mr, j + 4)
                v.tensor_tensor_reduce(sq[:], XL[:, b, :], XL[:, b, :], 1.0, 0.0, ALU.mult, ALU.add,
                                       T["squares"][:, b:b + 1])
                v.sem_inc(s_x, 1)

            def rows(c):
                nb, j = blocks[c], jobs[c] - AH
                v.wait_ge(s_mr, j + 2)
                best = mx[:, :, 0:nb]
                if c:
                    step(v.tensor_reduce(best, pm[:, 0:c + 1, :, 0:nb].rearrange("p k h s -> p h s k"),
                                         AX, ALU.max))
                else:
                    step(v.tensor_copy(best, pm[:, 0, :, 0:nb]))
                part = nm[:, c % 2, :, 0:nb, :]
                step(v.tensor_scalar(part[:, :, :, 0], best, -1.0, None, ALU.mult))
                step(v.scalar_tensor_tensor(rest[:, :, 0:nb], best, -1.0, part[:, :, :, 0],
                                            ALU.mult, ALU.subtract))
                v.tensor_copy(part[:, :, :, 1], rest[:, :, 0:nb]).then_inc(s_nm, 1)
                q = QCH[c][0] * P
                for h in range(AH):
                    v.wait_ge(s_m, j + h + 1)
                    v.tensor_copy(QA[STACK:STACK + 2, h, q:q + nb * P],
                                  M[STACK:STACK + 2, h % 2, 0:nb * P]).then_inc(s_mr, 1)

            v.sem_inc(s_mr, 2)
            for j in range(AH * blocks[0]):
                reduce(j, 0, j // blocks[0], j % blocks[0], True)
            rows(0)
            for c, (q0, nb) in enumerate(QCH):
                w = nb * P

                def maxima(turn, i, kb, n, kc, j):
                    todo, proj = maxima_of(c, turn, i), projected(c, turn, i)
                    for k, (h, s, masked) in enumerate(todo):
                        reduce(j + k, c + 1 if masked else kc, h, s, masked)
                    for k, s in enumerate(proj):
                        combine(j + len(todo) + 2 * k, q0 - 4 + s)
                if c + 1 < nc_:
                    steps(v, c, maxima)
                    rows(c + 1)
                else:
                    for i in range(nb):
                        maxima("diagonal", i, 0, 0, c, jobs[c] + i * job_count(c, "diagonal", i))
                v.wait_ge(s_pv, base[c + 1] + 2)
                v.tensor_copy(os_[64:64 + HD + 1, :, 0:w], O[64:64 + HD + 1, :, 0:w]).then_inc(s_os, 1)
            for s in range(nb):
                combine(jobs[nc_] + 2 * s, q0 + s)


def experts_program(nc, t, T, out):
    X, XL, HT = T["X"], T["XL"], T["HT"]
    full = NP // BANK
    with ExitStack() as ctx:
        sem = lambda name: ctx.enter_context(nc.semaphore("e_" + name))
        tile = lambda name, shape, dt=F32: ctx.enter_context(nc.sbuf_tensor("e_" + name, shape, dt))
        ps = ctx.enter_context(nc.psum_tensor("e_ps", [P, 8, BANK], F32))
        r = tile("r", [P, NB, C])
        ms, inv, ln = tile("ms", [P, NB]), tile("inv", [P, NB]), tile("ln", [P, 1])
        rw, tie = tile("rw", [P, NE]), tile("tie", [P, NE, NE])
        w1, w3, w2 = tile("w1", [P, NE, HID]), tile("w3", [P, NE, HID]), tile("w2", [P, NE, len(HTILES), C])
        pr, sel = tile("pr", [P, NB, NE]), tile("sel", [P, NB, NE])
        big = [tile(f"pair{k}", [P, NB, NE, NE]) for k in range(2)]
        red = tile("red", [P, NB])
        wt = tile("wt", [P, NB, NE])
        sg = tile("sg", [P, 2, len(HTILES), BANK])
        s_in, s_w, s_dve, s_rt, s_r, s_tr, s_ht, s_lg, s_ex, s_exd = map(
            sem, ("in", "w", "dve", "rt", "r", "tr", "ht", "lg", "ex", "exd"))
        s_gu, s_sg, s_hh, s_y, s_yc, s_out, s_sent = map(sem, ("gu", "sg", "hh", "y", "yc", "out", "sent"))
        nt = len(HTILES)
        block = ctx.enter_context(nc.Block())

        @block.sync
        def _(sp):
            for dst, name in ((ln, "ln2"), (rw, "routerT"), (tie, "tie")):
                sp.dma_start(dst[:], t[name]).then_inc(s_in, 16)
            sp.dma_start(w1[:], t["w1T"]).then_inc(s_w, 16)
            sp.dma_start(w3[:], t["w3T"]).then_inc(s_w, 16)
            for i, (r0, rows) in enumerate(HTILES):
                sp.dma_start(w2[0:rows, :, i, :], t["w2T"][r0:r0 + rows]).then_inc(s_w, 16)
            rows = out.rearrange("(b p) c -> p b c", p=P)
            for c, (b0, nb) in enumerate(QCH):
                sp.wait_ge(s_out, c + 1)
                sp.dma_start(rows[:, b0:b0 + nb, :], X[:, b0:b0 + nb, :]).then_inc(s_sent, 16)
            sp.wait_ge(s_sent, 16 * len(QCH))

        @block.vector
        def _(v):
            step = chain(v, s_dve)
            v.wait_ge(s_rt, 1)
            step(v.reciprocal(inv[:], ms[:]))
            scale_rows(v, r, XL, inv[:], s_r)
            v.wait_ge(s_lg, 1)
            lg = ps[:, 7, 0:NB * NE].rearrange("p (b e) -> p b e", e=NE)
            step(v.tensor_reduce(red[:], lg, AX, ALU.max))
            v.tensor_tensor(pr[:], lg, red[:].unsqueeze(2).to_broadcast([P, NB, NE]), ALU.subtract).then_inc(s_ex, 1)
            v.wait_ge(s_exd, 1)
            step(v.tensor_reduce(red[:], pr[:], AX, ALU.add))
            step(v.reciprocal(inv[:], red[:]))
            step(v.tensor_tensor(pr[:], pr[:], inv[:].unsqueeze(2).to_broadcast([P, NB, NE]), ALU.mult))
            v.wait_ge(s_in, 48)
            mine = pr[:].unsqueeze(3).to_broadcast([P, NB, NE, NE])
            other = pr[:].unsqueeze(2).to_broadcast([P, NB, NE, NE])
            v.tensor_tensor(big[0][:], other, mine, ALU.is_gt)
            step(v.tensor_tensor(big[1][:], other, mine, ALU.is_equal))
            step(v.tensor_tensor(big[1][:].rearrange("p b e j -> p b (e j)"),
                                 big[1][:].rearrange("p b e j -> p b (e j)"),
                                 tie[:].rearrange("p e j -> p (e j)").unsqueeze(1).to_broadcast([P, NB, NE * NE]),
                                 ALU.mult))
            step(v.tensor_tensor(big[0][:].rearrange("p b e j -> p (b e j)"),
                                 big[0][:].rearrange("p b e j -> p (b e j)"),
                                 big[1][:].rearrange("p b e j -> p (b e j)"), ALU.add))
            step(v.tensor_reduce(sel[:].rearrange("p b e -> p (b e)"),
                                 big[0][:].rearrange("p b e j -> p (b e) j"), AX, ALU.add))
            step(v.scalar_tensor_tensor(wt[:].rearrange("p b e -> p (b e)"), sel[:].rearrange("p b e -> p (b e)"),
                                        float(TOPK), pr[:].rearrange("p b e -> p (b e)"), ALU.is_lt, ALU.mult))
            step(v.tensor_reduce(red[:], wt[:], AX, ALU.add))
            step(v.tensor_scalar(red[:], red[:], 1e-9, None, ALU.add))
            step(v.reciprocal(inv[:], red[:]))
            step(v.tensor_tensor(wt[:], wt[:], inv[:].unsqueeze(2).to_broadcast([P, NB, NE]), ALU.mult))

            def combine(b0, c, w, e):
                v.wait_ge(s_y, NE * c + (e + 3))
                for s in range(w // P):
                    x = XL[:, ds(b0 + s, 1), :].rearrange("p b c -> p (b c)")
                    m = v.scalar_tensor_tensor(x, ps[:, 6 + e % 2, s * P:(s + 1) * P],
                                               wt[:, ds(b0 + s, 1), e], x, ALU.mult, ALU.add)
                m.then_inc(s_yc, 1)

            def experts(col, b0, c, w):
                for e in range(NE):
                    for i, (r0, rows) in enumerate(HTILES):
                        v.wait_ge(s_sg, nt * NE * c + (nt * e + i + 1))
                        h = sg[0:rows, e % 2, i, 0:w]
                        v.tensor_tensor(h, h, ps[0:rows, 2 * i + 1, 0:w], ALU.mult).then_inc(s_hh, 1)
                        if i == 1 and e:
                            combine(b0, c, w, e - 1)
                combine(b0, c, w, NE - 1)
                v.wait_ge(s_yc, NE * c + (NE + 2))
                x = X[:, ds(b0, w // P), :]
                v.tensor_tensor(x, x, XL[:, ds(b0, w // P), :], ALU.add).then_inc(s_out, 1)
            with v.Fori(0, full) as c:
                experts(c * BANK, c * 4, c, BANK)
            experts(full * BANK, full * 4, full, NP - full * BANK)

        @block.scalar
        def _(a):
            a.activation(ms[:], T["squares"], ACT.Sqrt, bias=T["eps"][:, 1:2], scale=1.0 / C).then_inc(s_rt, 1)
            a.wait_ge(s_in, 48)
            turned_to(a, s_tr, s_ht, ps, HT, ln[:])
            a.wait_ge(s_ex, 1)
            a.activation(pr[:], pr[:], ACT.Exp).then_inc(s_exd, 1)

            def silus(col, c, w):
                for e in range(NE):
                    for i, (r0, rows) in enumerate(HTILES):
                        a.wait_ge(s_gu, nt * NE * c + (nt * e + i + 1))
                        a.wait_ge(s_y, NE * c + (e + 1))
                        a.activation(sg[0:rows, e % 2, i, 0:w], ps[0:rows, 2 * i, 0:w],
                                     ACT.Silu).then_inc(s_sg, 1)
            chunk_loop(a, silus)

        @block.tensor
        def _(pe):
            transpose_all(pe, ps, r[:], T["eye"][:], s_tr, s_ht, s_src=s_r)
            pe.wait_ge(s_ht, len(QCH))
            pe.wait_ge(s_in, 48)
            for b in range(NB):
                m = pe.matmul(ps[:, 7, b * NE:(b + 1) * NE], HT[:, b * P:(b + 1) * P], rw[:],
                              start=True, stop=True)
            m.then_inc(s_lg, 1)
            pe.wait_ge(s_w, 16 * (2 + nt))
            pe.wait_ge(s_ex, 1)
            pe.sem_inc(s_y, 2)
            pe.sem_inc(s_yc, 2)
            pe.sem_inc(s_hh, nt)

            def down(c, w, e):
                pe.wait_ge(s_hh, nt * NE * c + (nt * (e + 2)))
                pe.wait_ge(s_yc, NE * c + (e + 1))
                for s in range(w // P):
                    for i, (r0, rows) in enumerate(HTILES):
                        m = pe.matmul(ps[:, 6 + e % 2, s * P:(s + 1) * P], sg[0:rows, e % 2, i, s * P:(s + 1) * P],
                                      w2[0:rows, e, i, :], start=(i == 0), stop=(i == nt - 1))
                m.then_inc(s_y, 1)

            def experts(col, c, w):
                h = HT[:, ds(col, w)]
                for e in range(NE):
                    for i, (r0, rows) in enumerate(HTILES):
                        pe.wait_ge(s_hh, nt * NE * c + (nt * e + i + 1))
                        pe.matmul(ps[0:rows, 2 * i, 0:w], w1[:, e, r0:r0 + rows], h, start=True, stop=True)
                        pe.matmul(ps[0:rows, 2 * i + 1, 0:w], w3[:, e, r0:r0 + rows], h, start=True,
                                  stop=True).then_inc(s_gu, 1)
                        if i == 0 and e:
                            down(c, w, e - 1)
                down(c, w, NE - 1)
            chunk_loop(pe, experts)


def build(nc, t, out):
    with ExitStack() as ctx:
        sb = lambda name, shape, dt=F32: ctx.enter_context(nc.sbuf_tensor(name, shape, dt))
        T = {}
        T["eye"], T["noteye"], T["ones"] = sb("eye", [P, P]), sb("noteye", [P, P]), sb("ones", [P, P])
        T["eps"] = sb("eps", [P, 2])
        T["dcol"] = sb("dcol", [P, NB])
        T["sums"] = sb("sums", [P, NB])[:]
        XR = sb("XR", [P, NB, C])
        with ExitStack() as graph:
            gb = lambda name, shape, dt=F32: graph.enter_context(nc.sbuf_tensor(name, shape, dt))
            T["selE"], T["selB"] = gb("selE", [EP, EROWS]), gb("selB", [EP, EROWS, P])
            T["Ecol"], T["EcolN"] = gb("Ecol", [P, NB * EROWS]), gb("EcolN", [P, NB * EROWS])
            T["nmax"], T["den"] = gb("nmax", [P, 2, NB * HEADS]), gb("den", [P, 2, NB * HEADS])
            T["rden"] = gb("rden", [P, NB * HEADS])
            T["signed"] = gb("signed", [P, 1], I32)
            H = gb("H", [P, NB, C])
            NS = gb("NS", [P, NP])
            T["H"], T["NS"] = H[:], NS[:]
            with ExitStack() as c1:
                E = c1.enter_context(nc.sbuf_tensor("E", [P, NP], F32))
                T["E"] = E[:]
                with ExitStack() as c2:
                    T["U3"] = c2.enter_context(nc.sbuf_tensor("U3", [P, NB, 2, EW], BF16))
                    with ExitStack() as c3:
                        T["X"] = XR[:]
                        T["SQ"] = c3.enter_context(nc.sbuf_tensor("SQ", [P, NB, C], F32))[:]
                        T["HTR"] = c3.enter_context(nc.sbuf_tensor("HT1", [P, NP], F32))[:]
                        norm_program(nc, t, T)
                    spmm_program(nc, t, T)
                shared = {}
                T["sem"] = lambda name: shared.get(name) or shared.setdefault(
                    name, graph.enter_context(nc.semaphore(name)))
                signed = nc.values_load(T["signed"][0:1, 0:1], min_val=0, max_val=1)
                with nc.If(signed > 0):
                    graph_attention(nc, t, T, E, XR, (1, -1))
                with nc.Else():
                    graph_attention(nc, t, T, E, XR, (1,))
                T["ES"] = E[:].rearrange("p (b c) -> p b c", c=C)
                with ExitStack() as c6:
                    big = lambda name: c6.enter_context(nc.sbuf_tensor(name, [P, NP], F32))[:]
                    T["X"] = XR[:]
                    T["HTR"], T["EST"], T["OT"] = big("HT2"), big("EST"), big("OT")
                    gru_program(nc, t, T)

        T["eyeb"], T["cmask"] = sb("eyeb", [P, P], BF16), sb("cmask", [P, P], BF16)
        T["cmaskT"] = sb("cmaskT", [P, P], BF16)
        T["XL"] = sb("XL", [P, NB, C])[:]
        T["HT"] = sb("HT", [P, NP])[:]
        T["squares"] = sb("squares", [P, NB])[:]
        load_masks(nc, t, T)
        with ExitStack() as attn:
            ab = lambda name, shape, dt=F32: attn.enter_context(nc.sbuf_tensor(name, shape, dt))[:]
            T["QA"], T["QB"] = ab("QA", [P, AH, NP], BF16), ab("QB", [P, AH, NP], BF16)
            T["KA"], T["KB"] = ab("KA", [P, KV, NP], BF16), ab("KB", [P, KV, NP], BF16)
            T["V"] = ab("V", [P, NB, KV, HD + 1])
            T["parts"] = [ab("part" + n, [P, 2, NP], BF16) for n in ("h", "m", "l")]
            T["s_stack"] = [attn.enter_context(nc.semaphore(f"stack{g}")) for g in range(3)]
            qkv_program(nc, t, T)
            attention_program(nc, t, T)
        experts_program(nc, t, T, out)


def load_masks(nc, t, T):
    with nc.semaphore("c_in") as s, nc.sbuf_tensor("c_f", [P, 3 * P], F32) as f, \
            nc.semaphore("c_w") as s_w, nc.Block() as block:
        parts = [(T["cmask"][:], 0, P), (T["cmaskT"][:], P, P),
                 (T["eyeb"][:], 2 * P, P)]

        @block.sync
        def _(sp):
            sp.dma_start(f[:], t["masks"]).then_inc(s, 16)

        @block.vector
        def _(v):
            v.wait_ge(s, 16)
            for dst, a, w in parts:
                v.tensor_copy(dst, f[:, a:a + w]).then_inc(s_w, 1)
            v.wait_ge(s_w, len(parts))


def kernel(x, adj, **w):
    import numpy as np
    import concourse.bacc as bacc
    from concourse import mybir as mb
    from concourse.bass_utils import run_bass_kernel_spmd as run

    pad = NP - N
    f32 = np.float32
    a = {}
    a["x"] = np.pad(np.asarray(x), ((0, pad), (0, 0)))
    A = np.pad(np.asarray(adj), ((0, pad), (0, pad)))
    a["adj"] = A
    a["adjT"] = np.ascontiguousarray(A.T)
    a["diag"] = np.ascontiguousarray(np.diagonal(A).reshape(NB, P).T)
    a["gat_W"] = np.asarray(w["L0_gnn_gat_W"])
    a["gat_WT"] = np.ascontiguousarray(a["gat_W"].transpose(0, 2, 1))
    a["gat_a"] = np.ascontiguousarray(np.asarray(w["L0_gnn_gat_a"]).reshape(HEADS, 2, C).transpose(2, 0, 1))
    for kind in ("edge", "node"):
        a[kind + "_WihT"] = np.ascontiguousarray(np.asarray(w[f"L0_gnn_{kind}_Wih"]).T)
        a[kind + "_WhhT"] = np.ascontiguousarray(np.asarray(w[f"L0_gnn_{kind}_Whh"]).T)
        a[kind + "_bih"] = np.ascontiguousarray(np.asarray(w[f"L0_gnn_{kind}_bih"]).reshape(3, C).T)
        a[kind + "_bhh"] = np.ascontiguousarray(np.asarray(w[f"L0_gnn_{kind}_bhh"]).reshape(3, C).T)
    a["eye"] = np.eye(P, dtype=f32)
    a["noteye"] = 1 - np.eye(P, dtype=f32)
    selE = np.zeros((2, EW, EROWS), f32)
    for part in range(PARTS):
        selE[:, 1 + part * EROWS + np.arange(EROWS), np.arange(EROWS)] = 1
    a["selE"] = selE.reshape(EP, EROWS)
    a["selB"] = np.ascontiguousarray(np.broadcast_to(a["selE"][:, :, None], (EP, EROWS, P)))
    inv = 1.0 / 10000.0 ** (np.arange(0, HD, 2, dtype=f32) / HD)
    ang = np.outer(np.arange(NP, dtype=f32), inv)
    ang = np.concatenate([ang, ang], axis=1).T
    sign = np.where(np.arange(HD) < HD // 2, -1, 1).astype(f32)[:, None]
    rope = np.stack([np.cos(ang), np.sin(ang) * sign], axis=1).astype(f32)
    a["rope"] = np.ascontiguousarray(np.tile(rope, (AH, 1, 1)))
    q = np.arange(P)
    low = f32(-1e30)
    late = np.where(q[None] > q[:, None], low, 0)
    a["masks"] = np.ascontiguousarray(np.concatenate(
        [late, late.T, np.eye(P)],
        axis=1).astype(f32))
    a["tie"] = np.ascontiguousarray(np.broadcast_to(np.tril(np.ones((NE, NE), f32), -1), (P, NE, NE)))

    half = np.concatenate([np.arange(HD // 2, HD), np.arange(HD // 2)])
    wq, wk, wv, wo = (np.asarray(w["L0_ffn_" + n]) for n in ("wq", "wk", "wv", "wo"))
    a["wqT"] = np.ascontiguousarray(wq.T)
    a["wkT"] = np.ascontiguousarray(wk.T)
    a["wqpT"] = np.ascontiguousarray(wq.reshape(AH, HD, C)[:, half].reshape(AH * HD, C).T)
    a["wkpT"] = np.ascontiguousarray(wk.reshape(KV, HD, C)[:, half].reshape(KV * HD, C).T)
    a["wvT"] = np.ascontiguousarray(wv.T)
    a["woT"] = np.pad(wo.reshape(C, AH, HD).transpose(2, 1, 0), ((0, 1), (0, 0), (0, 1)))
    a["woT"][HD, :, C] = 1.0
    a["ln1"] = np.asarray(w["L0_ffn_ln1_w"]).reshape(C, 1)
    a["ln2"] = np.asarray(w["L0_ffn_ln2_w"]).reshape(C, 1)
    a["routerT"] = np.ascontiguousarray(np.asarray(w["L0_ffn_router_w"]).T)
    a["w1T"] = np.ascontiguousarray(np.asarray(w["L0_ffn_w1"]).transpose(2, 0, 1))
    a["w3T"] = np.ascontiguousarray(np.asarray(w["L0_ffn_w3"]).transpose(2, 0, 1))
    a["w2T"] = np.ascontiguousarray(np.asarray(w["L0_ffn_w2"]).transpose(2, 0, 1))

    nc = bacc.Bacc("TRN2", target_bir_lowering=False, num_devices=1)
    arrays, t = {}, {}
    for name, v in a.items():
        arrays["in_" + name] = v
        t[name] = nc.dram_tensor("in_" + name, v.shape, mb.dt.from_np(v.dtype), kind="ExternalInput").ap()
    out = nc.dram_tensor("out_0", (NP, C), mb.dt.float32, kind="ExternalOutput").ap()
    build(nc, t, out)
    r = run(nc, [arrays], core_ids=[0])
    return r.results[0]["out_0"][:N]
```
